# Optimizing a Trainium2 kernel written in Bass

```python
import numpy as np
import jax
import jax.numpy as jnp

def _softmax(x, axis=-1):
    return jax.nn.softmax(x, axis=axis)

def _gelu(x):
    return jax.nn.gelu(x, approximate=True)

def _silu(x):
    return jax.nn.silu(x)

def _sigmoid(x):
    return jax.nn.sigmoid(x)

def _layernorm(x, axis=-1, eps=1e-05):
    m = jnp.mean(x, axis=axis, keepdims=True)
    v = jnp.var(x, axis=axis, keepdims=True)
    return (x - m) / jnp.sqrt(v + eps)

def _scatter_add(tgt, idx, src, axis=0):
    return tgt.at[idx].add(src)

def _segment_sum(src, seg, n):
    return jax.ops.segment_sum(src, seg, n)
kernel_name = 'mk_recurrent_d4_jaxref_r8_098524'

def setup_inputs(seed: int=0):
    np.random.seed(seed)
    _w = jnp.asarray

    def _L0_attn_setup():
        import jax, jax.numpy as jnp
        import numpy as np
        B, L, D, E, N, DDELTA, DCONV = (4, 256, 128, 256, 16, 64, 4)
        EPS = 1e-05
        key = jax.random.key(seed)
        ks = jax.random.split(key, 12)

        def rn(k, shape, scale=0.02):
            return (jax.random.normal(k, shape) * scale).astype(jnp.float32)
        return {'resid': jax.random.normal(ks[0], (B, L, D), dtype=jnp.float32), 'norm_w': jnp.ones((D,), jnp.float32), 'skip_w': rn(ks[1], (E, D)), 'in_w': rn(ks[2], (E, D)), 'conv_w': rn(ks[3], (E, 1, DCONV), 0.1), 'conv_b': jnp.zeros((E,), jnp.float32), 'Wd1': rn(ks[4], (DDELTA, E)), 'Wd2_w': rn(ks[5], (E, DDELTA)), 'Wd2_b': rn(ks[6], (E,), 0.01), 'WB': rn(ks[7], (N, E)), 'WC': rn(ks[8], (N, E)), 'A_log': (jax.random.normal(ks[9], (E, N)) * 0.5).astype(jnp.float32), 'W_D': jnp.ones((E,), jnp.float32), 'out_w': rn(ks[10], (D, E))}
    _L0_attn_in = _L0_attn_setup()

    def _L0_ffn_setup():
        import jax, jax.numpy as jnp
        import numpy as np
        E = 16
        G = 4
        EPG = E // G
        K = 4
        TOPK_GROUP = 2
        PER_GROUP_K = K // TOPK_GROUP

        def _route(xf, router_w, correction_bias):
            S = xf.shape[0]
            logits = xf @ router_w.T
            scores = jax.nn.sigmoid(logits)
            sb = scores + correction_bias
            grp_top = jax.lax.top_k(sb.reshape(S, G, EPG), PER_GROUP_K)[0]
            group_scores = grp_top.sum(axis=-1)
            _, group_idx = jax.lax.top_k(group_scores, TOPK_GROUP)
            group_mask = jnp.zeros((S, G), sb.dtype).at[jnp.arange(S)[:, None], group_idx].set(1.0)
            score_mask = jnp.broadcast_to(group_mask[:, :, None], (S, G, EPG)).reshape(S, E)
            masked = jnp.where(score_mask > 0, sb, -jnp.inf)
            _, topk_idx = jax.lax.top_k(masked, K)
            w = jnp.take_along_axis(scores, topk_idx, axis=1)
            w = w / (w.sum(axis=-1, keepdims=True) + 1e-20)
            return (topk_idx, w, scores)
        key = jax.random.key(seed)
        ks = jax.random.split(key, 9)
        B, T, C, H, HS = (2, 128, 128, 32, 256)
        std = 0.02
        return {'x': jax.random.normal(ks[0], (B, T, C), jnp.float32), 'router_w': jax.random.normal(ks[1], (E, C), jnp.float32) * std, 'correction_bias': jnp.zeros((E,), jnp.float32), 'gate_w': jax.random.normal(ks[2], (E, C, H), jnp.float32) * std, 'up_w': jax.random.normal(ks[3], (E, C, H), jnp.float32) * std, 'down_w': jax.random.normal(ks[4], (E, H, C), jnp.float32) * std, 'shared_gate_w': jax.random.normal(ks[5], (HS, C), jnp.float32) * std, 'shared_up_w': jax.random.normal(ks[6], (HS, C), jnp.float32) * std, 'shared_down_w': jax.random.normal(ks[7], (C, HS), jnp.float32) * std}
    _L0_ffn_in = _L0_ffn_setup()

    def _L1_attn_setup():
        import jax, jax.numpy as jnp
        import numpy as np
        EMBED_DIM = 128
        NUM_HEADS = 16
        HEAD_DIM = EMBED_DIM // NUM_HEADS
        BATCH = 2
        SEQ = 256
        BASE = 10000.0
        EPS = 1e-05

        def _lrpe(t, theta, offset=0):
            n = t.shape[-2]
            idx = (jnp.arange(n) + offset).reshape(1, -1, 1).astype(theta.dtype)
            ang = theta * idx
            return jnp.concatenate([t * jnp.cos(ang), t * jnp.sin(ang)], axis=-1)
        key = jax.random.key(seed)
        ks = jax.random.split(key, 8)
        d, h, hd = (EMBED_DIM, NUM_HEADS, HEAD_DIM)
        s = d ** (-0.5)
        x = jax.random.normal(ks[0], (BATCH, SEQ, d), dtype=jnp.float32)
        Wq = jax.random.normal(ks[1], (d, d), dtype=jnp.float32) * s
        Wk = jax.random.normal(ks[2], (d, d), dtype=jnp.float32) * s
        Wv = jax.random.normal(ks[3], (d, d), dtype=jnp.float32) * s
        Wo = jax.random.normal(ks[4], (d, d), dtype=jnp.float32) * s
        G1 = jax.random.normal(ks[5], (d, hd), dtype=jnp.float32) * s
        G2 = jax.random.normal(ks[6], (hd, d), dtype=jnp.float32) * hd ** (-0.5)
        gamma = jnp.ones((d,), jnp.float32)
        beta = jnp.zeros((d,), jnp.float32)
        theta = jnp.asarray((BASE ** (-2.0 / (h * hd) * np.arange(h * hd))).reshape(h, 1, hd), dtype=jnp.float32)
        return {'x': x, 'Wq': Wq, 'Wk': Wk, 'Wv': Wv, 'Wo': Wo, 'G1': G1, 'G2': G2, 'gamma': gamma, 'beta': beta, 'theta': theta}
    _L1_attn_in = _L1_attn_setup()

    def _L1_ffn_setup():
        import jax, jax.numpy as jnp
        import numpy as np
        NUM_EXPERTS = 160
        TOP_K = 8
        ROUTED_SCALE = 2.5
        HIDDEN = 128
        INTER = 64
        key = jax.random.key(seed)
        ks = jax.random.split(key, 7)
        B, S = (1, 256)
        return {'hidden_states': jax.random.normal(ks[0], (B, S, HIDDEN), dtype=jnp.float32), 'router_w': jax.random.normal(ks[1], (NUM_EXPERTS, HIDDEN), dtype=jnp.float32) * 0.02, 'expert_bias': jnp.zeros((NUM_EXPERTS,), dtype=jnp.float32), 'w_gate': jax.random.normal(ks[2], (NUM_EXPERTS, INTER, HIDDEN), dtype=jnp.float32) * 0.02, 'w_down': jax.random.normal(ks[3], (NUM_EXPERTS, HIDDEN, INTER), dtype=jnp.float32) * 0.02, 'w_gate_shared': jax.random.normal(ks[4], (INTER, HIDDEN), dtype=jnp.float32) * 0.02, 'w_down_shared': jax.random.normal(ks[5], (HIDDEN, INTER), dtype=jnp.float32) * 0.02}
    _L1_ffn_in = _L1_ffn_setup()

    def _L2_attn_setup():
        import jax, jax.numpy as jnp
        import numpy as np
        EMB, HEADS = (128, 16)
        S = EMB // HEADS
        key = jax.random.key(seed)
        ks = jax.random.split(key, 7)
        b, t = (2, 256)
        sc = 0.02
        return {'x': jax.random.normal(ks[0], (b, t, EMB), jnp.float32), 'W_down': jax.random.normal(ks[1], (EMB, EMB), jnp.float32) * sc, 'tokeys': jax.random.normal(ks[2], (HEADS, S, S), jnp.float32) * sc, 'toqueries': jax.random.normal(ks[3], (HEADS, S, S), jnp.float32) * sc, 'tovalues': jax.random.normal(ks[4], (HEADS, S, S), jnp.float32) * sc, 'W_unify': jax.random.normal(ks[5], (EMB, EMB), jnp.float32) * sc, 'b_unify': jax.random.normal(ks[6], (EMB,), jnp.float32) * sc}
    _L2_attn_in = _L2_attn_setup()

    def _L2_ffn_setup():
        import jax, jax.numpy as jnp
        import numpy as np
        TOP_K = 4
        N_GROUP = 4
        TOPK_GROUP = 2
        ROUTED_SCALING = 1.0

        def _route(x_flat, gate_weight, e_bias):
            T = x_flat.shape[0]
            E = gate_weight.shape[0]
            logits = jnp.einsum('th,eh->te', x_flat, gate_weight)
            scores = jax.nn.sigmoid(logits)
            scores_for_choice = scores + e_bias[None, :]
            grp = scores_for_choice.reshape(T, N_GROUP, E // N_GROUP)
            top2, _ = jax.lax.top_k(grp, 2)
            group_scores = top2.sum(axis=-1)
            _, group_idx = jax.lax.top_k(group_scores, TOPK_GROUP)
            group_mask = jax.nn.one_hot(group_idx, N_GROUP, dtype=scores.dtype).sum(axis=1)
            score_mask = jnp.repeat(group_mask, E // N_GROUP, axis=1)
            tmp_scores = jnp.where(score_mask > 0, scores_for_choice, 0.0)
            _, topk_idx = jax.lax.top_k(tmp_scores, TOP_K)
            topk_weight = jnp.take_along_axis(scores, topk_idx, axis=1)
            denom = topk_weight.sum(axis=-1, keepdims=True) + 1e-20
            topk_weight = topk_weight / denom * ROUTED_SCALING
            return (topk_idx, topk_weight)
        key = jax.random.key(seed)
        k1, k2, k3, k4, k5 = jax.random.split(key, 5)
        B, S, H, I, E = (1, 256, 128, 64, 16)
        hidden_states = jax.random.normal(k1, (B, S, H), dtype=jnp.float32)
        gate_weight = jax.random.normal(k2, (E, H), dtype=jnp.float32) * (1.0 / np.sqrt(H))
        e_bias = jnp.zeros((E,), dtype=jnp.float32)
        gate_proj = jax.random.normal(k3, (E, I, H), dtype=jnp.float32) * 0.02
        up_proj = jax.random.normal(k4, (E, I, H), dtype=jnp.float32) * 0.02
        down_proj = jax.random.normal(k5, (E, H, I), dtype=jnp.float32) * 0.02
        return {'hidden_states': hidden_states, 'gate_weight': gate_weight, 'e_bias': e_bias, 'gate_proj': gate_proj, 'up_proj': up_proj, 'down_proj': down_proj}
    _L2_ffn_in = _L2_ffn_setup()

    def _L3_attn_setup():
        import jax, jax.numpy as jnp
        import numpy as np
        import math
        B, S, E = (2, 256, 128)
        H, DC, DR = (16, 32, 128)
        HD = E // H

        def _linear_params(key, din, dout):
            k1, k2 = jax.random.split(key)
            bound = 1.0 / math.sqrt(din)
            w = jax.random.uniform(k1, (din, dout), minval=-bound, maxval=bound, dtype=jnp.float32)
            b = jax.random.uniform(k2, (dout,), minval=-bound, maxval=bound, dtype=jnp.float32)
            return (w, b)

        def _gelu(x):
            return jax.nn.gelu(x, approximate=False)

        def _rope_cos_sin(seq_len, d_rope):
            inv_freq = 1.0 / 10000.0 ** (jnp.arange(0, d_rope, 2, dtype=jnp.float32) / d_rope)
            t = jnp.arange(seq_len, dtype=jnp.float32)
            freqs = t[:, None] * inv_freq[None, :]
            emb = jnp.concatenate([freqs, freqs], axis=-1)
            return (jnp.cos(emb), jnp.sin(emb))

        def _apply_rope(x, cos, sin):
            d = x.shape[-1]
            x1, x2 = (x[..., :d // 2], x[..., d // 2:])
            rot = jnp.concatenate([-x2, x1], axis=-1)
            return x * cos + rot * sin
        key = jax.random.key(seed)
        ks = jax.random.split(key, 10)
        x = jax.random.normal(ks[0], (B, S, E), dtype=jnp.float32)
        wq, bq = _linear_params(ks[1], E, DC)
        wqc, bqc = _linear_params(ks[2], DC, E - DR)
        wqr, bqr = _linear_params(ks[3], E, DR)
        wkv, bkv = _linear_params(ks[4], E, DC)
        wkr, bkr = _linear_params(ks[5], E, DR)
        wkc, bkc = _linear_params(ks[6], DC, E - DR)
        wv, bv = _linear_params(ks[7], DC, E)
        wo, bo = _linear_params(ks[8], E, E)
        return dict(x=x, wq=wq, bq=bq, wqc=wqc, bqc=bqc, wqr=wqr, bqr=bqr, wkv=wkv, bkv=bkv, wkr=wkr, bkr=bkr, wkc=wkc, bkc=bkc, wv=wv, bv=bv, wo=wo, bo=bo)
    _L3_attn_in = _L3_attn_setup()

    def _L3_ffn_setup():
        import jax, jax.numpy as jnp
        import numpy as np
        E = 8
        K = 2
        D = 128
        F = 512
        FS = 256
        B, S = (2, 128)
        key = jax.random.key(seed)
        ks = jax.random.split(key, 8)
        scale = jnp.float32(0.02)
        return {'x': jax.random.normal(ks[0], (B, S, D), jnp.float32), 'gate_w': jax.random.normal(ks[1], (E, D), jnp.float32) * scale, 'gate_k': jax.random.normal(ks[2], (E, D, F), jnp.float32) * scale, 'up_k': jax.random.normal(ks[3], (E, D, F), jnp.float32) * scale, 'down_k': jax.random.normal(ks[4], (E, F, D), jnp.float32) * scale, 'sh_gate': jax.random.normal(ks[5], (D, FS), jnp.float32) * scale, 'sh_up': jax.random.normal(ks[6], (D, FS), jnp.float32) * scale, 'sh_down': jax.random.normal(ks[7], (FS, D), jnp.float32) * scale}
    _L3_ffn_in = _L3_ffn_setup()
    _d = {'L0_attn_resid': _L0_attn_in['resid'], 'L0_attn_norm_w': _L0_attn_in['norm_w'], 'L0_attn_skip_w': _L0_attn_in['skip_w'], 'L0_attn_in_w': _L0_attn_in['in_w'], 'L0_attn_conv_w': _L0_attn_in['conv_w'], 'L0_attn_conv_b': _L0_attn_in['conv_b'], 'L0_attn_Wd1': _L0_attn_in['Wd1'], 'L0_attn_Wd2_w': _L0_attn_in['Wd2_w'], 'L0_attn_Wd2_b': _L0_attn_in['Wd2_b'], 'L0_attn_WB': _L0_attn_in['WB'], 'L0_attn_WC': _L0_attn_in['WC'], 'L0_attn_A_log': _L0_attn_in['A_log'], 'L0_attn_W_D': _L0_attn_in['W_D'], 'L0_attn_out_w': _L0_attn_in['out_w'], 'L0_ffn_router_w': _L0_ffn_in['router_w'], 'L0_ffn_correction_bias': _L0_ffn_in['correction_bias'], 'L0_ffn_gate_w': _L0_ffn_in['gate_w'], 'L0_ffn_up_w': _L0_ffn_in['up_w'], 'L0_ffn_down_w': _L0_ffn_in['down_w'], 'L0_ffn_shared_gate_w': _L0_ffn_in['shared_gate_w'], 'L0_ffn_shared_up_w': _L0_ffn_in['shared_up_w'], 'L0_ffn_shared_down_w': _L0_ffn_in['shared_down_w'], 'L1_attn_Wq': _L1_attn_in['Wq'], 'L1_attn_Wk': _L1_attn_in['Wk'], 'L1_attn_Wv': _L1_attn_in['Wv'], 'L1_attn_Wo': _L1_attn_in['Wo'], 'L1_attn_G1': _L1_attn_in['G1'], 'L1_attn_G2': _L1_attn_in['G2'], 'L1_attn_gamma': _L1_attn_in['gamma'], 'L1_attn_beta': _L1_attn_in['beta'], 'L1_attn_theta': _L1_attn_in['theta'], 'L1_ffn_router_w': _L1_ffn_in['router_w'], 'L1_ffn_expert_bias': _L1_ffn_in['expert_bias'], 'L1_ffn_w_gate': _L1_ffn_in['w_gate'], 'L1_ffn_w_down': _L1_ffn_in['w_down'], 'L1_ffn_w_gate_shared': _L1_ffn_in['w_gate_shared'], 'L1_ffn_w_down_shared': _L1_ffn_in['w_down_shared'], 'L2_attn_W_down': _L2_attn_in['W_down'], 'L2_attn_tokeys': _L2_attn_in['tokeys'], 'L2_attn_toqueries': _L2_attn_in['toqueries'], 'L2_attn_tovalues': _L2_attn_in['tovalues'], 'L2_attn_W_unify': _L2_attn_in['W_unify'], 'L2_attn_b_unify': _L2_attn_in['b_unify'], 'L2_ffn_gate_weight': _L2_ffn_in['gate_weight'], 'L2_ffn_e_bias': _L2_ffn_in['e_bias'], 'L2_ffn_gate_proj': _L2_ffn_in['gate_proj'], 'L2_ffn_up_proj': _L2_ffn_in['up_proj'], 'L2_ffn_down_proj': _L2_ffn_in['down_proj'], 'L3_attn_wq': _L3_attn_in['wq'], 'L3_attn_bq': _L3_attn_in['bq'], 'L3_attn_wqc': _L3_attn_in['wqc'], 'L3_attn_bqc': _L3_attn_in['bqc'], 'L3_attn_wqr': _L3_attn_in['wqr'], 'L3_attn_bqr': _L3_attn_in['bqr'], 'L3_attn_wkv': _L3_attn_in['wkv'], 'L3_attn_bkv': _L3_attn_in['bkv'], 'L3_attn_wkr': _L3_attn_in['wkr'], 'L3_attn_bkr': _L3_attn_in['bkr'], 'L3_attn_wkc': _L3_attn_in['wkc'], 'L3_attn_bkc': _L3_attn_in['bkc'], 'L3_attn_wv': _L3_attn_in['wv'], 'L3_attn_bv': _L3_attn_in['bv'], 'L3_attn_wo': _L3_attn_in['wo'], 'L3_attn_bo': _L3_attn_in['bo'], 'L3_ffn_gate_w': _L3_ffn_in['gate_w'], 'L3_ffn_gate_k': _L3_ffn_in['gate_k'], 'L3_ffn_up_k': _L3_ffn_in['up_k'], 'L3_ffn_down_k': _L3_ffn_in['down_k'], 'L3_ffn_sh_gate': _L3_ffn_in['sh_gate'], 'L3_ffn_sh_up': _L3_ffn_in['sh_up'], 'L3_ffn_sh_down': _L3_ffn_in['sh_down']}
    _x0 = _d['L0_attn_resid']
    _d['L0_attn_resid'] = jax.random.normal(jax.random.fold_in(jax.random.key(seed), 1), (4, 1024, 128), dtype=_x0.dtype)
    del _x0
    return _d

def reference(L0_attn_resid, L0_attn_norm_w, L0_attn_skip_w, L0_attn_in_w, L0_attn_conv_w, L0_attn_conv_b, L0_attn_Wd1, L0_attn_Wd2_w, L0_attn_Wd2_b, L0_attn_WB, L0_attn_WC, L0_attn_A_log, L0_attn_W_D, L0_attn_out_w, L0_ffn_router_w, L0_ffn_correction_bias, L0_ffn_gate_w, L0_ffn_up_w, L0_ffn_down_w, L0_ffn_shared_gate_w, L0_ffn_shared_up_w, L0_ffn_shared_down_w, L1_attn_Wq, L1_attn_Wk, L1_attn_Wv, L1_attn_Wo, L1_attn_G1, L1_attn_G2, L1_attn_gamma, L1_attn_beta, L1_attn_theta, L1_ffn_router_w, L1_ffn_expert_bias, L1_ffn_w_gate, L1_ffn_w_down, L1_ffn_w_gate_shared, L1_ffn_w_down_shared, L2_attn_W_down, L2_attn_tokeys, L2_attn_toqueries, L2_attn_tovalues, L2_attn_W_unify, L2_attn_b_unify, L2_ffn_gate_weight, L2_ffn_e_bias, L2_ffn_gate_proj, L2_ffn_up_proj, L2_ffn_down_proj, L3_attn_wq, L3_attn_bq, L3_attn_wqc, L3_attn_bqc, L3_attn_wqr, L3_attn_bqr, L3_attn_wkv, L3_attn_bkv, L3_attn_wkr, L3_attn_bkr, L3_attn_wkc, L3_attn_bkc, L3_attn_wv, L3_attn_bv, L3_attn_wo, L3_attn_bo, L3_ffn_gate_w, L3_ffn_gate_k, L3_ffn_up_k, L3_ffn_down_k, L3_ffn_sh_gate, L3_ffn_sh_up, L3_ffn_sh_down):

    def _L0_attn_ref(resid, norm_w, skip_w, in_w, conv_w, conv_b, Wd1, Wd2_w, Wd2_b, WB, WC, A_log, W_D, out_w):
        import jax, jax.numpy as jnp
        import numpy as np
        B, L, D, E, N, DDELTA, DCONV = (4, 256, 128, 256, 16, 64, 4)
        EPS = 1e-05
        x = resid * jax.lax.rsqrt(jnp.mean(resid * resid, axis=-1, keepdims=True) + EPS) * norm_w
        skip = x @ skip_w.T
        x = x @ in_w.T
        xc = jnp.transpose(x, (0, 2, 1))
        xc = jax.lax.conv_general_dilated(xc, conv_w, window_strides=(1,), padding=[(DCONV - 1, 0)], dimension_numbers=('NCH', 'OIH', 'NCH'), feature_group_count=conv_w.shape[0])
        x = jnp.transpose(xc, (0, 2, 1)) + conv_b
        x = jax.nn.silu(x)
        A = -jnp.exp(A_log)
        delta = jax.nn.softplus(x @ Wd1.T @ Wd2_w.T + Wd2_b)
        Bm = x @ WB.T
        Cm = x @ WC.T

        def step(h, inp):
            x_l, d_l, B_l, C_l = inp
            A_bar = jnp.exp(d_l[:, :, None] * A)
            h = A_bar * h + (d_l * x_l)[:, :, None] * B_l[:, None, :]
            y_l = jnp.einsum('ben,bn->be', h, C_l)
            return (h, y_l)
        h0 = jnp.zeros((resid.shape[0], A.shape[0], A.shape[1]), x.dtype)
        xs = (jnp.swapaxes(x, 0, 1), jnp.swapaxes(delta, 0, 1), jnp.swapaxes(Bm, 0, 1), jnp.swapaxes(Cm, 0, 1))
        _, ys = jax.lax.scan(step, h0, xs)
        y = jnp.swapaxes(ys, 0, 1)
        y = y + x * W_D
        y = y * jax.nn.silu(skip)
        y = y @ out_w.T
        return resid + y

    def _L0_ffn_ref(x, router_w, correction_bias, gate_w, up_w, down_w, shared_gate_w, shared_up_w, shared_down_w):
        import jax, jax.numpy as jnp
        import numpy as np
        E = 16
        G = 4
        EPG = E // G
        K = 4
        TOPK_GROUP = 2
        PER_GROUP_K = K // TOPK_GROUP

        def _route(xf, router_w, correction_bias):
            S = xf.shape[0]
            logits = xf @ router_w.T
            scores = jax.nn.sigmoid(logits)
            sb = scores + correction_bias
            grp_top = jax.lax.top_k(sb.reshape(S, G, EPG), PER_GROUP_K)[0]
            group_scores = grp_top.sum(axis=-1)
            _, group_idx = jax.lax.top_k(group_scores, TOPK_GROUP)
            group_mask = jnp.zeros((S, G), sb.dtype).at[jnp.arange(S)[:, None], group_idx].set(1.0)
            score_mask = jnp.broadcast_to(group_mask[:, :, None], (S, G, EPG)).reshape(S, E)
            masked = jnp.where(score_mask > 0, sb, -jnp.inf)
            _, topk_idx = jax.lax.top_k(masked, K)
            w = jnp.take_along_axis(scores, topk_idx, axis=1)
            w = w / (w.sum(axis=-1, keepdims=True) + 1e-20)
            return (topk_idx, w, scores)
        B, T, C = x.shape
        S = B * T
        xf = x.reshape(S, C)
        sg = xf @ shared_gate_w.T
        su = xf @ shared_up_w.T
        shared_out = jax.nn.silu(sg) * su @ shared_down_w.T
        topk_idx, w, _scores = _route(xf, router_w, correction_bias)
        combine = jnp.zeros((S, E), xf.dtype).at[jnp.arange(S)[:, None], topk_idx].add(w)
        g = jnp.einsum('sc,ech->esh', xf, gate_w)
        u = jnp.einsum('sc,ech->esh', xf, up_w)
        h = jax.nn.silu(g) * u
        hw = h * combine.T[:, :, None]
        routed = jnp.einsum('esh,ehc->sc', hw, down_w)
        return (shared_out + routed).reshape(B, T, C)

    def _L1_attn_ref(x, Wq, Wk, Wv, Wo, G1, G2, gamma, beta, theta):
        import jax, jax.numpy as jnp
        import numpy as np
        EMBED_DIM = 128
        NUM_HEADS = 16
        HEAD_DIM = EMBED_DIM // NUM_HEADS
        BATCH = 2
        SEQ = 256
        BASE = 10000.0
        EPS = 1e-05

        def _lrpe(t, theta, offset=0):
            n = t.shape[-2]
            idx = (jnp.arange(n) + offset).reshape(1, -1, 1).astype(theta.dtype)
            ang = theta * idx
            return jnp.concatenate([t * jnp.cos(ang), t * jnp.sin(ang)], axis=-1)
        b, n, d = x.shape
        h, hd = (NUM_HEADS, HEAD_DIM)
        q = jax.nn.silu(x @ Wq)
        k = jax.nn.silu(x @ Wk)
        v = x @ Wv
        split = lambda t: t.reshape(b, n, h, hd).transpose(0, 2, 1, 3)
        q, k, v = (split(q), split(k), split(v))
        q = _lrpe(q, theta)
        k = _lrpe(k, theta)
        mask = jnp.tril(jnp.ones((n, n), dtype=x.dtype))
        energy = jnp.einsum('bhnd,bhmd->bhnm', q, k) * mask
        out = jnp.einsum('bhnm,bhmd->bhnd', energy, v)
        out = out.transpose(0, 2, 1, 3).reshape(b, n, d)
        out = out @ Wo
        gate = jax.nn.sigmoid(x @ G1 @ G2)
        out = out * gate
        mu = jnp.mean(out, axis=-1, keepdims=True)
        var = jnp.var(out, axis=-1, keepdims=True)
        out = (out - mu) / jnp.sqrt(var + EPS) * gamma + beta
        return out

    def _L1_ffn_ref(hidden_states, router_w, expert_bias, w_gate, w_down, w_gate_shared, w_down_shared):
        import jax, jax.numpy as jnp
        import numpy as np
        NUM_EXPERTS = 160
        TOP_K = 8
        ROUTED_SCALE = 2.5
        HIDDEN = 128
        INTER = 64
        B, S, H = hidden_states.shape
        x = hidden_states.reshape(-1, H)
        T = x.shape[0]
        logits = x @ router_w.T + expert_bias[None, :]
        probs = jax.nn.sigmoid(logits)
        top_w, top_idx = jax.lax.top_k(probs, TOP_K)
        top_w = top_w / (jnp.sum(top_w, axis=-1, keepdims=True) + 1e-09)
        top_w = top_w * ROUTED_SCALE
        combine = jnp.zeros((T, NUM_EXPERTS), dtype=x.dtype)
        combine = combine.at[jnp.arange(T)[:, None], top_idx].set(top_w)
        h1 = jax.nn.silu(jnp.einsum('th,eih->eti', x, w_gate))
        h1w = h1 * combine.T[:, :, None]
        routed = jnp.einsum('eti,ehi->th', h1w, w_down)
        shared = jax.nn.silu(x @ w_gate_shared.T) @ w_down_shared.T
        return (routed + shared).reshape(B, S, H)

    def _L2_attn_ref(x, W_down, tokeys, toqueries, tovalues, W_unify, b_unify):
        import jax, jax.numpy as jnp
        import numpy as np
        EMB, HEADS = (128, 16)
        S = EMB // HEADS
        b, t, e = x.shape
        h, s = (HEADS, S)
        scale = s ** (-0.25)
        xd = (x @ W_down).reshape(b, t, h, s)
        keys = jnp.einsum('bthk,hik->bthi', xd, tokeys) * scale
        queries = jnp.einsum('bthk,hik->bthi', xd, toqueries) * scale
        values = jnp.einsum('bthk,hik->bthi', xd, tovalues)
        dot = jnp.einsum('bqhs,bkhs->bhqk', queries, keys)
        attn = jax.nn.softmax(dot, axis=-1)
        out = jnp.einsum('bhqk,bkhs->bqhs', attn, values).reshape(b, t, e)
        return out @ W_unify + b_unify

    def _L2_ffn_ref(hidden_states, gate_weight, e_bias, gate_proj, up_proj, down_proj):
        import jax, jax.numpy as jnp
        import numpy as np
        TOP_K = 4
        N_GROUP = 4
        TOPK_GROUP = 2
        ROUTED_SCALING = 1.0

        def _route(x_flat, gate_weight, e_bias):
            T = x_flat.shape[0]
            E = gate_weight.shape[0]
            logits = jnp.einsum('th,eh->te', x_flat, gate_weight)
            scores = jax.nn.sigmoid(logits)
            scores_for_choice = scores + e_bias[None, :]
            grp = scores_for_choice.reshape(T, N_GROUP, E // N_GROUP)
            top2, _ = jax.lax.top_k(grp, 2)
            group_scores = top2.sum(axis=-1)
            _, group_idx = jax.lax.top_k(group_scores, TOPK_GROUP)
            group_mask = jax.nn.one_hot(group_idx, N_GROUP, dtype=scores.dtype).sum(axis=1)
            score_mask = jnp.repeat(group_mask, E // N_GROUP, axis=1)
            tmp_scores = jnp.where(score_mask > 0, scores_for_choice, 0.0)
            _, topk_idx = jax.lax.top_k(tmp_scores, TOP_K)
            topk_weight = jnp.take_along_axis(scores, topk_idx, axis=1)
            denom = topk_weight.sum(axis=-1, keepdims=True) + 1e-20
            topk_weight = topk_weight / denom * ROUTED_SCALING
            return (topk_idx, topk_weight)
        B, S, H = hidden_states.shape
        E = gate_proj.shape[0]
        x = hidden_states.reshape(-1, H).astype(jnp.float32)
        topk_idx, topk_weight = _route(x, gate_weight, e_bias)
        combine = (jax.nn.one_hot(topk_idx, E, dtype=x.dtype) * topk_weight[..., None]).sum(axis=1)
        g = jnp.einsum('th,eih->tei', x, gate_proj)
        u = jnp.einsum('th,eih->tei', x, up_proj)
        act = jax.nn.silu(g) * u
        expert_out = jnp.einsum('tei,ehi->teh', act, down_proj)
        y = jnp.einsum('teh,te->th', expert_out, combine)
        return y.reshape(B, S, H)

    def _L3_attn_ref(x, wq, bq, wqc, bqc, wqr, bqr, wkv, bkv, wkr, bkr, wkc, bkc, wv, bv, wo, bo):
        import jax, jax.numpy as jnp
        import numpy as np
        import math
        B, S, E = (2, 256, 128)
        H, DC, DR = (16, 32, 128)
        HD = E // H

        def _linear_params(key, din, dout):
            k1, k2 = jax.random.split(key)
            bound = 1.0 / math.sqrt(din)
            w = jax.random.uniform(k1, (din, dout), minval=-bound, maxval=bound, dtype=jnp.float32)
            b = jax.random.uniform(k2, (dout,), minval=-bound, maxval=bound, dtype=jnp.float32)
            return (w, b)

        def _gelu(x):
            return jax.nn.gelu(x, approximate=False)

        def _rope_cos_sin(seq_len, d_rope):
            inv_freq = 1.0 / 10000.0 ** (jnp.arange(0, d_rope, 2, dtype=jnp.float32) / d_rope)
            t = jnp.arange(seq_len, dtype=jnp.float32)
            freqs = t[:, None] * inv_freq[None, :]
            emb = jnp.concatenate([freqs, freqs], axis=-1)
            return (jnp.cos(emb), jnp.sin(emb))

        def _apply_rope(x, cos, sin):
            d = x.shape[-1]
            x1, x2 = (x[..., :d // 2], x[..., d // 2:])
            rot = jnp.concatenate([-x2, x1], axis=-1)
            return x * cos + rot * sin
        b, s, _ = x.shape
        cq = _gelu(x @ wq + bq)
        q_c = cq @ wqc + bqc
        q_r = x @ wqr + bqr
        ckv = _gelu(x @ wkv + bkv)
        k_r = x @ wkr + bkr
        k_c = ckv @ wkc + bkc
        v = (ckv @ wv + bv).reshape(b, s, H, HD).transpose(0, 2, 1, 3)
        cos, sin = _rope_cos_sin(s, DR)
        q_r = _apply_rope(q_r, cos, sin)
        k_r = _apply_rope(k_r, cos, sin)
        q = _gelu(jnp.concatenate([q_c, q_r], axis=-1)).reshape(b, s, H, HD).transpose(0, 2, 1, 3)
        k = _gelu(jnp.concatenate([k_c, k_r], axis=-1)).reshape(b, s, H, HD).transpose(0, 2, 1, 3)
        scale = 1.0 / math.sqrt(HD)
        scores = jnp.einsum('bhqd,bhkd->bhqk', q, k) * scale
        causal = jnp.triu(jnp.ones((s, s), dtype=bool), k=1)
        scores = jnp.where(causal[None, None], -jnp.inf, scores)
        attn = jax.nn.softmax(scores, axis=-1)
        out = jnp.einsum('bhqk,bhkd->bhqd', attn, v)
        out = out.transpose(0, 2, 1, 3).reshape(b, s, E)
        return out @ wo + bo

    def _L3_ffn_ref(x, gate_w, gate_k, up_k, down_k, sh_gate, sh_up, sh_down):
        import jax, jax.numpy as jnp
        import numpy as np
        E = 8
        K = 2
        D = 128
        F = 512
        FS = 256
        B, S = (2, 128)
        b, s, d = x.shape
        xt = x.reshape(-1, d)
        logits = xt @ gate_w.T
        scores = jax.nn.softmax(logits, axis=-1)
        topk_w, topk_i = jax.lax.top_k(scores, K)
        combine = (jax.nn.one_hot(topk_i, E, dtype=xt.dtype) * topk_w[..., None]).sum(axis=1)
        g = jnp.einsum('nd,edf->enf', xt, gate_k)
        u = jnp.einsum('nd,edf->enf', xt, up_k)
        a = jax.nn.silu(g) * u
        eo = jnp.einsum('enf,efd->end', a, down_k)
        y = jnp.einsum('end,ne->nd', eo, combine)
        shared = jax.nn.silu(xt @ sh_gate) * (xt @ sh_up) @ sh_down
        return (y + shared).reshape(b, s, d)
    x = L0_attn_resid
    xn = _layernorm(x, axis=-1)
    s = _L0_attn_ref(xn, L0_attn_norm_w, L0_attn_skip_w, L0_attn_in_w, L0_attn_conv_w, L0_attn_conv_b, L0_attn_Wd1, L0_attn_Wd2_w, L0_attn_Wd2_b, L0_attn_WB, L0_attn_WC, L0_attn_A_log, L0_attn_W_D, L0_attn_out_w)
    g = _silu(_L0_ffn_ref(xn, L0_ffn_router_w, L0_ffn_correction_bias, L0_ffn_gate_w, L0_ffn_up_w, L0_ffn_down_w, L0_ffn_shared_gate_w, L0_ffn_shared_up_w, L0_ffn_shared_down_w))
    x = x + s * g
    xn = _layernorm(x, axis=-1)
    s = _L1_attn_ref(xn, L1_attn_Wq, L1_attn_Wk, L1_attn_Wv, L1_attn_Wo, L1_attn_G1, L1_attn_G2, L1_attn_gamma, L1_attn_beta, L1_attn_theta)
    g = _silu(_L1_ffn_ref(xn, L1_ffn_router_w, L1_ffn_expert_bias, L1_ffn_w_gate, L1_ffn_w_down, L1_ffn_w_gate_shared, L1_ffn_w_down_shared))
    x = x + s * g
    xn = _layernorm(x, axis=-1)
    s = _L2_attn_ref(xn, L2_attn_W_down, L2_attn_tokeys, L2_attn_toqueries, L2_attn_tovalues, L2_attn_W_unify, L2_attn_b_unify)
    g = _silu(_L2_ffn_ref(xn, L2_ffn_gate_weight, L2_ffn_e_bias, L2_ffn_gate_proj, L2_ffn_up_proj, L2_ffn_down_proj))
    x = x + s * g
    xn = _layernorm(x, axis=-1)
    s = _L3_attn_ref(xn, L3_attn_wq, L3_attn_bq, L3_attn_wqc, L3_attn_bqc, L3_attn_wqr, L3_attn_bqr, L3_attn_wkv, L3_attn_bkv, L3_attn_wkr, L3_attn_bkr, L3_attn_wkc, L3_attn_bkc, L3_attn_wv, L3_attn_bv, L3_attn_wo, L3_attn_bo)
    g = _silu(_L3_ffn_ref(xn, L3_ffn_gate_w, L3_ffn_gate_k, L3_ffn_up_k, L3_ffn_down_k, L3_ffn_sh_gate, L3_ffn_sh_up, L3_ffn_sh_down))
    x = x + s * g
    return x

_drawn_inputs = setup_inputs


def setup_inputs(seed=0):
    import zlib

    import numpy as np

    out = dict(_drawn_inputs(seed))
    spreads = {'L0_attn_norm_w': (1.0, 0.2),
     'L0_attn_conv_b': (0.0, 0.1),
     'L0_attn_W_D': (1.0, 0.2),
     'L0_ffn_correction_bias': (0.0, 0.1),
     'L1_attn_gamma': (1.0, 0.2),
     'L1_attn_beta': (0.0, 0.1),
     'L1_ffn_expert_bias': (0.0, 0.1),
     'L2_ffn_e_bias': (0.0, 0.1)}
    factors = {}
    for name, (base, spread) in spreads.items():
        noise = np.random.default_rng([zlib.crc32(name.encode()), seed]).standard_normal(out[name].shape)
        drawn = base * np.exp(spread * noise) if base else spread * noise
        out[name] = jnp.asarray(drawn.astype(out[name].dtype))
    for name, factor in factors.items():
        out[name] = (out[name] * factor).astype(out[name].dtype)
    return out
```

```python
from contextlib import ExitStack, contextmanager

import numpy as np

import concourse.bass as bass
from concourse import mybir

ALU = mybir.AluOpType
ACT = mybir.ActivationFunctionType
F32 = mybir.dt.float32
BF16 = mybir.dt.bfloat16
AX = mybir.AxisListType

P = 128
B, L = 4, 1024
T = B * L
CH = 512
NC = T // CH
EPS = 1e-5
BIG = 1e30

NS = 16
DD = 64
NT = 4
SP = 32

NH, HD = 16, 8
GH = 4
KT = L // P
NPART = 3
ROWS = NPART * NPART * HD


@contextmanager
def stage(nc, name):
    sems = []
    with ExitStack() as ctx:
        def sb(n, shape, dt=F32):
            return ctx.enter_context(nc.sbuf_tensor(f"{name}_{n}", shape, dt))

        def ps(n, shape, dt=F32):
            return ctx.enter_context(nc.psum_tensor(f"{name}_{n}", shape, dt))

        def sem(n):
            sems.append(nc.alloc_semaphore(f"{name}_{n}"))
            return sems[-1]

        yield sb, ps, sem
        nc.clear_and_free_semaphores(sems)
        nc.all_engine_barrier()


class Steps:

    def __init__(self, eng, sem, base=0):
        self.eng, self.sem, self.base, self.n = eng, sem, base, 0

    def __call__(self, ins, apart=False):
        self.n += 1
        ins.then_inc(self.sem, 1)
        if apart:
            wait_apart(self.eng, self.sem, self.base + self.n)
        else:
            self.eng.wait_ge(self.sem, self.base + self.n)


def wait_apart(eng, sem, value):
    eng.wait_ge(sem, value)
    eng.nop(nofuse=True)


def at(t, start, size):
    return t[:, bass.ds(start, size)]


def load(eng, sem, pairs):
    for dst, src in pairs:
        eng.dma_start(dst, src).then_inc(sem, 16)


def normalise(nc, name, src, dst, average, centre, weight=None, shift=None, first_load=None, eps=EPS):
    with stage(nc, name) as (sb, ps, sem):
        dev = sb("dev", [P, 2, CH])
        sq = sb("sq", [P, 2, CH])
        sd = sb("sd", [P, 2, CH])
        rs = sb("rs", [P, 2, CH])
        epst = sb("eps", [P, 1])
        mean = ps("mean", [P, 2, CH])
        var = ps("var", [P, 2, CH])
        loaded = sem("loaded")
        eps_set = sem("eps_set")
        scaled = sem("scaled")
        mean_ready = [sem(f"mean_ready{u}") for u in range(2)]
        dev_ready = [sem(f"dev_ready{u}") for u in range(2)]
        sq_ready = [sem(f"sq_ready{u}") for u in range(2)]
        var_ready = [sem(f"var_ready{u}") for u in range(2)]
        sd_ready = [sem(f"sd_ready{u}") for u in range(2)]
        rs_ready = [sem(f"rs_ready{u}") for u in range(2)]
        out_ready = [sem(f"out_ready{u}") for u in range(2)]
        n_load = len(first_load or [])
        with nc.Block() as block:
            @block.sync
            def _(sp):
                load(sp, loaded, first_load or [])
                if n_load:
                    sp.wait_ge(loaded, 16 * n_load)

            @block.tensor
            def _(pe):
                if n_load:
                    pe.wait_ge(loaded, 16 * n_load)
                with pe.Fori(0, NC // 2) as i:
                    if centre:
                        for u in range(2):
                            pe.wait_ge(dev_ready[u], i)
                            pe.matmul(mean[:, u, :], average[:, :], at(src, i * 2 * CH + u * CH, CH),
                                      start=True, stop=True).then_inc(mean_ready[u], 1)
                    for u in range(2):
                        pe.wait_ge(sq_ready[u], i + 1)
                        pe.wait_ge(sd_ready[u], i)
                        pe.matmul(var[:, u, :], average[:, :], sq[:, u, :],
                                  start=True, stop=True).then_inc(var_ready[u], 1)

            @block.scalar
            def _(act):
                act.wait_ge(eps_set, 1)
                if n_load:
                    act.wait_ge(loaded, 16 * n_load)
                with act.Fori(0, NC // 2) as i:
                    for u in range(2):
                        act.wait_ge(var_ready[u], i)
                        if centre:
                            act.wait_ge(dev_ready[u], i + 1)
                            act.activation(sq[:, u, :], dev[:, u, :], ACT.Square).then_inc(sq_ready[u], 1)
                        else:
                            act.activation(sq[:, u, :], at(src, i * 2 * CH + u * CH, CH),
                                           ACT.Square).then_inc(sq_ready[u], 1)
                    for u in range(2):
                        act.wait_ge(rs_ready[u], i)
                        act.wait_ge(var_ready[u], i + 1)
                        act.activation(sd[:, u, :], var[:, u, :], ACT.Sqrt,
                                       bias=epst[:, 0:1]).then_inc(sd_ready[u], 1)

            @block.vector
            def _(dve):
                dve.memset(epst[:, :], eps).then_inc(eps_set, 1)
                if n_load:
                    dve.wait_ge(loaded, 16 * n_load)
                with dve.Fori(0, NC // 2) as i:
                    if centre:
                        for u in range(2):
                            dve.wait_ge(mean_ready[u], i + 1)
                            dve.wait_ge(sq_ready[u], i)
                            dve.wait_ge(out_ready[u], i)
                            dve.tensor_tensor(dev[:, u, :], at(src, i * 2 * CH + u * CH, CH), mean[:, u, :],
                                              ALU.subtract).then_inc(dev_ready[u], 1)
                    for u in range(2):
                        dve.wait_ge(sd_ready[u], i + 1)
                        dve.wait_ge(out_ready[u], i)
                        dve.reciprocal(rs[:, u, :], sd[:, u, :]).then_inc(rs_ready[u], 1)
                    for u in range(2):
                        dve.wait_ge(rs_ready[u], i + 1)
                        out = at(dst, i * 2 * CH + u * CH, CH)
                        if centre and weight is None:
                            dve.tensor_tensor(out, dev[:, u, :], rs[:, u, :], ALU.mult).then_inc(out_ready[u], 1)
                        else:
                            in0 = dev[:, u, :] if centre else at(src, i * 2 * CH + u * CH, CH)
                            ins = dve.scalar_tensor_tensor(out=out, in0=in0, scalar=weight[:, 0:1], in1=rs[:, u, :],
                                                           op0=ALU.mult, op1=ALU.mult)
                            if shift is not None:
                                ins.then_inc(scaled, 1)
                                dve.wait_ge(scaled, 2 * i + u + 1)
                                ins = dve.tensor_scalar(out, out, shift[:, 0:1], None, ALU.add)
                            ins.then_inc(out_ready[u], 1)


def mamba_inputs(nc, io, x2, gate, xs, consts):
    with stage(nc, "mi") as (sb, ps, sem):
        w = sb("w", [P, 2, 2, P])
        cw = sb("cw", [P, 2, NT])
        cb = sb("cb", [P, 2])
        padded = sb("padded", [P, 2, NT - 1 + L])
        conv = sb("conv", [P, 2, L])
        pskip = ps("pskip", [P, 2, L])
        pin = ps("pin", [P, 2, L])
        loaded = sem("loaded")
        pad_set = sem("pad_set")
        skip_ready = sem("skip_ready")
        gate_ready = sem("gate_ready")
        in_ready = sem("in_ready")
        padded_ready = sem("padded_ready")
        conv_steps = sem("conv_steps")
        conv_ready = sem("conv_ready")
        xs_ready = sem("xs_ready")
        with nc.Block() as block:
            @block.sync
            def _(sp):
                load(sp, loaded, [(w[:, :, :, :], io["m_w"]), (cw[:, :, :], io["m_cw"]), (cb[:, :], io["m_cb"])])
                sp.wait_ge(loaded, 48)

            @block.tensor
            def _(pe):
                pe.wait_ge(loaded, 48)
                with pe.Fori(0, B) as b:
                    for h in range(2):
                        pe.wait_ge(gate_ready, 2 * b)
                        for c in range(2):
                            mm = pe.matmul(pskip[:, h, c * CH:(c + 1) * CH], w[:, 0, h, :],
                                           at(x2, b * L + c * CH, CH), start=True, stop=True)
                        mm.then_inc(skip_ready, 1)
                    for h in range(2):
                        pe.wait_ge(padded_ready, 2 * b)
                        for c in range(2):
                            mm = pe.matmul(pin[:, h, c * CH:(c + 1) * CH], w[:, 1, h, :],
                                           at(x2, b * L + c * CH, CH), start=True, stop=True)
                        mm.then_inc(in_ready, 1)

            @block.scalar
            def _(act):
                act.wait_ge(pad_set, 1)
                with act.Fori(0, B) as b:
                    for h in range(2):
                        act.wait_ge(in_ready, 2 * b + h + 1)
                        act.wait_ge(conv_ready, 2 * b)
                        act.activation(padded[:, h, NT - 1:], pin[:, h, :], ACT.Copy).then_inc(padded_ready, 1)
                    for h in range(2):
                        act.wait_ge(skip_ready, 2 * b + h + 1)
                        act.activation(at(gate, (b * 2 + h) * L, L), pskip[:, h, :],
                                       ACT.Silu).then_inc(gate_ready, 1)
                    for h in range(2):
                        act.wait_ge(conv_ready, 2 * b + h + 1)
                        act.activation(at(xs, (b * 2 + h) * L, L), conv[:, h, :], ACT.Silu,
                                       bias=cb[:, h:h + 1]).then_inc(xs_ready, 1)

            @block.vector
            def _(dve):
                dve.memset(padded[:, :, 0:NT - 1], 0.0).then_inc(pad_set, 1)
                dve.wait_ge(loaded, 48)
                with dve.Fori(0, B) as b:
                    for h in range(2):
                        dve.wait_ge(padded_ready, 2 * b + h + 1)
                        dve.wait_ge(xs_ready, 2 * b)
                        dve.wait_ge(conv_ready, 2 * b + h)
                        for k in range(NT):
                            tap = padded[:, h, k:k + L]
                            if k == 0:
                                ins = dve.tensor_scalar(conv[:, h, :], tap, cw[:, h, 0:1], None, ALU.mult)
                            else:
                                ins = dve.scalar_tensor_tensor(out=conv[:, h, :], in0=tap, scalar=cw[:, h, k:k + 1],
                                                               in1=conv[:, h, :], op0=ALU.mult, op1=ALU.add)
                            if k < NT - 1:
                                ins.then_inc(conv_steps, 1)
                                dve.wait_ge(conv_steps, (2 * b + h) * (NT - 1) + k + 1)
                        ins.then_inc(conv_ready, 1)


def mamba_steps(nc, io, xs, delta, parts_b, parts_c):
    with stage(nc, "md") as (sb, ps, sem):
        w1 = sb("w1", [P, 2, DD])
        wbc = sb("wbc", [P, 2, 2, NPART * SP])
        w2 = sb("w2", [DD, 2, P])
        b2 = sb("b2", [P, 2])
        low = sb("low", [DD, L])
        rest = sb("rest", [NPART * SP, 2, L])
        mid = sb("mid", [NPART * SP, 2, L], BF16)
        z = sb("z", [P, 2, L])
        za = sb("za", [P, 2, L])
        one = sb("one", [P, 1])
        pslot = ps("pslot", [P, 4, L])
        plow, pb, pc = pslot[:, 0, :], pslot[:, 1, :], pslot[:, 2, :]
        pz = pslot[:, 3, :]
        loaded = sem("loaded")
        one_set = sem("one_set")
        low_mm, bc_mm, z_mm = sem("low_mm"), sem("bc_mm"), sem("z_mm")
        low_ready = sem("low_ready")
        hi_ready, rest_ready, mid_ready, lo_ready = sem("hi_ready"), sem("rest_ready"), sem("mid_ready"), sem("lo_ready")
        z_ready = sem("z_ready")
        soft_steps = sem("soft_steps")
        soft_ready = sem("soft_ready")
        delta_ready = sem("delta_ready")
        R = NPART * SP
        store = [parts_b, parts_c]
        with nc.Block() as block:
            @block.sync
            def _(sp):
                load(sp, loaded, [(w1[:, :, :], io["m_w1"]), (wbc[:, :, :, :], io["m_wbc"]),
                                  (w2[:, :, :], io["m_w2"]), (b2[:, :], io["m_b2"])])
                sp.wait_ge(loaded, 64)

            @block.tensor
            def _(pe):
                pe.wait_ge(loaded, 64)
                with pe.Fori(0, B) as b:
                    pe.wait_ge(low_ready, b)
                    for c in range(2):
                        for h in range(2):
                            mm = pe.matmul(plow[0:DD, c * CH:(c + 1) * CH], w1[:, h, :],
                                           at(xs, (b * 2 + h) * L + c * CH, CH), start=(h == 0), stop=(h == 1))
                    mm.then_inc(low_mm, 1)
                    for j, p in enumerate((pb, pc)):
                        pe.wait_ge(rest_ready, 2 * b)
                        for c in range(2):
                            for h in range(2):
                                mm = pe.matmul(p[0:R, c * CH:(c + 1) * CH], wbc[:, h, j, :],
                                               at(xs, (b * 2 + h) * L + c * CH, CH), start=(h == 0), stop=(h == 1))
                        mm.then_inc(bc_mm, 1)
                    pe.wait_ge(low_ready, b + 1)
                    for h in range(2):
                        pe.wait_ge(z_ready, 2 * b + h)
                        for c in range(2):
                            mm = pe.matmul(pz[:, c * CH:(c + 1) * CH], w2[:, h, :], low[:, c * CH:(c + 1) * CH],
                                           start=True, stop=True)
                        mm.then_inc(z_mm, 1)

            @block.scalar
            def _(act):
                act.wait_ge(loaded, 64)
                act.wait_ge(one_set, 1)
                with act.Fori(0, B) as b:
                    act.wait_ge(low_mm, b + 1)
                    act.wait_ge(z_mm, 2 * b)
                    act.activation(low[:, :], plow[0:DD, :], ACT.Copy).then_inc(low_ready, 1)
                    for j, p in enumerate((pb, pc)):
                        act.wait_ge(bc_mm, 2 * b + j + 1)
                        act.activation(store[j][:, bass.ds(b * L, L)], p[0:R, :], ACT.Copy).then_inc(hi_ready, 1)
                    for h in range(2):
                        act.wait_ge(z_mm, 2 * b + h + 1)
                        act.wait_ge(delta_ready, 2 * b)
                        act.activation(z[:, h, :], pz[:, :], ACT.Identity, bias=b2[:, h:h + 1]).then_inc(z_ready, 1)
                    for j in range(2):
                        act.wait_ge(rest_ready, 2 * b + j + 1)
                        act.activation(store[j][SP:2 * SP, bass.ds(b * L, L)], rest[SP:2 * SP, j, :],
                                       ACT.Copy).then_inc(mid_ready, 1)
                        act.wait_ge(lo_ready, 2 * b)
                        act.activation(mid[2 * SP:R, j, :], rest[2 * SP:R, j, :], ACT.Copy).then_inc(mid_ready, 1)
                    step = Steps(act, soft_steps, 6 * b)
                    for h in range(2):
                        act.wait_ge(z_ready, 2 * b + h + 1)
                        act.wait_ge(delta_ready, 2 * b)
                        step(act.activation(za[:, h, :], z[:, h, :], ACT.Abs))
                        step(act.activation(za[:, h, :], za[:, h, :], ACT.Exp, scale=-1.0))
                        step(act.activation(za[:, h, :], za[:, h, :], ACT.Ln, bias=one[:, 0:1]))

            @block.vector
            def _(dve):
                dve.memset(one[:, :], 1.0).then_inc(one_set, 1)
                with dve.Fori(0, B) as b:
                    for j, p in enumerate((pb, pc)):
                        dve.wait_ge(hi_ready, 2 * b + j + 1)
                        dve.wait_ge(mid_ready, 4 * b)
                        dve.wait_ge(lo_ready, 2 * b)
                        dve.tensor_tensor(rest[:, j, :], p[0:R, :], store[j][:, bass.ds(b * L, L)],
                                          ALU.subtract).then_inc(rest_ready, 1)
                    for j in range(2):
                        dve.wait_ge(mid_ready, 4 * b + 2 * j + 2)
                        dve.wait_ge(rest_ready, 2 * b + j + 1)
                        dve.tensor_tensor(store[j][2 * SP:R, bass.ds(b * L, L)], rest[2 * SP:R, j, :], mid[2 * SP:R, j, :],
                                          ALU.subtract).then_inc(lo_ready, 1)
                    for h in range(2):
                        dve.wait_ge(soft_steps, 6 * b + 3 * h + 3)
                        dve.scalar_tensor_tensor(out=at(delta, (b * 2 + h) * L, L), in0=z[:, h, :], scalar=0.0,
                                                 in1=za[:, h, :], op0=ALU.max, op1=ALU.add).then_inc(delta_ready, 1)


def mamba_scan(nc, io, xs, gate, delta, parts_b, parts_c, ident):
    R = NPART * SP
    with stage(nc, "ms") as (sb, ps, sem):
        sel = sb("sel", [R, NS, P], BF16)
        a_log = sb("a_log", [P, 2, NS])
        a_exp = sb("a_exp", [P, 2, NS])
        a_neg = sb("a_neg", [P, 2, NS])
        w_d = sb("w_d", [P, 2])
        a_cur = sb("a_cur", [P, NS])
        d_cur = sb("d_cur", [P, 1])
        u = sb("u", [P, L])
        decay = sb("decay", [P, 2, L])
        c_sb = sb("c_sb", [P, 2, L])
        drive = sb("drive", [P, 2, L])
        hs = sb("hs", [P, 2, L])
        hc = sb("hc", [P, 2, L])
        y1 = sb("y1", [P, L])
        p_b = ps("p_b", [P, 2, L])
        p_c = ps("p_c", [P, L])
        p_y = ps("p_y", [P, L])
        loaded = sem("loaded")
        a_ready = sem("a_ready")
        cur_ready = sem("cur_ready")
        b_mm, c_mm, y_mm = sem("b_mm"), sem("c_mm"), sem("y_mm")
        decay_ready, c_ready = sem("decay_ready"), sem("c_ready")
        drive_ready, h_ready, hc_ready = sem("drive_ready"), sem("h_ready"), sem("hc_ready")
        y1_ready, y_done = sem("y1_ready"), sem("y_done")
        with nc.Block() as block:
            @block.sync
            def _(sp):
                load(sp, loaded, [(sel[:, :, :], io["m_sel"]), (a_log[:, :, :], io["m_alog"]), (w_d[:, :], io["m_wd"])])
                sp.wait_ge(loaded, 48)

            @block.tensor
            def _(pe):
                pe.wait_ge(loaded, 48)
                with pe.Fori(0, B) as b, pe.Fori(0, 2) as h:
                    it = b * 2 + h

                    def spread(n):
                        if n >= 2:
                            pe.wait_ge(drive_ready, it * NS + n - 1)
                        else:
                            pe.wait_ge(drive_ready, it * NS)
                        for c in range(2):
                            mm = pe.matmul(p_b[:, n % 2, c * CH:(c + 1) * CH], sel[:, n, :],
                                           parts_b[:, bass.ds(b * L + c * CH, CH)], start=True, stop=True)
                        mm.then_inc(b_mm, 1)
                        pe.wait_ge(c_ready, it * NS + n)
                        for c in range(2):
                            mm = pe.matmul(p_c[:, c * CH:(c + 1) * CH], sel[:, n, :],
                                           parts_c[:, bass.ds(b * L + c * CH, CH)], start=True, stop=True)
                        mm.then_inc(c_mm, 1)

                    def add(n):
                        if n == 0:
                            pe.wait_ge(y1_ready, it)
                        pe.wait_ge(hc_ready, it * NS + n + 1)
                        for c in range(2):
                            mm = pe.matmul(p_y[:, c * CH:(c + 1) * CH], ident[:, :], hc[:, n % 2, c * CH:(c + 1) * CH],
                                           start=(n == 0), stop=(n == NS - 1))
                        mm.then_inc(y_mm, 1)

                    spread(0)
                    for n in range(NS):
                        if n + 1 < NS:
                            spread(n + 1)
                        if n >= 1:
                            add(n - 1)
                    add(NS - 1)

            @block.scalar
            def _(act):
                act.wait_ge(loaded, 48)
                act.activation(a_exp[:, :, :], a_log[:, :, :], ACT.Exp).then_inc(a_ready, 1)
                with act.Fori(0, B) as b, act.Fori(0, 2) as h:
                    it = b * 2 + h
                    act.wait_ge(cur_ready, it + 1)
                    for n in range(NS):
                        if n >= 2:
                            wait_apart(act, h_ready, it * NS + n - 1)
                        act.activation(decay[:, n % 2, :], at(delta, it * L, L), ACT.Exp,
                                       scale=a_cur[:, n:n + 1]).then_inc(decay_ready, 1)
                        act.wait_ge(c_mm, it * NS + n + 1)
                        if n >= 2:
                            act.wait_ge(hc_ready, it * NS + n - 1)
                        else:
                            act.wait_ge(hc_ready, it * NS)
                        act.activation(c_sb[:, n % 2, :], p_c[:, :], ACT.Copy).then_inc(c_ready, 1)

            @block.gpsimd
            def _(pool):
                with pool.Fori(0, B * 2) as it:
                    for n in range(NS):
                        pool.wait_ge(h_ready, it * NS + n + 1)
                        pool.wait_ge(c_ready, it * NS + n + 1)
                        if n >= 2:
                            pool.wait_ge(y_mm, it * NS + n - 1)
                        else:
                            pool.wait_ge(y_mm, it * NS)
                        pool.tensor_tensor(hc[:, n % 2, :], hs[:, n % 2, :], c_sb[:, n % 2, :],
                                           ALU.mult).then_inc(hc_ready, 1)

            @block.vector
            def _(dve):
                dve.wait_ge(a_ready, 1)
                dve.tensor_scalar(a_neg[:, :, :], a_exp[:, :, :], -1.0, None, ALU.mult).then_inc(a_ready, 1)
                dve.wait_ge(a_ready, 2)
                with dve.Fori(0, B) as b, dve.Fori(0, 2) as h:
                    it = b * 2 + h
                    dve.wait_ge(decay_ready, it * NS)
                    dve.wait_ge(y_done, it)
                    dve.tensor_copy(a_cur[:, :], a_neg[:, bass.ds(h, 1), :].rearrange("p a n -> p (a n)"))
                    dve.tensor_copy(d_cur[:, :], w_d[:, bass.ds(h, 1)])
                    dve.tensor_tensor(u[:, :], at(delta, it * L, L), at(xs, it * L, L),
                                      ALU.mult).then_inc(cur_ready, 1)
                    dve.wait_ge(cur_ready, it + 1)
                    for n in range(NS):
                        dve.wait_ge(b_mm, it * NS + n + 1)
                        if n >= 2:
                            dve.wait_ge(h_ready, it * NS + n - 1)
                        dve.tensor_tensor(drive[:, n % 2, :], p_b[:, n % 2, :], u[:, :],
                                          ALU.mult).then_inc(drive_ready, 1)
                        dve.wait_ge(drive_ready, it * NS + n + 1)
                        dve.wait_ge(decay_ready, it * NS + n + 1)
                        if n >= 2:
                            dve.wait_ge(hc_ready, it * NS + n - 1)
                        else:
                            dve.wait_ge(hc_ready, it * NS)
                        dve.tensor_tensor_scan(hs[:, n % 2, :], decay[:, n % 2, :], drive[:, n % 2, :], 0.0,
                                               ALU.mult, ALU.add).then_inc(h_ready, 1)
                    dve.wait_ge(y_mm, it * NS + NS)
                    dve.scalar_tensor_tensor(out=y1[:, :], in0=at(xs, it * L, L), scalar=d_cur[:, 0:1], in1=p_y[:, :],
                                             op0=ALU.mult, op1=ALU.add).then_inc(y1_ready, 1)
                    dve.wait_ge(y1_ready, it + 1)
                    dve.tensor_tensor(at(xs, it * L, L), y1[:, :], at(gate, it * L, L),
                                      ALU.mult).then_inc(y_done, 1)


def mamba_out(nc, io, y, xn, s):
    with stage(nc, "mo") as (sb, ps, sem):
        w = sb("w", [P, 2, P])
        p = ps("p", [P, 2, L])
        loaded = sem("loaded")
        mm_ready = [sem(f"mm_ready{u}") for u in range(2)]
        s_ready = [sem(f"s_ready{u}") for u in range(2)]
        with nc.Block() as block:
            @block.sync
            def _(sp):
                load(sp, loaded, [(w[:, :, :], io["m_wo"])])
                sp.wait_ge(loaded, 16)

            @block.tensor
            def _(pe):
                pe.wait_ge(loaded, 16)
                with pe.Fori(0, B // 2) as i:
                    for u in range(2):
                        b = i * 2 + u
                        pe.wait_ge(s_ready[u], i)
                        for c in range(2):
                            for h in range(2):
                                mm = pe.matmul(p[:, u, c * CH:(c + 1) * CH], w[:, h, :],
                                               at(y, (b * 2 + h) * L + c * CH, CH), start=(h == 0), stop=(h == 1))
                        mm.then_inc(mm_ready[u], 1)

            @block.vector
            def _(dve):
                with dve.Fori(0, B // 2) as i:
                    for u in range(2):
                        dve.wait_ge(mm_ready[u], i + 1)
                        dve.tensor_tensor(at(s, (i * 2 + u) * L, L), at(xn, (i * 2 + u) * L, L), p[:, u, :],
                                          ALU.add).then_inc(s_ready[u], 1)


def route(nc, io, tag, xn, comb, experts, per_group, top, kind):
    E, EG = experts, per_group
    NG = E // EG
    R = NPART * EG + 1
    TT = CH // P
    grouped = kind.startswith("grouped")
    PAD = 256 if E > P else P
    with stage(nc, "r" + tag) as (sb, ps, sem):
        w = sb("w", [P, E])
        bias = sb("bias", [P, E])
        tri = sb("tri", [P, 4, 4])
        xst = sb("xst", [P, 2, CH])
        lin = sb("lin", [P, 2, TT, E])
        sc = sb("sc", [P, 2, TT, E])
        biased = sb("biased", [P, TT, E])
        pair = sb("pair", [P, TT * 4, 6])
        gsum = sb("gsum", [P, TT * 4])
        beats = sb("beats", [P, TT, 4, 4])
        ties = sb("ties", [P, TT, 4, 4])
        rank = sb("rank", [P, TT * 4])
        gmask = sb("gmask", [P, TT * 4])
        glow = sb("glow", [P, TT * 4])
        cand = sb("cand", [P, TT, E])
        top8 = sb("top8", [P, TT, 8])
        above = sb("above", [P, TT, E])
        equal = sb("equal", [P, TT, E])
        order = sb("order", [P, TT, E])
        ones = sb("ones", [P, E])
        count = sb("count", [P, TT])
        need = sb("need", [P, TT])
        low = sb("low", [P, TT, E])
        weight = sb("weight", [P, TT, E])
        total = sb("total", [P, TT])
        recip = sb("recip", [P, TT])
        rest = sb("rest", [P, TT, E])
        parts = sb("parts", [P, 2, TT, NG, R], BF16)
        plog = ps("plog", [P, 2, TT, PAD])
        pt = ps("pt", [P, NG, 2 * CH], BF16)
        loaded, set_up = sem("loaded"), sem("set_up")
        staged = [sem(f"staged{u}") for u in range(2)]
        logit_mm = [sem(f"logit_mm{u}") for u in range(2)]
        lin_ready = [sem(f"lin_ready{u}") for u in range(2)]
        sc_ready = [sem(f"sc_ready{u}") for u in range(2)]
        steps = sem("steps")
        parts_ready = [sem(f"parts_ready{u}") for u in range(2)]
        turned = sem("turned")
        comb_ready = sem("comb_ready")
        identb = io["sb_identb"]
        loads = [(w[:, :], io[f"r{tag}_w"]), (tri[:, :, :], io["tri"])]
        has_bias = kind != "softmax"
        if has_bias:
            loads.append((bias[:, :], io[f"r{tag}_b"]))
        NL = 16 * len(loads)
        prob_steps = 3 if kind == "softmax" else 0
        period = {"softmax": 0, "sigmoid": 0, "grouped": 12, "grouped_low": 14}[kind] + prob_steps
        period += 2 * TT + 8 + (0 if kind == "softmax" else 4 if kind != "sigmoid" else 5) + 3

        def wide(t, n):
            return t[:, :].unsqueeze(2).to_broadcast([P, TT, n])

        with nc.Block() as block:
            @block.sync
            def _(sp):
                load(sp, loaded, loads)
                sp.wait_ge(loaded, NL)

            @block.gpsimd
            def _(pool):
                with pool.Fori(0, NC // 2) as i:
                    for u in range(2):
                        pool.wait_ge(logit_mm[u], i)
                        pool.tensor_copy(xst[:, u, :], at(xn, i * 2 * CH + u * CH, CH)).then_inc(staged[u], 1)

            @block.tensor
            def _(pe):
                pe.wait_ge(loaded, NL)
                with pe.Fori(0, NC // 2) as i:
                    for u in range(2):
                        pe.wait_ge(staged[u], i + 1)
                        pe.wait_ge(sc_ready[u], i)
                        for t in range(TT):
                            mm = pe.matmul(plog[:, u, t, 0:E], xst[:, u, t * P:(t + 1) * P], w[:, :],
                                           start=True, stop=True)
                        mm.then_inc(logit_mm[u], 1)
                    for u in range(2):
                        pe.wait_ge(parts_ready[u], i + 1)
                        for g in range(NG):
                            wait_apart(pe, comb_ready, (2 * i + u) * NG)
                            for t in range(TT):
                                mm = pe.transpose(pt[0:R, g, t * P:(t + 1) * P], parts[:, u, t, g, :], identb[:, :])
                            mm.then_inc(turned, 1)

            @block.scalar
            def _(act):
                with act.Fori(0, NC // 2) as i:
                    for u in range(2):
                        act.wait_ge(parts_ready[u], i)
                        if kind == "softmax":
                            act.wait_ge(lin_ready[u], i + 1)
                            act.activation(sc[:, u], lin[:, u], ACT.Exp).then_inc(sc_ready[u], 1)
                        elif kind == "sigmoid":
                            act.wait_ge(lin_ready[u], i + 1)
                            act.activation(sc[:, u], lin[:, u], ACT.Sigmoid).then_inc(sc_ready[u], 1)
                        else:
                            act.wait_ge(logit_mm[u], i + 1)
                            act.activation(sc[:, u], plog[:, u, :, 0:E], ACT.Sigmoid).then_inc(sc_ready[u], 1)
                    for u in range(2):
                        for g in range(NG):
                            act.wait_ge(turned, (2 * i + u) * NG + g + 1)
                            act.activation(comb[0:R, g, bass.ds(i * 2 * CH + u * CH, CH)], pt[0:R, g, 0:CH],
                                           ACT.Copy).then_inc(comb_ready, 1)

            @block.vector
            def _(dve):
                dve.memset(parts[:, :, :, :, R - 1:R], 1.0).then_inc(set_up, 1)
                dve.memset(ones[:, :], 1.0).then_inc(set_up, 1)
                dve.wait_ge(set_up, 2)
                dve.wait_ge(loaded, NL)
                with dve.Fori(0, NC // 2) as i:
                    if kind in ("softmax", "sigmoid"):
                        for u in range(2):
                            dve.wait_ge(logit_mm[u], i + 1)
                            dve.wait_ge(sc_ready[u], i)
                            if kind == "softmax":
                                step = Steps(dve, steps, (2 * i + u) * 1 + 2 * i * period + 0)
                                ins = dve.tensor_reduce(total[:, :], plog[:, u, :, 0:E], AX.X, ALU.max)
                                step(ins)
                                dve.tensor_tensor(lin[:, u], plog[:, u, :, 0:E], wide(total, E),
                                                  ALU.subtract).then_inc(lin_ready[u], 1)
                                dve.wait_ge(lin_ready[u], i + 1)
                            else:
                                dve.tensor_tensor(lin[:, u], plog[:, u, :, 0:E],
                                                  bias[:, :].unsqueeze(1).to_broadcast([P, TT, E]),
                                                  ALU.add).then_inc(lin_ready[u], 1)
                    extra = 2 if kind == "softmax" else 0
                    for u in range(2):
                        dve.wait_ge(sc_ready[u], i + 1)
                        wait_apart(dve, turned, (2 * i + u) * NG)
                        step = Steps(dve, steps, (2 * i + u) * period + (2 * i + 2 if extra else 0))
                        score = sc[:, u]
                        if kind == "softmax":
                            step(dve.tensor_reduce(total[:, :], score, AX.X, ALU.add))
                            step(dve.reciprocal(recip[:, :], total[:, :]))
                            step(dve.tensor_tensor(cand[:, :, :], score, wide(recip, E), ALU.mult), apart=True)
                            score = cand[:, :, :]
                        elif kind == "sigmoid":
                            pass
                        else:
                            step(dve.tensor_tensor(biased[:, :, :], score,
                                                   bias[:, :].unsqueeze(1).to_broadcast([P, TT, E]), ALU.add))
                            four = biased[:, :, :].rearrange("p t (g e) -> p (t g) e", e=4)
                            for o, n, d in ((0, 3, 1), (3, 2, 2), (5, 1, 3)):
                                step(dve.tensor_tensor(pair[:, :, o:o + n], four[:, :, 0:n], four[:, :, d:d + n], ALU.add))
                            step(dve.tensor_reduce(gsum[:, :], pair[:, :, :], AX.X, ALU.max))
                            mine = gsum[:, :].rearrange("p (t g) -> p t g", g=4).unsqueeze(3).to_broadcast([P, TT, 4, 4])
                            other = gsum[:, :].rearrange("p (t g) -> p t g", g=4).unsqueeze(2).to_broadcast([P, TT, 4, 4])
                            step(dve.tensor_tensor(beats[:, :, :, :], other, mine, ALU.is_gt))
                            step(dve.tensor_tensor(ties[:, :, :, :], other, mine, ALU.is_equal))
                            step(dve.tensor_tensor(ties[:, :, :, :], ties[:, :, :, :],
                                                   tri[:, :, :].unsqueeze(1).to_broadcast([P, TT, 4, 4]), ALU.mult))
                            step(dve.tensor_tensor(beats[:, :, :, :], beats[:, :, :, :], ties[:, :, :, :], ALU.add))
                            step(dve.tensor_reduce(rank[:, :], beats[:, :, :, :], AX.X, ALU.add))
                            step(dve.tensor_scalar(gmask[:, :], rank[:, :], 2.0, None, ALU.is_lt))
                            cand4 = cand[:, :, :].rearrange("p t (g e) -> p (t g) e", e=4)
                            step(dve.tensor_tensor(cand4, four, gmask[:, :].unsqueeze(2).to_broadcast([P, TT * 4, 4]),
                                                   ALU.mult), apart=True)
                            if kind == "grouped_low":
                                step(dve.tensor_scalar(glow[:, :], gmask[:, :], BIG, -BIG, ALU.mult, ALU.add))
                                step(dve.tensor_tensor(cand4, cand4, glow[:, :].unsqueeze(2).to_broadcast([P, TT * 4, 4]),
                                                       ALU.add), apart=True)
                        src = sc[:, u] if kind == "sigmoid" else cand[:, :, :]
                        for t in range(TT):
                            step(dve.max(top8[:, t, :], src[:, t, :]), apart=True)
                        least = top8[:, :, top - 1:top].to_broadcast([P, TT, E])
                        step(dve.tensor_tensor(above[:, :, :], src, least, ALU.is_gt))
                        step(dve.tensor_tensor(equal[:, :, :], src, least, ALU.is_equal))
                        step(dve.tensor_reduce(count[:, :], above[:, :, :], AX.X, ALU.add))
                        step(dve.tensor_scalar(need[:, :], count[:, :], -1.0, float(top), ALU.mult, ALU.add))
                        for t in range(TT):
                            step(dve.tensor_tensor_scan(order[:, t, :], ones[:, :], equal[:, t, :], 0.0,
                                                        ALU.mult, ALU.add))
                        step(dve.tensor_tensor(low[:, :, :], order[:, :, :], wide(need, E), ALU.is_le))
                        step(dve.tensor_tensor(equal[:, :, :], equal[:, :, :], low[:, :, :], ALU.mult))
                        step(dve.tensor_tensor(above[:, :, :], above[:, :, :], equal[:, :, :], ALU.add))
                        step(dve.tensor_tensor(weight[:, :, :], score, above[:, :, :], ALU.mult))
                        if kind != "softmax":
                            step(dve.tensor_reduce(total[:, :], weight[:, :, :], AX.X, ALU.add))
                            step(dve.tensor_scalar(total[:, :], total[:, :], 1e-9 if kind == "sigmoid" else 1e-20, None,
                                                   ALU.add))
                            step(dve.reciprocal(recip[:, :], total[:, :]))
                            if kind == "sigmoid":
                                step(dve.tensor_scalar(recip[:, :], recip[:, :], 2.5, None, ALU.mult))
                            step(dve.tensor_tensor(weight[:, :, :], weight[:, :, :], wide(recip, E), ALU.mult))
                        wv = weight[:, :, :].rearrange("p t (g e) -> p t g e", e=EG)
                        rv = rest[:, :, :].rearrange("p t (g e) -> p t g e", e=EG)
                        part = [parts[:, u, :, :, a * EG:(a + 1) * EG] for a in range(NPART)]
                        step(dve.tensor_copy(part[0], wv))
                        step(dve.tensor_tensor(rv, wv, part[0], ALU.subtract))
                        step(dve.tensor_copy(part[1], rv))
                        dve.tensor_tensor(part[2], rv, part[1], ALU.subtract).then_inc(parts_ready[u], 1)
                        dve.wait_ge(parts_ready[u], i + 1)
                        assert step.n == period, (kind, step.n, period)


def experts_sum(nc, io, tag, xn, s, x, comb, R, groups, per_group, resident, up, first_load=(), out=None):
    W = 3 if up else 2
    NQ = groups * per_group
    NR = resident
    NB = NQ * 4 + NR
    NSEL = per_group * 4 + NR
    with stage(nc, "e" + tag) as (sb, ps, sem):
        ring = sb("ring", [P, 4, W, P])
        keep = sb("keep", [P, NR, W, P])
        sel = sb("sel", [R, NSEL, P], BF16)
        sg = sb("sg", [P, 2, CH])
        prod = sb("prod", [P, 2, CH])
        hid = sb("hid", [P, 2, CH])
        fs = sb("fs", [P, CH])
        sfs = sb("sfs", [P, CH])
        pg = ps("pg", [P, 2, CH])
        pu = ps("pu", [P, 2, CH])
        pw = ps("pw", [P, 2, CH])
        acc = ps("acc", [P, CH])
        loaded = sem("loaded")
        ring_loaded = [sem(f"ring_loaded{u}") for u in range(4)]
        gate_mm, block_mm = sem("gate_mm"), sem("block_mm")
        sg_ready, prod_ready, hid_ready = sem("sg_ready"), sem("prod_ready"), sem("hid_ready")
        ring_done = [sem(f"ring_done{u}") for u in range(4)]
        keep_done = sem("keep_done")
        fs_ready, x_steps, written = sem("fs_ready"), sem("x_steps"), sem("written")
        loads = [(keep[:, :, :, :], io[f"e{tag}_w"][:, NQ * 4:, :, :]), (sel[:, :, :], io[f"e{tag}_sel"])] + list(first_load)
        NL = 16 * len(loads)
        wd = io[f"e{tag}_w"]

        def blocks(c, eng, visit):
            if NQ:
                for u in range(4):
                    visit(u, u, 0, True)
                if NQ > 1:
                    with eng.Fori(1, NQ) as q:
                        for u in range(4):
                            visit(q * 4 + u, u, q, True)
            for r in range(NR):
                visit(NQ * 4 + r, r, None, False)

        with nc.Block() as block:
            @block.sync
            def _(sp):
                load(sp, loaded, loads)
                if NQ:
                    with sp.Fori(0, NC) as c, sp.Fori(0, NQ) as q:
                        for u in range(4):
                            sp.wait_ge(ring_done[u], c * NQ + q)
                            sp.dma_start(ring[:, u, :, :],
                                         wd[:, bass.ds(q * 4 + u, 1), :, :].rearrange("p a w m -> p (a w) m")
                                         ).then_inc(ring_loaded[u], 16)
                sp.wait_ge(loaded, NL)

            @block.tensor
            def _(pe):
                pe.wait_ge(loaded, NL)
                with pe.Fori(0, NC) as c:
                    base = c * NB
                    prev = []

                    def down(k, u, in_ring, first, last):
                        pe.wait_ge(hid_ready, base + k + 1)
                        if first:
                            pe.wait_ge(fs_ready, c)
                        w = ring if in_ring else keep
                        mm = pe.matmul(acc[:, :], w[:, u, W - 1, :], hid[:, u % 2, :], start=first, stop=last)
                        mm.then_inc(ring_done[u] if in_ring else keep_done, 1)

                    def visit(k, u, q, in_ring):
                        w = ring if in_ring else keep
                        if in_ring:
                            pe.wait_ge(ring_loaded[u], 16 * (c * NQ + q + 1))
                        if isinstance(k, int) and k < 2:
                            pe.wait_ge(hid_ready, base)
                        else:
                            pe.wait_ge(hid_ready, base + k - 1)
                        xc = at(xn, c * CH, CH)
                        pe.matmul(pg[:, u % 2, :], w[:, u, 0, :], xc, start=True, stop=True).then_inc(gate_mm, 1)
                        if up:
                            pe.matmul(pu[:, u % 2, :], w[:, u, 1, :], xc, start=True, stop=True)
                        if in_ring:
                            si = (q % per_group) * 4 + u if groups > 1 else q * 4 + u
                            lhs = sel[:, bass.ds(si, 1), :].rearrange("r a m -> r (a m)")
                            gi = q // per_group if groups > 1 else 0
                        else:
                            lhs, gi = sel[:, per_group * 4 + u, :], 0
                        rhs = comb[0:R, bass.ds(gi, 1), bass.ds(c * CH, CH)].rearrange("r a t -> r (a t)")
                        pe.matmul(pw[:, u % 2, :], lhs, rhs, start=True, stop=True).then_inc(block_mm, 1)
                        if in_ring:
                            if u > 0:
                                down(k - 1, u - 1, True, isinstance(k, int) and k == 1, False)
                            elif not isinstance(k, int):
                                down(k - 1, 3, True, False, False)
                        elif u > 0:
                            down(k - 1, u - 1, False, k == 1, False)
                        elif NQ:
                            down(k - 1, 3, True, False, False)

                    blocks(c, pe, visit)
                    down(NB - 1, NR - 1, False, NB == 1, True)

            @block.scalar
            def _(act):
                with act.Fori(0, NC) as c:
                    base = c * NB

                    def visit(k, u, q, in_ring):
                        act.wait_ge(gate_mm, base + k + 1)
                        if isinstance(k, int) and k < 2:
                            act.wait_ge(hid_ready, base)
                        else:
                            act.wait_ge(hid_ready, base + k - 1)
                        act.activation(sg[:, u % 2, :], pg[:, u % 2, :], ACT.Silu).then_inc(sg_ready, 1)

                    blocks(c, act, visit)
                    act.wait_ge(keep_done, (c + 1) * NR)
                    act.wait_ge(x_steps, 2 * c)
                    act.activation(fs[:, :], acc[:, :], ACT.Silu).then_inc(fs_ready, 1)

            @block.vector
            def _(dve):
                with dve.Fori(0, NC) as c:
                    base = c * NB

                    def visit(k, u, q, in_ring):
                        dve.wait_ge(sg_ready, base + k + 1)
                        dve.wait_ge(block_mm, base + k + 1)
                        if in_ring:
                            if u >= 2:
                                dve.wait_ge(ring_done[u - 2], c * NQ + q + 1)
                            else:
                                dve.wait_ge(ring_done[u + 2], c * NQ + q)
                                dve.wait_ge(keep_done, c * NR)
                        elif u >= 2:
                            dve.wait_ge(keep_done, c * NR + u - 1)
                        elif NQ:
                            dve.wait_ge(ring_done[u + 2], (c + 1) * NQ)
                        else:
                            dve.wait_ge(keep_done, c * NR)
                        gate = sg[:, u % 2, :]
                        if isinstance(k, int) and k < 2:
                            dve.wait_ge(hid_ready, base)
                        else:
                            dve.wait_ge(hid_ready, base + k - 1)
                        if up:
                            dve.tensor_tensor(prod[:, u % 2, :], pu[:, u % 2, :], gate, ALU.mult).then_inc(prod_ready, 1)
                            dve.wait_ge(prod_ready, base + k + 1)
                            gate = prod[:, u % 2, :]
                        dve.tensor_tensor(hid[:, u % 2, :], pw[:, u % 2, :], gate, ALU.mult).then_inc(hid_ready, 1)

                    blocks(c, dve, visit)

            @block.gpsimd
            def _(pool):
                pool.wait_ge(loaded, NL)
                with pool.Fori(0, NC) as c:
                    pool.wait_ge(fs_ready, c + 1)
                    pool.tensor_tensor(sfs[:, :], at(s, c * CH, CH), fs[:, :], ALU.mult).then_inc(x_steps, 1)
                    pool.wait_ge(x_steps, 2 * c + 1)
                    pool.tensor_tensor(at(x, c * CH, CH), at(x, c * CH, CH), sfs[:, :], ALU.add).then_inc(x_steps, 1)
                    wait_apart(pool, x_steps, 2 * c + 2)
                    if out is not None:
                        pool.dma_start(out[:, bass.ds(c * CH, CH)], at(x, c * CH, CH)).then_inc(written, 16)
                if out is not None:
                    pool.wait_ge(written, 16 * NC)


def angles(nc, io, cos, sin):
    two_pi = 2 * np.pi
    c1 = 6.28125
    c2 = float(np.float32(np.round((two_pi - c1) * 2**21) / 2**21))
    c3 = float(np.float32(two_pi - c1 - c2))
    magic = 1.5 * 2**23
    with stage(nc, "an") as (sb, ps, sem):
        pos = sb("pos", [P, L])
        theta = sb("theta", [P, 1])
        ang = sb("ang", [P, L])
        turns = sb("turns", [P, L])
        mag = sb("mag", [P, L])
        quarter = sb("quarter", [P, 1])
        loaded, steps, table = sem("loaded"), sem("steps"), sem("table")
        with nc.Block() as block:
            @block.sync
            def _(sp):
                load(sp, loaded, [(pos[:, :], io["pos"]), (theta[:, :], io["a1_theta"])])
                sp.wait_ge(loaded, 32)

            @block.vector
            def _(dve):
                dve.wait_ge(loaded, 32)
                step = Steps(dve, steps)
                step(dve.memset(quarter[:, :], np.pi / 2))
                step(dve.tensor_scalar(ang[:, :], pos[:, :], theta[:, 0:1], None, ALU.mult))
                step(dve.tensor_scalar(turns[:, :], ang[:, :], 1 / two_pi, magic, ALU.mult, ALU.add))
                step(dve.tensor_scalar(turns[:, :], turns[:, :], -magic, None, ALU.add))
                for c in (c1, c2, c3):
                    step(dve.scalar_tensor_tensor(out=ang[:, :], in0=turns[:, :], scalar=-c, in1=ang[:, :],
                                                  op0=ALU.mult, op1=ALU.add))
                step(dve.tensor_scalar(ang[:, :], ang[:, :], 3.1415925, -3.1415925, ALU.min, ALU.max))

            @block.scalar
            def _(act):
                act.wait_ge(steps, 8)
                act.activation(mag[:, :], ang[:, :], ACT.Abs).then_inc(table, 1)
                act.activation(sin[:, :], ang[:, :], ACT.Sin).then_inc(table, 1)
                act.wait_ge(table, 2)
                act.activation(cos[:, :], mag[:, :], ACT.Sin, scale=-1.0, bias=quarter[:, 0:1]).then_inc(table, 1)


def project_linear(nc, io, xn, feat, v, cos, sin):
    with stage(nc, "p1") as (sb, ps, sem):
        wq, wk, wv = sb("wq", [P, P]), sb("wk", [P, P]), sb("wv", [P, P])
        xst = sb("xst", [P, L])
        qk = sb("qk", [P, 2, L])
        pq = ps("pq", [P, 2, L])
        pv = ps("pv", [P, L])
        loaded, staged, qk_mm, v_mm = sem("loaded"), sem("staged"), sem("qk_mm"), sem("v_mm")
        qk_ready, v_ready, feat_ready = sem("qk_ready"), sem("v_ready"), sem("feat_ready")
        with nc.Block() as block:
            @block.sync
            def _(sp):
                load(sp, loaded, [(wq[:, :], io["a1_wq"]), (wk[:, :], io["a1_wk"]), (wv[:, :], io["a1_wv"])])
                sp.wait_ge(loaded, 48)

            @block.gpsimd
            def _(pool):
                with pool.Fori(0, B) as b:
                    pool.wait_ge(v_mm, b)
                    pool.tensor_copy(xst[:, :], at(xn, b * L, L)).then_inc(staged, 1)

            @block.tensor
            def _(pe):
                pe.wait_ge(loaded, 48)
                with pe.Fori(0, B) as b:
                    for j, w in enumerate((wq, wk)):
                        pe.wait_ge(qk_ready, 2 * b)
                        for c in range(2):
                            mm = pe.matmul(pq[:, j, c * CH:(c + 1) * CH], w[:, :], at(xn, b * L + c * CH, CH),
                                           start=True, stop=True)
                        mm.then_inc(qk_mm, 1)
                    pe.wait_ge(staged, b + 1)
                    pe.wait_ge(v_ready, b)
                    for t in range(KT):
                        mm = pe.matmul(pv[:, t * P:(t + 1) * P], xst[:, t * P:(t + 1) * P], wv[:, :],
                                       start=True, stop=True)
                    mm.then_inc(v_mm, 1)

            @block.scalar
            def _(act):
                with act.Fori(0, B) as b:
                    for j in range(2):
                        act.wait_ge(qk_mm, 2 * b + j + 1)
                        act.wait_ge(feat_ready, 4 * b)
                        act.activation(qk[:, j, :], pq[:, j, :], ACT.Silu).then_inc(qk_ready, 1)
                    act.wait_ge(v_mm, b + 1)
                    act.activation(at(v, b * L, L), pv[:, :], ACT.Copy).then_inc(v_ready, 1)

            @block.vector
            def _(dve):
                with dve.Fori(0, B) as b:
                    for j in range(2):
                        dve.wait_ge(qk_ready, 2 * b + j + 1)
                        for m, trig in enumerate((cos, sin)):
                            dve.tensor_tensor(at(feat, ((2 * j + m) * B + b) * L, L), qk[:, j, :], trig[:, :],
                                              ALU.mult).then_inc(feat_ready, 1)


def project_plain(nc, io, xn, feat, v):
    with stage(nc, "p2") as (sb, ps, sem):
        w = sb("w", [P, 4, P])
        xd = sb("xd", [P, L])
        pd = ps("pd", [P, L])
        pq = ps("pq", [P, 2, L])
        pv = ps("pv", [P, L])
        loaded, d_mm, qk_mm, v_mm = sem("loaded"), sem("d_mm"), sem("qk_mm"), sem("v_mm")
        d_ready, qk_ready, v_ready = sem("d_ready"), sem("qk_ready"), sem("v_ready")
        with nc.Block() as block:
            @block.sync
            def _(sp):
                load(sp, loaded, [(w[:, :, :], io["a2_w"])])
                sp.wait_ge(loaded, 16)

            @block.tensor
            def _(pe):
                pe.wait_ge(loaded, 16)
                with pe.Fori(0, B) as b:
                    for c in range(2):
                        mm = pe.matmul(pd[:, c * CH:(c + 1) * CH], w[:, 0, :], at(xn, b * L + c * CH, CH),
                                       start=True, stop=True)
                    mm.then_inc(d_mm, 1)
                    pe.wait_ge(d_ready, b + 1)
                    for j in range(2):
                        pe.wait_ge(qk_ready, 2 * b)
                        for c in range(2):
                            mm = pe.matmul(pq[:, j, c * CH:(c + 1) * CH], w[:, 1 + j, :], xd[:, c * CH:(c + 1) * CH],
                                           start=True, stop=True)
                        mm.then_inc(qk_mm, 1)
                    pe.wait_ge(v_ready, b)
                    for t in range(KT):
                        mm = pe.matmul(pv[:, t * P:(t + 1) * P], xd[:, t * P:(t + 1) * P], w[:, 3, :],
                                       start=True, stop=True)
                    mm.then_inc(v_mm, 1)

            @block.scalar
            def _(act):
                with act.Fori(0, B) as b:
                    act.wait_ge(d_mm, b + 1)
                    act.wait_ge(v_mm, b)
                    act.activation(xd[:, :], pd[:, :], ACT.Copy).then_inc(d_ready, 1)
                    for j in range(2):
                        act.wait_ge(qk_mm, 2 * b + j + 1)
                        act.activation(at(feat, (j * B + b) * L, L), pq[:, j, :], ACT.Copy,
                                       scale=float(HD) ** -0.25).then_inc(qk_ready, 1)

            @block.vector
            def _(dve):
                with dve.Fori(0, B) as b:
                    dve.wait_ge(v_mm, b + 1)
                    dve.tensor_copy(at(v, b * L, L), pv[:, :]).then_inc(v_ready, 1)


def project_rotary(nc, io, xn, feat, v):
    DC = 32
    with stage(nc, "p3") as (sb, ps, sem):
        w = sb("w", [P, 4, P])
        bias = sb("bias", [P, 4])
        wkv = sb("wkv", [P, DC])
        bkv = sb("bkv", [DC, 1])
        wv = sb("wv", [DC + 1, P])
        trig = sb("trig", [P, 2, L])
        ckv = sb("ckv", [DC + 1, L])
        rot = sb("rot", [P, 4, L])
        pre = sb("pre", [P, 2, L])
        pw = ps("pw", [P, 4, L])
        loaded, one_set, w_mm, c_mm, v_mm = sem("loaded"), sem("one_set"), sem("w_mm"), sem("c_mm"), sem("v_mm")
        rot_ready, pre_ready, feat_ready = sem("rot_ready"), sem("pre_ready"), sem("feat_ready")
        ckv_ready, v_ready = sem("ckv_ready"), sem("v_ready")
        with nc.Block() as block:
            @block.sync
            def _(sp):
                load(sp, loaded, [(w[:, :, :], io["a3_w"]), (bias[:, :], io["a3_b"]), (wkv[:, :], io["a3_wkv"]),
                                  (bkv[:, :], io["a3_bkv"]), (wv[:, :], io["a3_wv"]), (trig[:, :, :], io["trig"])])
                sp.wait_ge(loaded, 96)

            @block.tensor
            def _(pe):
                pe.wait_ge(loaded, 96)
                with pe.Fori(0, B) as b:
                    for j in range(4):
                        pe.wait_ge(rot_ready, 4 * b)
                        if j == 0:
                            pe.wait_ge(ckv_ready, b)
                        if j == 1:
                            pe.wait_ge(v_ready, b)
                        for c in range(2):
                            mm = pe.matmul(pw[:, j, c * CH:(c + 1) * CH], w[:, j, :], at(xn, b * L + c * CH, CH),
                                           start=True, stop=True)
                        mm.then_inc(w_mm, 1)
                    wait_apart(pe, rot_ready, 4 * b + 1)
                    for c in range(2):
                        mm = pe.matmul(pw[0:DC, 0, c * CH:(c + 1) * CH], wkv[:, :], at(xn, b * L + c * CH, CH),
                                       start=True, stop=True)
                    mm.then_inc(c_mm, 1)
                    pe.wait_ge(ckv_ready, b + 1)
                    pe.wait_ge(rot_ready, 4 * b + 2)
                    pe.wait_ge(one_set, 1)
                    for t in range(KT):
                        mm = pe.matmul(pw[:, 1, t * P:(t + 1) * P], ckv[:, t * P:(t + 1) * P], wv[:, :],
                                       start=True, stop=True)
                    mm.then_inc(v_mm, 1)

            @block.scalar
            def _(act):
                act.wait_ge(loaded, 96)
                with act.Fori(0, B) as b:
                    act.wait_ge(c_mm, b + 1)
                    act.wait_ge(v_mm, b)
                    act.activation(ckv[0:DC, :], pw[0:DC, 0, :], ACT.Gelu, bias=bkv[:, 0:1]).then_inc(ckv_ready, 1)
                    for j in range(2):
                        act.wait_ge(pre_ready, 2 * b + j + 1)
                        act.activation(at(feat, (j * B + b) * L, L), pre[:, j, :], ACT.Gelu).then_inc(feat_ready, 1)

            @block.vector
            def _(dve):
                dve.memset(ckv[DC:DC + 1, :], 1.0).then_inc(one_set, 1)
                dve.wait_ge(loaded, 96)
                with dve.Fori(0, B) as b:
                    for j in range(4):
                        dve.wait_ge(w_mm, 4 * b + j + 1)
                        dve.wait_ge(pre_ready, 2 * b)
                        dve.scalar_tensor_tensor(out=rot[:, j, :], in0=pw[:, j, :], scalar=bias[:, j:j + 1],
                                                 in1=trig[:, j % 2, :], op0=ALU.add, op1=ALU.mult).then_inc(rot_ready, 1)
                    dve.wait_ge(v_mm, b + 1)
                    dve.tensor_copy(at(v, b * L, L), pw[:, 1, :]).then_inc(v_ready, 1)

            @block.gpsimd
            def _(pool):
                with pool.Fori(0, B) as b:
                    for j in range(2):
                        pool.wait_ge(rot_ready, 4 * b + 2 * j + 2)
                        pool.wait_ge(feat_ready, 2 * b)
                        pool.tensor_tensor(pre[:, j, :], rot[:, 2 * j, :], rot[:, 2 * j + 1, :],
                                           ALU.add).then_inc(pre_ready, 1)


def split_store(nc, tag, feat, items, scratch):
    with stage(nc, "s" + tag) as (sb, ps, sem):
        parts = sb("parts", [P, 2, NPART, L], BF16)
        rest = sb("rest", [P, 2, L])
        hi = [sem(f"hi{u}") for u in range(2)]
        rest_ready = [sem(f"rest_ready{u}") for u in range(2)]
        mid = [sem(f"mid{u}") for u in range(2)]
        lo = [sem(f"lo{u}") for u in range(2)]
        stored = [sem(f"stored{u}") for u in range(2)]
        n = items // 2
        with nc.Block() as block:
            @block.sync
            def _(sp):
                with sp.Fori(0, n) as i:
                    for u in range(2):
                        sp.wait_ge(lo[u], i + 1)
                        for a in range(NPART):
                            dst = bass.AP(scratch.tensor, ((i * 2 + u) * NH * NPART + a) * HD * L,
                                          [[NPART * HD * L, NH], [L, HD], [1, L]])
                            sp.dma_start(dst, parts[:, u, a, :]).then_inc(stored[u], 16)
                for u in range(2):
                    sp.wait_ge(stored[u], 16 * NPART * n)

            @block.scalar
            def _(act):
                with act.Fori(0, n) as i:
                    for u in range(2):
                        act.wait_ge(stored[u], 16 * NPART * i)
                        act.activation(parts[:, u, 0, :], at(feat, (i * 2 + u) * L, L), ACT.Copy).then_inc(hi[u], 1)
                    for u in range(2):
                        act.wait_ge(rest_ready[u], i + 1)
                        act.activation(parts[:, u, 1, :], rest[:, u, :], ACT.Copy).then_inc(mid[u], 1)

            @block.vector
            def _(dve):
                with dve.Fori(0, n) as i:
                    for u in range(2):
                        dve.wait_ge(hi[u], i + 1)
                        dve.wait_ge(lo[u], i)
                        dve.tensor_tensor(rest[:, u, :], at(feat, (i * 2 + u) * L, L), parts[:, u, 0, :],
                                          ALU.subtract).then_inc(rest_ready[u], 1)
                    for u in range(2):
                        dve.wait_ge(mid[u], i + 1)
                        dve.wait_ge(rest_ready[u], i + 1)
                        dve.tensor_tensor(parts[:, u, 2, :], rest[:, u, :], parts[:, u, 1, :],
                                          ALU.subtract).then_inc(lo[u], 1)


def attend_old(nc, io, tag, v, scratch, result, causal, terms, softmax, scale=1.0):
    MR = NPART if softmax else 0
    NG = NH // GH
    LOADS = (1 + NPART) * terms * GH * 16
    tiles = []
    if softmax:
        for qt in range(KT):
            for half in range(2):
                end = min((half + 1) * CH, (qt + 1) * P if causal else L)
                if end > half * CH:
                    tiles.append((qt, half, half * CH, end))
    uses = []
    for hh in range(GH if softmax else 0):
        uses += [("tile", hh, t) for t in tiles]
    order = []
    for n, use in enumerate(uses):
        order.append(use)
        hh = (n - 4) // len(tiles)
        if n >= len(tiles) and (n - 4) % len(tiles) == 0 and n - 4 > 0:
            order.append(("turn", hh - 1, None))
    if softmax:
        order.append(("turn", GH - 1, None))
    uses = order
    NU = len(uses)
    assert NU % 2 == 0
    last_tile = {hh: max(m for m, x in enumerate(uses) if x[0] == "tile" and x[1] == hh) for hh in range(GH)} if softmax else {}
    turn_at = {x[1]: m for m, x in enumerate(uses) if x[0] == "turn"}
    with stage(nc, "a" + tag) as (sb, ps, sem):
        kst = sb("kst", [ROWS + MR, 2, terms, GH, L], BF16)
        qst = sb("qst", [ROWS + MR, 2, terms, GH, L], BF16)
        if softmax:
            ksr = sb("ksr", [ROWS, GH, L], BF16)
            qsr = sb("qsr", [ROWS, GH, L], BF16)
            mx = sb("mx", [P, GH, KT, 2])
            mxf = sb("mxf", [P, GH, KT])
            neg = sb("neg", [P, GH, KT])
            nrest = sb("nrest", [P, GH, KT])
            mparts = sb("mparts", [P, GH, NPART, KT], BF16)
            mrow = sb("mrow", [NPART * KT, GH, P], BF16)
            search = ps("search", [P, 2, CH])
        vst = sb("vst", [P, KT, GH, 32])
        prob = sb("prob", [P, 2, GH, L])
        accs = sb("accs", [P, L])
        mask = sb("mask", [P, 2, P], BF16)
        keep = sb("keep", [P, P])
        score = ps("score", [P, 2, L])
        acc = ps("acc", [P, L])
        set_up, mx_set, loaded = sem("set_up"), sem("mx_set"), sem("loaded")
        stacks, ones_in = sem("stacks"), sem("ones_in")
        search_in = [sem(f"search_in{h}") for h in range(GH)]
        search_mm, search_used = sem("search_mm"), sem("search_used")
        max_ready, pool_steps, mparts_ready = sem("max_ready"), sem("pool_steps"), sem("mparts_ready")
        mrow_in = [sem(f"mrow_in{h}") for h in range(GH)]
        v_staged, score_mm, prob_ready, diag_ready = sem("v_staged"), sem("score_mm"), sem("prob_ready"), sem("diag_ready")
        av_mm, acc_read, acc_out = sem("av_mm"), sem("acc_read"), sem("acc_out")
        identb = io["sb_identb"]
        consts = []
        if causal:
            consts = [(mask[:, :, :], io["mask"]), (keep[:, :], io["keep"])]
        NCST = 16 * len(consts)

        NCOPY = KT * GH if softmax else (KT - 1) * GH

        def copied(it, n):
            return it * NCOPY + min(n, NCOPY)

        def stack(eng, q_dst, k_dst, it, hh, term, signal):
            head = it * GH + hh
            q_at = term * B * NH * NPART * HD * L + head * (NPART * HD * L)
            k_at = (terms + term) * B * NH * NPART * HD * L + head * (NPART * HD * L)
            eng.dma_start(q_dst(0, ROWS), bass.AP(scratch.tensor, q_at, [[0, NPART], [L, NPART * HD], [1, L]])
                          ).then_inc(signal, 16)
            for t in range(NPART):
                eng.dma_start(k_dst(t * NPART * HD, (t + 1) * NPART * HD),
                              bass.AP(scratch.tensor, k_at + t * HD * L, [[0, NPART], [L, HD], [1, L]])
                              ).then_inc(signal, 16)

        with nc.Block() as block:
            @block.sync
            def _(sp):
                load(sp, loaded, consts)

                def load_stacks(it, par):
                    for hh in range(GH):
                        for term in range(terms):
                            def into(t):
                                return lambda r0, r1: t[r0:r1, bass.ds(par, 1), term, hh, :].rearrange("r o t -> r (o t)")

                            stack(sp, into(qst), into(kst), it, hh, term, stacks)

                def load_search(it, hh):
                    stack(sp, lambda r0, r1: qsr[r0:r1, hh, :], lambda r0, r1: ksr[r0:r1, hh, :], it, hh, 0,
                          search_in[hh])

                def store(it):
                    sp.wait_ge(acc_read, it + 1)
                    for hh in range(GH):
                        for nd in range(2 if softmax else 1):
                            dst = bass.AP(result.tensor, ((nd * P + ((it % NG) * GH + hh) * HD) * B + it // NG) * L,
                                          [[B * L, HD], [1, L]])
                            sp.dma_start(dst, accs[32 * hh + HD * nd:32 * hh + HD * nd + HD, :]).then_inc(acc_out, 16)

                if softmax:
                    for hh in range(GH):
                        load_search(0, hh)
                    for par in range(2):
                        sp.dma_start(kst[ROWS:ROWS + MR, par, 0, :, :], io["ones_rows"]).then_inc(ones_in, 16)
                load_stacks(0, 0)
                with sp.Fori(0, B * NG - 1) as it:
                    for hh in range(GH if softmax else 0):
                        sp.wait_ge(search_mm, it * NU + last_tile[hh] + 1)
                        load_search(it + 1, hh)
                    wait_apart(sp, score_mm, it * KT * GH)
                    sp.wait_ge(stacks, LOADS * (it + 1))
                    load_stacks(it + 1, (it + 1) % 2)
                    store(it)
                store(B * NG - 1)
                sp.wait_ge(acc_out, B * NG * GH * (2 if softmax else 1) * 16)
                if NCST:
                    sp.wait_ge(loaded, NCST)

            @block.gpsimd
            def _(pool):
                pool.memset(vst[:, :, :, HD:32], 0.0).then_inc(set_up, 1)
                pool.wait_ge(set_up, 1)
                pool.memset(vst[:, :, :, HD:2 * HD], 1.0).then_inc(set_up, 1)
                pool.wait_ge(set_up, 2)

                def stage_values(it):
                    pool.wait_ge(av_mm, it * KT)
                    src = v[:, bass.ds((it // NG) * L, L)].rearrange("p (k f) -> p k f", f=P)
                    src = src[:, :, bass.ds((it % NG) * GH * HD, GH * HD)].rearrange("p k (h e) -> p k h e", e=HD)
                    pool.tensor_copy(vst[:, :, :, 0:HD], src).then_inc(v_staged, 1)

                def maxima(grp, heads):
                    for hh in heads:
                        step = Steps(pool, pool_steps, (grp * GH + hh) * 4)
                        wait_apart(pool, max_ready, grp * GH + hh + 1)
                        step(pool.tensor_scalar(neg[:, hh, :], mxf[:, hh, :], -1.0, None, ALU.mult), apart=True)
                        step(pool.tensor_copy(mparts[:, hh, 0, :], neg[:, hh, :]))
                        step(pool.tensor_tensor(nrest[:, hh, :], neg[:, hh, :], mparts[:, hh, 0, :], ALU.subtract), apart=True)
                        step(pool.tensor_copy(mparts[:, hh, 1, :], nrest[:, hh, :]))
                        pool.tensor_tensor(mparts[:, hh, 2, :], nrest[:, hh, :], mparts[:, hh, 1, :],
                                           ALU.subtract).then_inc(mparts_ready, 1)
                        pool.wait_ge(search_used, grp * NU + turn_at[hh] + 1)
                        if hh == 0 and not isinstance(grp, int):
                            pool.wait_ge(score_mm, (grp - 1) * KT * GH)
                        dst = qst[ROWS:ROWS + MR, bass.ds(grp % 2, 1), 0, hh, :]
                        for a in range(NPART):
                            d = qst[ROWS + a:ROWS + a + 1, bass.ds(grp % 2, 1), 0, hh, :].rearrange(
                                "r o (k q) -> r (o k) q", q=P)
                            pool.dma_start(d, mrow[a * KT:(a + 1) * KT, hh, :]).then_inc(mrow_in[hh], 16)

                if softmax:
                    maxima(0)
                with pool.Fori(0, B * NG - 1) as it:
                    stage_values(it)
                    if softmax:
                        maxima(it + 1)
                stage_values(B * NG - 1)

            @block.tensor
            def _(pe):
                if NCST:
                    pe.wait_ge(loaded, NCST)

                def use(grp, m):
                    what, hh, tile = uses[m]
                    if m >= 2:
                        pe.wait_ge(search_used, grp * NU + m - 1)
                    else:
                        pe.wait_ge(search_used, grp * NU)
                    slot = search[:, m % 2, :]
                    if what == "turn":
                        pe.wait_ge(mparts_ready, grp * GH + hh + 1)
                        out = slot.bitcast(BF16)[0:NPART * KT, 0:P]
                        pe.transpose(out, mparts[:, hh, :, :].rearrange("p a k -> p (a k)"), identb[:, :]
                                     ).then_inc(search_mm, 1)
                        return
                    qt, half, k0, k1 = tile
                    pe.wait_ge(search_in[hh], (1 + NPART) * 16 * (grp + 1))
                    diag = causal and k0 <= qt * P < k1
                    mm = pe.matmul(slot[:, 0:k1 - k0], qsr[:, hh, qt * P:(qt + 1) * P], ksr[:, hh, k0:k1],
                                   start=True, stop=True)
                    if diag:
                        mm = pe.matmul(slot[:, qt * P - k0:qt * P - k0 + P], identb[:, :], mask[:, 0, :],
                                       start=False, stop=True, skip_group_check=True)
                    mm.then_inc(search_mm, 1)

                def weigh(it, kt):
                    pe.wait_ge(prob_ready, copied(it, (kt + 1) * GH))
                    if not softmax:
                        pe.wait_ge(diag_ready, (it * KT + kt + 1) * GH)
                    if kt == 0:
                        pe.wait_ge(v_staged, it + 1)
                        pe.wait_ge(acc_read, it)
                    q0 = kt * P if causal else 0
                    for c in range(2):
                        lo, hi = max(q0, c * CH), (c + 1) * CH
                        if lo >= hi:
                            continue
                        last = kt == (KT - 1 if (c or not causal) else KT // 2 - 1)
                        for hh in range(GH):
                            mm = pe.matmul(acc[32 * hh:32 * hh + 32, lo:hi], vst[:, kt, hh, :], prob[:, kt % 2, hh, lo:hi],
                                           start=(kt == 0), stop=last, skip_group_check=True)
                    mm.then_inc(av_mm, 1)

                def main(it, par, grp):
                    pe.wait_ge(stacks, LOADS * (it + 1))
                    todo = list(range(NU if grp is not None else 0))
                    for kt in range(KT):
                        for hh in range(GH):
                            n = kt * GH + hh
                            if softmax and kt == 0:
                                pe.wait_ge(mrow_in[hh], 16 * NPART * (it + 1))
                            if n >= 2:
                                pe.wait_ge(prob_ready, copied(it, n - 1))
                                if not softmax:
                                    pe.wait_ge(diag_ready, it * KT * GH + n - 1)
                            else:
                                pe.wait_ge(prob_ready, copied(it, 0))
                                if not softmax:
                                    pe.wait_ge(diag_ready, it * KT * GH)
                            q0 = kt * P if causal else 0
                            for c in range(2):
                                lo, hi = max(q0, c * CH), (c + 1) * CH
                                if lo >= hi:
                                    continue
                                diag = causal and softmax and lo == q0
                                for term in range(terms):
                                    mm = pe.matmul(
                                        score[:, n % 2, lo:hi],
                                        kst[:, bass.ds(par, 1), term, hh, kt * P:(kt + 1) * P].rearrange("r o t -> r (o t)"),
                                        qst[:, bass.ds(par, 1), term, hh, lo:hi].rearrange("r o t -> r (o t)"),
                                        start=(term == 0), stop=(term == terms - 1))
                                if diag:
                                    mm = pe.matmul(score[:, n % 2, lo:lo + P], identb[:, :], mask[:, 1, :],
                                                   start=False, stop=True, skip_group_check=True)
                            mm.then_inc(score_mm, 1)
                            share = len(todo) * 1 // (KT * GH - n) if todo else 0
                            for _ in range(share):
                                use(grp, todo.pop(0))
                        if kt >= 1:
                            weigh(it, kt - 1)
                    weigh(it, KT - 1)
                    for m in todo:
                        use(grp, m)

                if softmax:
                    pe.wait_ge(ones_in, 32)
                    for m in range(NU):
                        use(0, m)
                with pe.Fori(0, B * NG - 1) as it:
                    main(it, it % 2, it + 1 if softmax else None)
                main(B * NG - 1, (B * NG - 1) % 2, None)

            @block.scalar
            def _(act):
                with act.Fori(0, B * NG) as it:
                    for kt in range(KT):
                        q0 = kt * P if causal else 0
                        if kt >= 2:
                            act.wait_ge(av_mm, it * KT + kt - 1)
                        else:
                            act.wait_ge(av_mm, it * KT)
                        for hh in range(GH):
                            n = kt * GH + hh
                            act.wait_ge(score_mm, it * KT * GH + n + 1)
                            if softmax:
                                act.activation(prob[:, kt % 2, hh, q0:L], score[:, n % 2, q0:L], ACT.Exp,
                                               scale=scale).then_inc(prob_ready, 1)
                            elif kt < KT // 2:
                                act.activation(prob[:, kt % 2, hh, CH:L], score[:, n % 2, CH:L],
                                               ACT.Copy).then_inc(prob_ready, 1)
                            else:
                                act.wait_ge(diag_ready, it * KT * GH + n + 1)
                                if q0 + P < L:
                                    act.activation(prob[:, kt % 2, hh, q0 + P:L], score[:, n % 2, q0 + P:L],
                                                   ACT.Copy).then_inc(prob_ready, 1)
                    act.wait_ge(av_mm, (it + 1) * KT)
                    act.wait_ge(acc_out, it * GH * (2 if softmax else 1) * 16)
                    act.activation(accs[:, :], acc[:, :], ACT.Copy).then_inc(acc_read, 1)

            @block.vector
            def _(dve):
                if softmax:
                    dve.memset(mx[:, :, :, :], -3e38).then_inc(mx_set, 1)
                    dve.wait_ge(mx_set, 1)

                    def consume(grp):
                        for m, (what, hh, tile) in enumerate(uses):
                            dve.wait_ge(search_mm, grp * NU + m + 1)
                            slot = search[:, m % 2, :]
                            if what == "turn":
                                dve.tensor_copy(mrow[:, hh, :], slot.bitcast(BF16)[0:NPART * KT, 0:P]
                                                ).then_inc(search_used, 1)
                                continue
                            qt, half, k0, k1 = tile
                            dve.tensor_reduce(mx[:, hh, qt, half:half + 1], slot[:, 0:k1 - k0], AX.X,
                                              ALU.max).then_inc(search_used, 1)
                            if m == last_tile[hh]:
                                dve.wait_ge(search_used, grp * NU + m + 1)
                                dve.wait_ge(mparts_ready, grp * GH)
                                dve.tensor_reduce(mxf[:, hh, :], mx[:, hh, :, :], AX.X, ALU.max).then_inc(max_ready, 1)

                    with dve.Fori(0, B * NG) as grp:
                        dve.wait_ge(max_ready, grp * GH)
                        for hh in range(GH):
                            dve.wait_ge(mrow_in[hh], 16 * NPART * grp)
                        consume(grp)
                else:
                    dve.wait_ge(loaded, NCST)
                    with dve.Fori(0, B * NG) as it:
                        for kt in range(KT):
                            if kt >= 2:
                                dve.wait_ge(av_mm, it * KT + kt - 1)
                            else:
                                dve.wait_ge(av_mm, it * KT)
                            for hh in range(GH):
                                n = kt * GH + hh
                                q0 = kt * P
                                dve.wait_ge(score_mm, it * KT * GH + n + 1)
                                done = dve.tensor_tensor(prob[:, kt % 2, hh, q0:q0 + P], score[:, n % 2, q0:q0 + P],
                                                         keep[:, :], ALU.mult)
                                if kt < KT // 2 and q0 + P < CH:
                                    done = dve.tensor_copy(prob[:, kt % 2, hh, q0 + P:CH], score[:, n % 2, q0 + P:CH])
                                done.then_inc(diag_ready, 1)


def pass_plan(groups, width, uses, use_cost):
    NU = len(uses)
    total_use, total = sum(use_cost), sum(width) * GH
    plan, done, m, cost = [], 0, 0, 0
    for g in range(len(groups)):
        for hh in range(GH):
            plan.append(("score", g, hh))
            done += width[g]
            if hh == 1:
                plan.append(("sum", g - 1, 0))
            while m < NU and (cost + use_cost[m] / 2) * total <= done * total_use:
                plan.append(("use", m, 0))
                cost += use_cost[m]
                m += 1
    return plan + [("use", k, 0) for k in range(m, NU)]


def attend(nc, io, tag, v, scratch, result, causal, scale=1.0):
    MR = NPART
    NG = NH // GH
    NPASS = B * NG
    LOADS = (1 + NPART) * GH * 16
    tiles = []
    for qt in range(KT):
        for half in range(2):
            end = min((half + 1) * CH, (qt + 1) * P if causal else L)
            if end > half * CH:
                tiles.append((qt, half, half * CH, end))
    LEAD = len(tiles)
    uses = []
    for hh in (1, 2, 3, 0):
        for n, tile in enumerate(tiles):
            if n == 4:
                uses.append(("turn", (hh - 1) % GH, None))
            uses.append(("tile", hh, tile))
    NU = len(uses)
    NSE, NSC = 4, 2
    assert NU % NSE == 0 and LEAD % NSE == 0
    use_cost = [60 + (t[3] - t[2] if what == "tile" else P) for what, _, t in uses]
    last_tile = {hh: max(m for m, x in enumerate(uses) if x[0] == "tile" and x[1] == hh) for hh in range(GH)}
    turn_at = {x[1]: m for m, x in enumerate(uses) if x[0] == "turn"}
    groups = []
    for kt in range(KT):
        for c in range(2):
            lo = max(kt * P if causal else 0, c * CH)
            if lo < (c + 1) * CH:
                groups.append((kt, c, lo, (c + 1) * CH))
    NGR = len(groups)
    NS1 = NGR * GH
    assert NS1 % NSC == 0
    before = [max(n for n in range(g + NGR) if groups[n % NGR][0] % 2 == kt % 2 and groups[n % NGR][1] == c)
              for g, (kt, c, _, _) in enumerate(groups)]
    final = {c: max(g for g in range(NGR) if groups[g][1] == c) for c in range(2)}
    plan = pass_plan(groups, [hi - lo + 100 for _, _, lo, hi in groups], uses, use_cost)

    def searched(grp, m):
        return LEAD + grp * NU + m

    with stage(nc, "a" + tag) as (sb, ps, sem):
        kst = sb("kst", [ROWS + MR, 2, GH, L], BF16)
        qst = sb("qst", [ROWS + MR, 2, GH, L], BF16)
        ksr = sb("ksr", [ROWS, GH, L], BF16)
        qsr = sb("qsr", [ROWS, GH, L], BF16)
        mx = sb("mx", [P, GH, KT, 2])
        mxf = sb("mxf", [P, GH, KT])
        neg = sb("neg", [P, GH, KT])
        nrest = sb("nrest", [P, GH, KT])
        mparts = sb("mparts", [P, GH, NPART, KT], BF16)
        mrow = sb("mrow", [NPART * KT, GH, P], BF16)
        vst = sb("vst", [P, KT, GH, 32])
        prob = sb("prob", [P, 2, GH, L])
        accs = sb("accs", [P, L])
        search = ps("search", [P, NSE, CH])
        score = ps("score", [P, NSC, CH])
        acc = ps("acc", [P, L])
        set_up, mx_set, loaded = sem("set_up"), sem("mx_set"), sem("loaded")
        stacks, ones_in = sem("stacks"), sem("ones_in")
        search_in = [sem(f"search_in{h}") for h in range(GH)]
        search_mm, search_used = sem("search_mm"), sem("search_used")
        max_ready, pool_steps, mparts_ready = sem("max_ready"), sem("pool_steps"), sem("mparts_ready")
        mrow_in = [sem(f"mrow_in{h}") for h in range(GH)]
        v_staged, score_mm, prob_ready = sem("v_staged"), sem("score_mm"), sem("prob_ready")
        av_mm, acc_read, acc_out = sem("av_mm"), sem("acc_read"), sem("acc_out")
        identb = io["sb_identb"]
        consts = []
        if causal:
            mask = sb("mask", [P, 2, P], BF16)
            consts = [(mask[:, :, :], io["mask"])]
        NCST = 16 * len(consts)

        def stack(eng, q_dst, k_dst, it, hh, signal):
            q_at = (it * GH + hh) * (NPART * HD * L)
            k_at = B * NH * NPART * HD * L + q_at
            eng.dma_start(q_dst(0, ROWS), bass.AP(scratch.tensor, q_at, [[0, NPART], [L, NPART * HD], [1, L]])
                          ).then_inc(signal, 16)
            for t in range(NPART):
                eng.dma_start(k_dst(t * NPART * HD, (t + 1) * NPART * HD),
                              bass.AP(scratch.tensor, k_at + t * HD * L, [[0, NPART], [L, HD], [1, L]])
                              ).then_inc(signal, 16)

        with nc.Block() as block:
            @block.sync
            def _(sp):
                def load_stacks(it, par):
                    for hh in range(GH):
                        def into(t):
                            return lambda r0, r1: t[r0:r1, bass.ds(par, 1), hh, :].rearrange("r o t -> r (o t)")

                        stack(sp, into(qst), into(kst), it, hh, stacks)

                def load_search(grp, hh):
                    stack(sp, lambda r0, r1: qsr[r0:r1, hh, :], lambda r0, r1: ksr[r0:r1, hh, :], grp, hh,
                          search_in[hh])

                def store(it):
                    sp.wait_ge(acc_read, it + 1)
                    for hh in range(GH):
                        for nd in range(2):
                            dst = bass.AP(result.tensor, ((nd * P + ((it % NG) * GH + hh) * HD) * B + it // NG) * L,
                                          [[B * L, HD], [1, L]])
                            sp.dma_start(dst, accs[32 * hh + HD * nd:32 * hh + HD * nd + HD, :]).then_inc(acc_out, 16)

                for hh in range(GH):
                    load_search(0, hh)
                load(sp, loaded, consts)
                for par in range(2):
                    sp.dma_start(kst[ROWS:ROWS + MR, par, :, :], io["ones_rows"]).then_inc(ones_in, 16)
                load_stacks(0, 0)
                sp.wait_ge(search_mm, LEAD)
                load_search(1, 0)

                def next_search(it, hh):
                    sp.wait_ge(search_mm, searched(it, last_tile[hh] + 1))
                    load_search(it + (2 if hh == 0 else 1), hh)

                for hh in range(1, GH):
                    next_search(0, hh)

                def body(it, search=True):
                    if search:
                        next_search(it, 0)
                    if not isinstance(it, int) or it > 0:
                        wait_apart(sp, score_mm, it * NS1)
                    sp.wait_ge(stacks, LOADS * (it + 1))
                    load_stacks(it + 1, (it + 1) % 2)
                    if not isinstance(it, int) or it > 0:
                        store(it - 1)
                    for hh in range(1, GH if search else 1):
                        next_search(it + 1, hh)

                body(0)
                with sp.Fori(1, NPASS - 2) as it:
                    body(it)
                body(NPASS - 2, search=False)
                store(NPASS - 2)
                store(NPASS - 1)
                sp.wait_ge(acc_out, NPASS * GH * 2 * 16)
                if NCST:
                    sp.wait_ge(loaded, NCST)

            @block.gpsimd
            def _(pool):
                pool.memset(vst[:, :, :, HD:32], 0.0).then_inc(set_up, 1)
                pool.wait_ge(set_up, 1)
                pool.memset(vst[:, :, :, HD:2 * HD], 1.0).then_inc(set_up, 1)
                pool.wait_ge(set_up, 2)

                def stage_values(it):
                    if not isinstance(it, int) or it > 0:
                        pool.wait_ge(av_mm, it * NGR)
                    src = v[:, bass.ds((it // NG) * L, L)].rearrange("p (k f) -> p k f", f=P)
                    src = src[:, :, bass.ds((it % NG) * GH * HD, GH * HD)].rearrange("p k (h e) -> p k h e", e=HD)
                    pool.tensor_copy(vst[:, :, :, 0:HD], src).then_inc(v_staged, 1)

                def split_maxima(grp, hh):
                    step = Steps(pool, pool_steps, (grp * GH + hh) * 4)
                    wait_apart(pool, max_ready, grp * GH + hh + 1)
                    step(pool.tensor_scalar(neg[:, hh, :], mxf[:, hh, :], -1.0, None, ALU.mult), apart=True)
                    step(pool.tensor_copy(mparts[:, hh, 0, :], neg[:, hh, :]))
                    step(pool.tensor_tensor(nrest[:, hh, :], neg[:, hh, :], mparts[:, hh, 0, :], ALU.subtract),
                         apart=True)
                    step(pool.tensor_copy(mparts[:, hh, 1, :], nrest[:, hh, :]))
                    pool.tensor_tensor(mparts[:, hh, 2, :], nrest[:, hh, :], mparts[:, hh, 1, :],
                                       ALU.subtract).then_inc(mparts_ready, 1)

                def move_maxima(grp, hh):
                    pool.wait_ge(search_used, searched(grp, turn_at[hh] + 1))
                    if hh == 0 and (not isinstance(grp, int) or grp > 1):
                        pool.wait_ge(score_mm, (grp - 1) * NS1)
                    rows = qst[ROWS:ROWS + MR, bass.ds(grp % 2, 1), hh, :].rearrange("r o (k q) -> r (o k) q", q=P)
                    pool.dma_start(rows, mrow[:, hh, :]).then_inc(mrow_in[hh], 16)

                def maxima(grp, heads):
                    for hh in heads:
                        split_maxima(grp, hh)
                        move_maxima(grp, hh)

                maxima(0, range(GH))
                stage_values(0)
                maxima(1, range(GH))
                with pool.Fori(1, NPASS - 1) as it:
                    split_maxima(it + 1, 0)
                    stage_values(it)
                    move_maxima(it + 1, 0)
                    maxima(it + 1, range(1, GH))
                stage_values(NPASS - 1)

            @block.tensor
            def _(pe):
                def use(grp, m):
                    first_head = isinstance(grp, int) and grp < 0
                    what, hh, tile = ("tile", 0, tiles[m]) if first_head else uses[m]
                    n = m if first_head else searched(grp, m)
                    if not isinstance(n, int) or n >= NSE:
                        pe.wait_ge(search_used, n - NSE + 1)
                    slot = search[:, m % NSE, :]
                    if what == "turn":
                        pe.wait_ge(mparts_ready, grp * GH + hh + 1)
                        out = slot.bitcast(BF16)[0:NPART * KT, 0:P]
                        pe.transpose(out, mparts[:, hh, :, :].rearrange("p a k -> p (a k)"), identb[:, :]
                                     ).then_inc(search_mm, 1)
                        return
                    qt, half, k0, k1 = tile
                    loads = grp + (2 if hh == 0 else 1)
                    pe.wait_ge(search_in[hh], (1 + NPART) * 16 * (min(loads, NPASS) if isinstance(loads, int) else loads))
                    diag = causal and k0 <= qt * P < k1
                    mm = pe.matmul(slot[:, 0:k1 - k0], qsr[:, hh, qt * P:(qt + 1) * P], ksr[:, hh, k0:k1],
                                   start=True, stop=True)
                    if diag:
                        mm = pe.matmul(slot[:, qt * P - k0:qt * P - k0 + P], identb[:, :], mask[:, 0, :],
                                       start=False, stop=True, skip_group_check=True)
                    mm.then_inc(search_mm, 1)

                def add_up(it, g):
                    kt, c, lo, hi = groups[g]
                    pe.wait_ge(prob_ready, it * NS1 + (g + 1) * GH)
                    if g == 0:
                        pe.wait_ge(v_staged, it + 1)
                        if not isinstance(it, int) or it > 0:
                            pe.wait_ge(acc_read, it)
                    for hh in range(GH):
                        mm = pe.matmul(acc[32 * hh:32 * hh + 32, lo:hi], vst[:, kt, hh, :], prob[:, kt % 2, hh, lo:hi],
                                       start=(kt == 0), stop=(g == final[c]), skip_group_check=True)
                    mm.then_inc(av_mm, 1)

                def scores(it, par, g, hh):
                    kt, c, lo, hi = groups[g]
                    n = g * GH + hh
                    if n == 0:
                        pe.wait_ge(stacks, LOADS * (it + 1))
                    if g == 0:
                        pe.wait_ge(mrow_in[hh], 16 * (it + 1))
                    if not isinstance(it, int) or it * NS1 + n >= NSC:
                        pe.wait_ge(prob_ready, it * NS1 + n - NSC + 1)
                    slot = score[:, n % NSC, :]
                    mm = pe.matmul(slot[:, 0:hi - lo],
                                   kst[:, bass.ds(par, 1), hh, kt * P:(kt + 1) * P].rearrange("r o t -> r (o t)"),
                                   qst[:, bass.ds(par, 1), hh, lo:hi].rearrange("r o t -> r (o t)"),
                                   start=True, stop=True)
                    if causal and lo == kt * P:
                        mm = pe.matmul(slot[:, 0:P], identb[:, :], mask[:, 1, :],
                                       start=False, stop=True, skip_group_check=True)
                    mm.then_inc(score_mm, 1)

                def one_pass(it, par, carry=True, searches=NU):
                    for what, a, hh in plan:
                        if what == "score":
                            scores(it, par, a, hh)
                        elif what == "use":
                            if a < searches:
                                use(it + 1, a)
                        elif a >= 0:
                            add_up(it, a)
                        elif carry:
                            add_up(it - 1, NGR - 1)

                if NCST:
                    pe.wait_ge(loaded, NCST)
                for m in range(LEAD):
                    use(-1, m)
                for m in range(NU):
                    use(0, m)
                pe.wait_ge(ones_in, 32)
                one_pass(0, 0, carry=False)
                with pe.Fori(1, NPASS - 2) as it:
                    one_pass(it, it % 2)
                one_pass(NPASS - 2, 0, searches=turn_at[3] + 1)
                one_pass(NPASS - 1, 1, searches=0)
                add_up(NPASS - 1, NGR - 1)

            @block.scalar
            def _(act):
                def read_sums(it):
                    act.wait_ge(av_mm, (it + 1) * NGR)
                    if not isinstance(it, int) or it > 0:
                        act.wait_ge(acc_out, it * GH * 2 * 16)
                    act.activation(accs[:, :], acc[:, :], ACT.Copy).then_inc(acc_read, 1)

                def exponentials(it, g):
                    kt, c, lo, hi = groups[g]
                    if not isinstance(it, int) or (it - 1) * NGR + before[g] >= 0:
                        act.wait_ge(av_mm, (it - 1) * NGR + before[g] + 1)
                    for hh in range(GH):
                        n = g * GH + hh
                        act.wait_ge(score_mm, it * NS1 + n + 1)
                        act.activation(prob[:, kt % 2, hh, lo:hi], score[:, n % NSC, 0:hi - lo], ACT.Exp,
                                       scale=scale).then_inc(prob_ready, 1)

                for g in range(NGR):
                    exponentials(0, g)
                with act.Fori(1, NPASS) as it:
                    exponentials(it, 0)
                    read_sums(it - 1)
                    for g in range(1, NGR):
                        exponentials(it, g)
                read_sums(NPASS - 1)

            @block.vector
            def _(dve):
                dve.memset(mx[:, :, :, :], -3e38).then_inc(mx_set, 1)
                dve.wait_ge(mx_set, 1)

                def consume(grp, m):
                    first_head = isinstance(grp, int) and grp < 0
                    what, hh, tile = ("tile", 0, tiles[m]) if first_head else uses[m]
                    group = grp + 1 if hh == 0 and what == "tile" else grp
                    done = m + 1 if first_head else searched(grp, m + 1)
                    dve.wait_ge(search_mm, done)
                    slot = search[:, m % NSE, :]
                    if what == "turn":
                        if not isinstance(grp, int) or grp > 0:
                            dve.wait_ge(mrow_in[hh], 16 * grp)
                        dve.tensor_copy(mrow[:, hh, :], slot.bitcast(BF16)[0:NPART * KT, 0:P]
                                        ).then_inc(search_used, 1)
                        return
                    qt, half, k0, k1 = tile
                    if (qt, half) == (0, 0) and (not isinstance(group, int) or group > 0):
                        dve.wait_ge(max_ready, (group - 1) * GH + hh + 1)
                    dve.tensor_reduce(mx[:, hh, qt, half:half + 1], slot[:, 0:k1 - k0], AX.X,
                                      ALU.max).then_inc(search_used, 1)
                    if tile == tiles[-1]:
                        dve.wait_ge(search_used, done)
                        if not isinstance(group, int) or group > 0:
                            dve.wait_ge(mparts_ready, (group - 1) * GH + hh + 1)
                        dve.tensor_reduce(mxf[:, hh, :], mx[:, hh, :, :], AX.X, ALU.max).then_inc(max_ready, 1)

                for m in range(LEAD):
                    consume(-1, m)
                for m in range(NU):
                    consume(0, m)
                with dve.Fori(1, NPASS - 1) as grp:
                    for m in range(NU):
                        consume(grp, m)
                for m in range(turn_at[3] + 1):
                    consume(NPASS - 1, m)


def attention_out(nc, io, tag, result, s, softmax, xn=None):
    with stage(nc, "o" + tag) as (sb, ps, sem):
        w = sb("w", [P, P])
        bias = sb("bias", [P, 1])
        g1 = sb("g1", [P, HD])
        g2 = sb("g2", [HD, P])
        num = sb("num", [P, 2, L])
        den = sb("den", [P, 2, L])
        rec = sb("rec", [P, 2, L])
        ratio = sb("ratio", [P, 2, L])
        lowr = sb("lowr", [HD, L])
        gate = sb("gate", [P, L])
        po = ps("po", [P, 2, L])
        pl = ps("pl", [P, L])
        pgt = ps("pgt", [P, L])
        loaded = sem("loaded")
        fetched = [sem(f"fetched{u}") for u in range(2)]
        rec_ready = [sem(f"rec_ready{u}") for u in range(2)]
        ratio_ready = [sem(f"ratio_ready{u}") for u in range(2)]
        out_mm = [sem(f"out_mm{u}") for u in range(2)]
        s_ready = [sem(f"s_ready{u}") for u in range(2)]
        low_mm, low_ready, gate_mm, gate_ready = sem("low_mm"), sem("low_ready"), sem("gate_mm"), sem("gate_ready")
        loads = [(w[:, :], io[f"o{tag}_w"])]
        loads += [(bias[:, :], io[f"o{tag}_b"])] if softmax else [(g1[:, :], io["a1_g1"]), (g2[:, :], io["a1_g2"])]
        NL = 16 * len(loads)
        with nc.Block() as block:
            @block.sync
            def _(sp):
                load(sp, loaded, loads)
                with sp.Fori(0, B // 2) as i:
                    for u in range(2):
                        sp.wait_ge(out_mm[u], i)
                        for nd, t in ((0, num), (1, den))[:2 if softmax else 1]:
                            sp.dma_start(t[:, u, :], result[nd, :, bass.ds(i * 2 + u, 1), :].rearrange("f o t -> f (o t)")
                                         ).then_inc(fetched[u], 16)
                sp.wait_ge(loaded, NL)

            @block.tensor
            def _(pe):
                pe.wait_ge(loaded, NL)
                with pe.Fori(0, B // 2) as i:
                    for u in range(2):
                        b = i * 2 + u
                        if softmax:
                            pe.wait_ge(ratio_ready[u], i + 1)
                        else:
                            pe.wait_ge(fetched[u], 16 * (i + 1))
                        pe.wait_ge(s_ready[u], i)
                        for c in range(2):
                            mm = pe.matmul(po[:, u, c * CH:(c + 1) * CH], w[:, :],
                                           (ratio if softmax else num)[:, u, c * CH:(c + 1) * CH], start=True, stop=True)
                        mm.then_inc(out_mm[u], 1)
                        if not softmax:
                            pe.wait_ge(low_ready, b)
                            for c in range(2):
                                mm = pe.matmul(pl[0:HD, c * CH:(c + 1) * CH], g1[:, :], at(xn, b * L + c * CH, CH),
                                               start=True, stop=True)
                            mm.then_inc(low_mm, 1)
                            pe.wait_ge(low_ready, b + 1)
                            pe.wait_ge(gate_ready, b)
                            for c in range(2):
                                mm = pe.matmul(pgt[:, c * CH:(c + 1) * CH], g2[:, :], lowr[:, c * CH:(c + 1) * CH],
                                               start=True, stop=True)
                            mm.then_inc(gate_mm, 1)

            @block.scalar
            def _(act):
                act.wait_ge(loaded, NL)
                with act.Fori(0, B // 2) as i:
                    for u in range(2):
                        b = i * 2 + u
                        if softmax:
                            act.wait_ge(out_mm[u], i + 1)
                            act.activation(at(s, b * L, L), po[:, u, :], ACT.Identity,
                                           bias=bias[:, 0:1]).then_inc(s_ready[u], 1)
                        else:
                            act.wait_ge(low_mm, b + 1)
                            act.wait_ge(gate_mm, b)
                            act.activation(lowr[:, :], pl[0:HD, :], ACT.Copy).then_inc(low_ready, 1)
                            act.wait_ge(gate_mm, b + 1)
                            act.wait_ge(s_ready[1 - u], i + u)
                            act.activation(gate[:, :], pgt[:, :], ACT.Sigmoid).then_inc(gate_ready, 1)

            @block.vector
            def _(dve):
                with dve.Fori(0, B // 2) as i:
                    for u in range(2):
                        b = i * 2 + u
                        if softmax:
                            dve.wait_ge(fetched[u], 32 * (i + 1))
                            dve.wait_ge(ratio_ready[u], i)
                            dve.reciprocal(rec[:, u, :], den[:, u, :]).then_inc(rec_ready[u], 1)
                            dve.wait_ge(rec_ready[u], i + 1)
                            dve.wait_ge(out_mm[u], i)
                            dve.tensor_tensor(ratio[:, u, :], num[:, u, :], rec[:, u, :], ALU.mult).then_inc(ratio_ready[u], 1)
                        else:
                            dve.wait_ge(out_mm[u], i + 1)
                            dve.wait_ge(gate_ready, b + 1)
                            dve.tensor_tensor(at(s, b * L, L), po[:, u, :], gate[:, :], ALU.mult).then_inc(s_ready[u], 1)


def program(nc, io):
    with ExitStack() as ctx:
        def sb(n, shape, dt=F32):
            return ctx.enter_context(nc.sbuf_tensor(n, shape, dt))

        xn = sb("xn", [P, T])
        s = sb("s", [P, T])
        average = sb("average", [P, P])
        ident = sb("ident", [P, P])
        identb = sb("identb", [P, P], BF16)
        consts = [(average[:, :], io["average"]), (ident[:, :], io["ident"]), (identb[:, :], io["identb"])]
        with ExitStack() as early:
            x0 = early.enter_context(nc.sbuf_tensor("x0", [P, T], F32))
            normalise(nc, "n0", x0, xn, average, True, first_load=consts + [
                (x0[:, b * L:(b + 1) * L], io["x"][:, b * L:(b + 1) * L]) for b in range(B)])
        with ExitStack() as mamba:
            def msb(n, shape, dt=F32):
                return mamba.enter_context(nc.sbuf_tensor(n, shape, dt))

            norm_w = msb("norm_w", [P, 1])
            gate = msb("gate", [P, 2 * T])
            xs = msb("xs", [P, 2 * T])
            normalise(nc, "n0r", xn, s, average, False, weight=norm_w, first_load=[(norm_w[:, :], io["m_nw"])])
            mamba_inputs(nc, io, s, gate, xs, None)
            delta = msb("delta", [P, 2 * T])
            parts_b = msb("parts_b", [NPART * SP, T], BF16)
            parts_c = msb("parts_c", [NPART * SP, T], BF16)
            mamba_steps(nc, io, xs, delta, parts_b, parts_c)
            mamba_scan(nc, io, xs, gate, delta, parts_b, parts_c, ident)
            mamba_out(nc, io, xs, xn, s)
        io["sb_identb"] = identb
        x = sb("x", [P, T])
        with ExitStack() as ffn:
            comb = ffn.enter_context(nc.sbuf_tensor("comb0", [49, 1, T], BF16))
            route(nc, io, "0", xn, comb, 16, 16, 4, "grouped_low")
            experts_sum(nc, io, "0", xn, s, x, comb, 49, 0, 0, 6, True, first_load=[(x[:, :], io["x"])])

        normalise(nc, "n1", x, xn, average, True)
        scratch1 = nc.dram_tensor("scratch1", [4 * B, NH, NPART, HD, L], BF16).ap()
        result1 = nc.dram_tensor("result1", [2, P, B, L], F32).ap()
        with ExitStack() as mix:
            v = mix.enter_context(nc.sbuf_tensor("v1", [P, T], F32))
            with ExitStack() as project:
                feat = project.enter_context(nc.sbuf_tensor("feat1", [P, 4 * T], F32))
                cos = project.enter_context(nc.sbuf_tensor("cos", [P, L], F32))
                sin = project.enter_context(nc.sbuf_tensor("sin", [P, L], F32))
                angles(nc, io, cos, sin)
                project_linear(nc, io, xn, feat, v, cos, sin)
                split_store(nc, "1", feat, 4 * B, scratch1)
            attend_old(nc, io, "1", v, scratch1, result1, True, 2, False)
            attention_out(nc, io, "1", result1, s, False, xn=xn)
            gamma = mix.enter_context(nc.sbuf_tensor("gamma", [P, 1], F32))
            beta = mix.enter_context(nc.sbuf_tensor("beta", [P, 1], F32))
            normalise(nc, "n1s", s, s, average, True, weight=gamma, shift=beta,
                      first_load=[(gamma[:, :], io["a1_gamma"]), (beta[:, :], io["a1_beta"])])
        with ExitStack() as ffn:
            comb = ffn.enter_context(nc.sbuf_tensor("comb1", [121, 4, T], BF16))
            route(nc, io, "1", xn, comb, 160, 40, 8, "sigmoid")
            experts_sum(nc, io, "1", xn, s, x, comb, 121, 4, 5, 1, False)

        normalise(nc, "n2", x, xn, average, True)
        scratch2 = nc.dram_tensor("scratch2", [2 * B, NH, NPART, HD, L], BF16).ap()
        result2 = nc.dram_tensor("result2", [2, P, B, L], F32).ap()
        with ExitStack() as mix:
            v = mix.enter_context(nc.sbuf_tensor("v2", [P, T], F32))
            with ExitStack() as project:
                feat = project.enter_context(nc.sbuf_tensor("feat2", [P, 2 * T], F32))
                project_plain(nc, io, xn, feat, v)
                split_store(nc, "2", feat, 2 * B, scratch2)
            attend(nc, io, "2", v, scratch2, result2, False)
        attention_out(nc, io, "2", result2, s, True)
        with ExitStack() as ffn:
            comb = ffn.enter_context(nc.sbuf_tensor("comb2", [49, 1, T], BF16))
            route(nc, io, "2", xn, comb, 16, 16, 4, "grouped")
            experts_sum(nc, io, "2", xn, s, x, comb, 49, 0, 0, 8, True)

        normalise(nc, "n3", x, xn, average, True)
        with ExitStack() as mix:
            v = mix.enter_context(nc.sbuf_tensor("v3", [P, T], F32))
            with ExitStack() as project:
                feat = project.enter_context(nc.sbuf_tensor("feat3", [P, 2 * T], F32))
                project_rotary(nc, io, xn, feat, v)
                split_store(nc, "3", feat, 2 * B, scratch2)
            attend(nc, io, "3", v, scratch2, result2, True, scale=float(HD) ** -0.5)
        attention_out(nc, io, "3", result2, s, True)
        with ExitStack() as ffn:
            comb = ffn.enter_context(nc.sbuf_tensor("comb3", [25, 1, T], BF16))
            route(nc, io, "3", xn, comb, 8, 8, 2, "softmax")
            experts_sum(nc, io, "3", xn, s, x, comb, 25, 1, 8, 2, True, out=io["out"])


def layouts(i):
    f = {k: np.asarray(v) for k, v in i.items()}
    bf = mybir.dt.np(BF16)
    o = {}
    c = np.ascontiguousarray
    o["x"] = c(f["L0_attn_resid"].transpose(2, 0, 1).reshape(P, T))
    o["average"] = np.full((P, P), 1.0 / P, np.float32)
    o["ident"] = np.eye(P, dtype=np.float32)
    o["identb"] = np.eye(P).astype(bf)

    def col(v):
        return c(v.reshape(-1, P).T)

    o["m_nw"] = col(f["L0_attn_norm_w"])
    o["m_w"] = c(np.stack([f["L0_attn_skip_w"].T.reshape(P, 2, P), f["L0_attn_in_w"].T.reshape(P, 2, P)], axis=1))
    o["m_cw"] = c(f["L0_attn_conv_w"].reshape(2, P, NT).transpose(1, 0, 2))
    o["m_cb"] = col(f["L0_attn_conv_b"])
    o["m_w1"] = c(f["L0_attn_Wd1"].T.reshape(2, P, DD).transpose(1, 0, 2))
    wbc = np.zeros((P, 2, 2, NPART, SP), np.float32)
    for j, n in enumerate(("WB", "WC")):
        wbc[:, :, j, :, :NS] = f["L0_attn_" + n].T.reshape(2, P, NS).transpose(1, 0, 2)[:, :, None, :]
    o["m_wbc"] = wbc.reshape(P, 2, 2, NPART * SP)
    o["m_w2"] = c(f["L0_attn_Wd2_w"].T.reshape(DD, 2, P))
    o["m_b2"] = col(f["L0_attn_Wd2_b"])
    o["m_alog"] = c(f["L0_attn_A_log"].reshape(2, P, NS).transpose(1, 0, 2))
    o["m_wd"] = col(f["L0_attn_W_D"])
    o["m_wo"] = c(f["L0_attn_out_w"].T.reshape(2, P, P).transpose(1, 0, 2))
    sel = np.zeros((NPART, SP, NS, P), np.float32)
    for n in range(NS):
        sel[:, n, n, :] = 1.0
    o["m_sel"] = sel.reshape(NPART * SP, NS, P).astype(bf)
    o["pos"] = np.broadcast_to(np.arange(L, dtype=np.float32), (P, L)).copy()
    o["a1_theta"] = f["L1_attn_theta"].reshape(P, 1)
    for n in ("q", "k", "v"):
        o["a1_w" + n] = f["L1_attn_W" + n]
    o["a1_g1"], o["a1_g2"] = f["L1_attn_G1"], f["L1_attn_G2"]
    o["a1_gamma"], o["a1_beta"] = col(f["L1_attn_gamma"]), col(f["L1_attn_beta"])
    o["o1_w"] = f["L1_attn_Wo"]
    below = np.triu(np.ones((P, P), np.float32))
    o["keep"] = below
    o["mask"] = np.stack([np.where(below.T > 0, 0, -BIG), np.where(below > 0, 0, -BIG)], axis=1).astype(bf)
    o["ones_rows"] = np.ones((NPART, GH, L), bf)

    def diagonal(w):
        out = np.zeros((NH, HD, NH, HD), np.float32)
        for h in range(NH):
            out[h, :, h, :] = w[h].T
        return out.reshape(P, P)

    o["a2_w"] = c(np.stack([f["L2_attn_W_down"], diagonal(f["L2_attn_toqueries"]), diagonal(f["L2_attn_tokeys"]),
                            diagonal(f["L2_attn_tovalues"])], axis=1))
    o["o2_w"], o["o2_b"] = f["L2_attn_W_unify"], col(f["L2_attn_b_unify"])

    def swapped(v):
        return np.concatenate([v[..., P // 2:], v[..., :P // 2]], axis=-1)

    wq, wk, bq, bk = (f["L3_attn_" + n] for n in ("wqr", "wkr", "bqr", "bkr"))
    o["a3_w"] = c(np.stack([wq, swapped(wq), wk, swapped(wk)], axis=1))
    o["a3_b"] = c(np.stack([bq, swapped(bq), bk, swapped(bk)], axis=1))
    o["a3_wkv"], o["a3_bkv"] = f["L3_attn_wkv"], f["L3_attn_bkv"].reshape(-1, 1)
    o["a3_wv"] = np.concatenate([f["L3_attn_wv"], f["L3_attn_bv"][None, :]], axis=0)
    inv = (np.float32(1.0) / np.float32(10000.0) ** (np.arange(0, P, 2, dtype=np.float32) / np.float32(P))).astype(np.float32)
    ang = np.arange(L, dtype=np.float32)[None, :] * inv[:, None]
    sine = np.sin(ang)
    o["trig"] = c(np.stack([np.concatenate([np.cos(ang)] * 2), np.concatenate([-sine, sine])], axis=1).astype(np.float32))
    o["o3_w"], o["o3_b"] = f["L3_attn_wo"], col(f["L3_attn_bo"])
    o["tri"] = np.broadcast_to(np.tril(np.ones((4, 4), np.float32), -1), (P, 4, 4)).copy()

    def router(tag, w, b):
        o[f"r{tag}_w"] = c(f[w].T)
        if b is not None:
            o[f"r{tag}_b"] = np.broadcast_to(f[b], (P, f[b].shape[0])).copy()

    router("0", "L0_ffn_router_w", "L0_ffn_correction_bias")
    router("1", "L1_ffn_router_w", "L1_ffn_expert_bias")
    router("2", "L2_ffn_gate_weight", "L2_ffn_e_bias")
    router("3", "L3_ffn_gate_w", None)

    def pack(*blocks):
        return c(np.stack(blocks, axis=2).transpose(1, 0, 2, 3))

    def select(per_block, per_group, n_loop, n_res_shared, repeat=1):
        out = np.zeros((NPART * per_group + 1, n_loop + n_res_shared, P), np.float32)
        for blk in range(n_loop):
            for m in range(P):
                e = (blk // repeat) * per_block + m // (P // per_block)
                out[np.arange(NPART) * per_group + e, blk, m] = 1.0
        out[-1, n_loop:, :] = 1.0
        return out.astype(bf)

    def cat(a, b):
        return np.concatenate([a, b], axis=0)

    def gate0(w):
        return w.reshape(4, 4, P, 32).transpose(0, 2, 1, 3).reshape(4, P, P)

    o["e0_w"] = pack(cat(gate0(f["L0_ffn_gate_w"]), f["L0_ffn_shared_gate_w"].reshape(2, P, P).transpose(0, 2, 1)),
                     cat(gate0(f["L0_ffn_up_w"]), f["L0_ffn_shared_up_w"].reshape(2, P, P).transpose(0, 2, 1)),
                     cat(f["L0_ffn_down_w"].reshape(4, P, P), f["L0_ffn_shared_down_w"].T.reshape(2, P, P)))
    o["e0_sel"] = select(4, 16, 4, 2)
    sg = np.zeros((1, P, P), np.float32)
    sg[0, :, :64] = f["L1_ffn_w_gate_shared"].T
    sd = np.zeros((1, P, P), np.float32)
    sd[0, :64, :] = f["L1_ffn_w_down_shared"].T
    o["e1_w"] = pack(cat(f["L1_ffn_w_gate"].reshape(80, P, P).transpose(0, 2, 1), sg),
                     cat(f["L1_ffn_w_down"].reshape(80, 2, P, 64).transpose(0, 1, 3, 2).reshape(80, P, P), sd))
    o["e1_sel"] = select(2, 40, 20, 1)
    o["e2_w"] = pack(f["L2_ffn_gate_proj"].reshape(8, P, P).transpose(0, 2, 1),
                     f["L2_ffn_up_proj"].reshape(8, P, P).transpose(0, 2, 1),
                     f["L2_ffn_down_proj"].reshape(8, 2, P, 64).transpose(0, 1, 3, 2).reshape(8, P, P))
    o["e2_sel"] = select(2, 16, 8, 0)

    def gate3(w):
        return w.reshape(8, P, 4, P).transpose(0, 2, 1, 3).reshape(32, P, P)

    def shared3(w):
        return w.reshape(P, 2, P).transpose(1, 0, 2)

    o["e3_w"] = pack(cat(gate3(f["L3_ffn_gate_k"]), shared3(f["L3_ffn_sh_gate"])),
                     cat(gate3(f["L3_ffn_up_k"]), shared3(f["L3_ffn_sh_up"])),
                     cat(f["L3_ffn_down_k"].reshape(32, P, P), f["L3_ffn_sh_down"].reshape(2, P, P)))
    o["e3_sel"] = select(1, 8, 32, 2, repeat=4)
    return o


def kernel(**inputs):
    import concourse.bacc as bacc
    from concourse.bass_utils import run_bass_kernel_spmd

    nc = bacc.Bacc("TRN2", target_bir_lowering=False, num_devices=1)
    arrays, io = {}, {}
    for name, a in layouts(inputs).items():
        a = np.ascontiguousarray(a)
        arrays[f"in_{name}"] = a
        io[name] = nc.dram_tensor(f"in_{name}", a.shape, mybir.dt.from_np(a.dtype), kind="ExternalInput").ap()
    io["out"] = nc.dram_tensor("out_x", (P, T), F32, kind="ExternalOutput").ap()
    program(nc, io)
    r = run_bass_kernel_spmd(nc, [arrays], core_ids=[0])
    return np.ascontiguousarray(r.results[0]["out_x"].reshape(P, B, L).transpose(1, 2, 0))
```

```python
from contextlib import ExitStack, contextmanager

import numpy as np

import concourse.bass as bass
from concourse import mybir

ALU = mybir.AluOpType
ACT = mybir.ActivationFunctionType
F32 = mybir.dt.float32
BF16 = mybir.dt.bfloat16
AX = mybir.AxisListType

P = 128
B, L = 4, 1024
T = B * L
CH = 512
NC = T // CH
EPS = 1e-5
BIG = 1e30

NS = 16
DD = 64
NT = 4
SP = 32

NH, HD = 16, 8
GH = 4
KT = L // P
NPART = 3
ROWS = NPART * NPART * HD


@contextmanager
def stage(nc, name):
    sems = []
    with ExitStack() as ctx:
        def sb(n, shape, dt=F32):
            return ctx.enter_context(nc.sbuf_tensor(f"{name}_{n}", shape, dt))

        def ps(n, shape, dt=F32):
            return ctx.enter_context(nc.psum_tensor(f"{name}_{n}", shape, dt))

        def sem(n):
            sems.append(nc.alloc_semaphore(f"{name}_{n}"))
            return sems[-1]

        yield sb, ps, sem
        nc.clear_and_free_semaphores(sems)
        nc.all_engine_barrier()


class Steps:

    def __init__(self, eng, sem, base=0):
        self.eng, self.sem, self.base, self.n = eng, sem, base, 0

    def __call__(self, ins, apart=False):
        self.n += 1
        ins.then_inc(self.sem, 1)
        if apart:
            wait_apart(self.eng, self.sem, self.base + self.n)
        else:
            self.eng.wait_ge(self.sem, self.base + self.n)


def wait_apart(eng, sem, value):
    eng.wait_ge(sem, value)
    eng.nop(nofuse=True)


def at(t, start, size):
    return t[:, bass.ds(start, size)]


def load(eng, sem, pairs):
    for dst, src in pairs:
        eng.dma_start(dst, src).then_inc(sem, 16)


def normalise(nc, name, src, dst, average, centre, weight=None, shift=None, first_load=None, eps=EPS):
    with stage(nc, name) as (sb, ps, sem):
        dev = sb("dev", [P, 2, CH])
        sq = sb("sq", [P, 2, CH])
        sd = sb("sd", [P, 2, CH])
        rs = sb("rs", [P, 2, CH])
        epst = sb("eps", [P, 1])
        mean = ps("mean", [P, 2, CH])
        var = ps("var", [P, 2, CH])
        loaded = sem("loaded")
        eps_set = sem("eps_set")
        scaled = sem("scaled")
        mean_ready = [sem(f"mean_ready{u}") for u in range(2)]
        dev_ready = [sem(f"dev_ready{u}") for u in range(2)]
        sq_ready = [sem(f"sq_ready{u}") for u in range(2)]
        var_ready = [sem(f"var_ready{u}") for u in range(2)]
        sd_ready = [sem(f"sd_ready{u}") for u in range(2)]
        rs_ready = [sem(f"rs_ready{u}") for u in range(2)]
        out_ready = [sem(f"out_ready{u}") for u in range(2)]
        n_load = len(first_load or [])
        with nc.Block() as block:
            @block.sync
            def _(sp):
                load(sp, loaded, first_load or [])
                if n_load:
                    sp.wait_ge(loaded, 16 * n_load)

            @block.tensor
            def _(pe):
                if n_load:
                    pe.wait_ge(loaded, 16 * n_load)
                with pe.Fori(0, NC // 2) as i:
                    if centre:
                        for u in range(2):
                            pe.wait_ge(dev_ready[u], i)
                            pe.matmul(mean[:, u, :], average[:, :], at(src, i * 2 * CH + u * CH, CH),
                                      start=True, stop=True).then_inc(mean_ready[u], 1)
                    for u in range(2):
                        pe.wait_ge(sq_ready[u], i + 1)
                        pe.wait_ge(sd_ready[u], i)
                        pe.matmul(var[:, u, :], average[:, :], sq[:, u, :],
                                  start=True, stop=True).then_inc(var_ready[u], 1)

            @block.scalar
            def _(act):
                act.wait_ge(eps_set, 1)
                if n_load:
                    act.wait_ge(loaded, 16 * n_load)
                with act.Fori(0, NC // 2) as i:
                    for u in range(2):
                        act.wait_ge(var_ready[u], i)
                        if centre:
                            act.wait_ge(dev_ready[u], i + 1)
                            act.activation(sq[:, u, :], dev[:, u, :], ACT.Square).then_inc(sq_ready[u], 1)
                        else:
                            act.activation(sq[:, u, :], at(src, i * 2 * CH + u * CH, CH),
                                           ACT.Square).then_inc(sq_ready[u], 1)
                    for u in range(2):
                        act.wait_ge(rs_ready[u], i)
                        act.wait_ge(var_ready[u], i + 1)
                        act.activation(sd[:, u, :], var[:, u, :], ACT.Sqrt,
                                       bias=epst[:, 0:1]).then_inc(sd_ready[u], 1)

            @block.vector
            def _(dve):
                dve.memset(epst[:, :], eps).then_inc(eps_set, 1)
                if n_load:
                    dve.wait_ge(loaded, 16 * n_load)
                with dve.Fori(0, NC // 2) as i:
                    if centre:
                        for u in range(2):
                            dve.wait_ge(mean_ready[u], i + 1)
                            dve.wait_ge(sq_ready[u], i)
                            dve.wait_ge(out_ready[u], i)
                            dve.tensor_tensor(dev[:, u, :], at(src, i * 2 * CH + u * CH, CH), mean[:, u, :],
                                              ALU.subtract).then_inc(dev_ready[u], 1)
                    for u in range(2):
                        dve.wait_ge(sd_ready[u], i + 1)
                        dve.wait_ge(out_ready[u], i)
                        dve.reciprocal(rs[:, u, :], sd[:, u, :]).then_inc(rs_ready[u], 1)
                    for u in range(2):
                        dve.wait_ge(rs_ready[u], i + 1)
                        out = at(dst, i * 2 * CH + u * CH, CH)
                        if centre and weight is None:
                            dve.tensor_tensor(out, dev[:, u, :], rs[:, u, :], ALU.mult).then_inc(out_ready[u], 1)
                        else:
                            in0 = dev[:, u, :] if centre else at(src, i * 2 * CH + u * CH, CH)
                            ins = dve.scalar_tensor_tensor(out=out, in0=in0, scalar=weight[:, 0:1], in1=rs[:, u, :],
                                                           op0=ALU.mult, op1=ALU.mult)
                            if shift is not None:
                                ins.then_inc(scaled, 1)
                                dve.wait_ge(scaled, 2 * i + u + 1)
                                ins = dve.tensor_scalar(out, out, shift[:, 0:1], None, ALU.add)
                            ins.then_inc(out_ready[u], 1)


def mamba_inputs(nc, io, x2, gate, xs, consts):
    with stage(nc, "mi") as (sb, ps, sem):
        w = sb("w", [P, 2, 2, P])
        cw = sb("cw", [P, 2, NT])
        cb = sb("cb", [P, 2])
        padded = sb("padded", [P, 2, NT - 1 + L])
        conv = sb("conv", [P, 2, L])
        pskip = ps("pskip", [P, 2, L])
        pin = ps("pin", [P, 2, L])
        loaded = sem("loaded")
        pad_set = sem("pad_set")
        skip_ready = sem("skip_ready")
        gate_ready = sem("gate_ready")
        in_ready = sem("in_ready")
        padded_ready = sem("padded_ready")
        conv_steps = sem("conv_steps")
        conv_ready = sem("conv_ready")
        xs_ready = sem("xs_ready")
        with nc.Block() as block:
            @block.sync
            def _(sp):
                load(sp, loaded, [(w[:, :, :, :], io["m_w"]), (cw[:, :, :], io["m_cw"]), (cb[:, :], io["m_cb"])])
                sp.wait_ge(loaded, 48)

            @block.tensor
            def _(pe):
                pe.wait_ge(loaded, 48)
                with pe.Fori(0, B) as b:
                    for h in range(2):
                        pe.wait_ge(gate_ready, 2 * b)
                        for c in range(2):
                            mm = pe.matmul(pskip[:, h, c * CH:(c + 1) * CH], w[:, 0, h, :],
                                           at(x2, b * L + c * CH, CH), start=True, stop=True)
                        mm.then_inc(skip_ready, 1)
                    for h in range(2):
                        pe.wait_ge(padded_ready, 2 * b)
                        for c in range(2):
                            mm = pe.matmul(pin[:, h, c * CH:(c + 1) * CH], w[:, 1, h, :],
                                           at(x2, b * L + c * CH, CH), start=True, stop=True)
                        mm.then_inc(in_ready, 1)

            @block.scalar
            def _(act):
                act.wait_ge(pad_set, 1)
                with act.Fori(0, B) as b:
                    for h in range(2):
                        act.wait_ge(in_ready, 2 * b + h + 1)
                        act.wait_ge(conv_ready, 2 * b)
                        act.activation(padded[:, h, NT - 1:], pin[:, h, :], ACT.Copy).then_inc(padded_ready, 1)
                    for h in range(2):
                        act.wait_ge(skip_ready, 2 * b + h + 1)
                        act.activation(at(gate, (b * 2 + h) * L, L), pskip[:, h, :],
                                       ACT.Silu).then_inc(gate_ready, 1)
                    for h in range(2):
                        act.wait_ge(conv_ready, 2 * b + h + 1)
                        act.activation(at(xs, (b * 2 + h) * L, L), conv[:, h, :], ACT.Silu,
                                       bias=cb[:, h:h + 1]).then_inc(xs_ready, 1)

            @block.vector
            def _(dve):
                dve.memset(padded[:, :, 0:NT - 1], 0.0).then_inc(pad_set, 1)
                dve.wait_ge(loaded, 48)
                with dve.Fori(0, B) as b:
                    for h in range(2):
                        dve.wait_ge(padded_ready, 2 * b + h + 1)
                        dve.wait_ge(xs_ready, 2 * b)
                        dve.wait_ge(conv_ready, 2 * b + h)
                        for k in range(NT):
                            tap = padded[:, h, k:k + L]
                            if k == 0:
                                ins = dve.tensor_scalar(conv[:, h, :], tap, cw[:, h, 0:1], None, ALU.mult)
                            else:
                                ins = dve.scalar_tensor_tensor(out=conv[:, h, :], in0=tap, scalar=cw[:, h, k:k + 1],
                                                               in1=conv[:, h, :], op0=ALU.mult, op1=ALU.add)
                            if k < NT - 1:
                                ins.then_inc(conv_steps, 1)
                                dve.wait_ge(conv_steps, (2 * b + h) * (NT - 1) + k + 1)
                        ins.then_inc(conv_ready, 1)


def mamba_steps(nc, io, xs, delta, parts_b, parts_c):
    with stage(nc, "md") as (sb, ps, sem):
        w1 = sb("w1", [P, 2, DD])
        wbc = sb("wbc", [P, 2, 2, NPART * SP])
        w2 = sb("w2", [DD, 2, P])
        b2 = sb("b2", [P, 2])
        low = sb("low", [DD, L])
        rest = sb("rest", [NPART * SP, 2, L])
        mid = sb("mid", [NPART * SP, 2, L], BF16)
        z = sb("z", [P, 2, L])
        za = sb("za", [P, 2, L])
        one = sb("one", [P, 1])
        pslot = ps("pslot", [P, 4, L])
        plow, pb, pc = pslot[:, 0, :], pslot[:, 1, :], pslot[:, 2, :]
        pz = pslot[:, 3, :]
        loaded = sem("loaded")
        one_set = sem("one_set")
        low_mm, bc_mm, z_mm = sem("low_mm"), sem("bc_mm"), sem("z_mm")
        low_ready = sem("low_ready")
        hi_ready, rest_ready, mid_ready, lo_ready = sem("hi_ready"), sem("rest_ready"), sem("mid_ready"), sem("lo_ready")
        z_ready = sem("z_ready")
        soft_steps = sem("soft_steps")
        soft_ready = sem("soft_ready")
        delta_ready = sem("delta_ready")
        R = NPART * SP
        store = [parts_b, parts_c]
        with nc.Block() as block:
            @block.sync
            def _(sp):
                load(sp, loaded, [(w1[:, :, :], io["m_w1"]), (wbc[:, :, :, :], io["m_wbc"]),
                                  (w2[:, :, :], io["m_w2"]), (b2[:, :], io["m_b2"])])
                sp.wait_ge(loaded, 64)

            @block.tensor
            def _(pe):
                pe.wait_ge(loaded, 64)
                with pe.Fori(0, B) as b:
                    pe.wait_ge(low_ready, b)
                    for c in range(2):
                        for h in range(2):
                            mm = pe.matmul(plow[0:DD, c * CH:(c + 1) * CH], w1[:, h, :],
                                           at(xs, (b * 2 + h) * L + c * CH, CH), start=(h == 0), stop=(h == 1))
                    mm.then_inc(low_mm, 1)
                    for j, p in enumerate((pb, pc)):
                        pe.wait_ge(rest_ready, 2 * b)
                        for c in range(2):
                            for h in range(2):
                                mm = pe.matmul(p[0:R, c * CH:(c + 1) * CH], wbc[:, h, j, :],
                                               at(xs, (b * 2 + h) * L + c * CH, CH), start=(h == 0), stop=(h == 1))
                        mm.then_inc(bc_mm, 1)
                    pe.wait_ge(low_ready, b + 1)
                    for h in range(2):
                        pe.wait_ge(z_ready, 2 * b + h)
                        for c in range(2):
                            mm = pe.matmul(pz[:, c * CH:(c + 1) * CH], w2[:, h, :], low[:, c * CH:(c + 1) * CH],
                                           start=True, stop=True)
                        mm.then_inc(z_mm, 1)

            @block.scalar
            def _(act):
                act.wait_ge(loaded, 64)
                act.wait_ge(one_set, 1)
                with act.Fori(0, B) as b:
                    act.wait_ge(low_mm, b + 1)
                    act.wait_ge(z_mm, 2 * b)
                    act.activation(low[:, :], plow[0:DD, :], ACT.Copy).then_inc(low_ready, 1)
                    for j, p in enumerate((pb, pc)):
                        act.wait_ge(bc_mm, 2 * b + j + 1)
                        act.activation(store[j][:, bass.ds(b * L, L)], p[0:R, :], ACT.Copy).then_inc(hi_ready, 1)
                    for h in range(2):
                        act.wait_ge(z_mm, 2 * b + h + 1)
                        act.wait_ge(delta_ready, 2 * b)
                        act.activation(z[:, h, :], pz[:, :], ACT.Identity, bias=b2[:, h:h + 1]).then_inc(z_ready, 1)
                    for j in range(2):
                        act.wait_ge(rest_ready, 2 * b + j + 1)
                        act.activation(store[j][SP:2 * SP, bass.ds(b * L, L)], rest[SP:2 * SP, j, :],
                                       ACT.Copy).then_inc(mid_ready, 1)
                        act.wait_ge(lo_ready, 2 * b)
                        act.activation(mid[2 * SP:R, j, :], rest[2 * SP:R, j, :], ACT.Copy).then_inc(mid_ready, 1)
                    step = Steps(act, soft_steps, 6 * b)
                    for h in range(2):
                        act.wait_ge(z_ready, 2 * b + h + 1)
                        act.wait_ge(delta_ready, 2 * b)
                        step(act.activation(za[:, h, :], z[:, h, :], ACT.Abs))
                        step(act.activation(za[:, h, :], za[:, h, :], ACT.Exp, scale=-1.0))
                        step(act.activation(za[:, h, :], za[:, h, :], ACT.Ln, bias=one[:, 0:1]))

            @block.vector
            def _(dve):
                dve.memset(one[:, :], 1.0).then_inc(one_set, 1)
                with dve.Fori(0, B) as b:
                    for j, p in enumerate((pb, pc)):
                        dve.wait_ge(hi_ready, 2 * b + j + 1)
                        dve.wait_ge(mid_ready, 4 * b)
                        dve.wait_ge(lo_ready, 2 * b)
                        dve.tensor_tensor(rest[:, j, :], p[0:R, :], store[j][:, bass.ds(b * L, L)],
                                          ALU.subtract).then_inc(rest_ready, 1)
                    for j in range(2):
                        dve.wait_ge(mid_ready, 4 * b + 2 * j + 2)
                        dve.wait_ge(rest_ready, 2 * b + j + 1)
                        dve.tensor_tensor(store[j][2 * SP:R, bass.ds(b * L, L)], rest[2 * SP:R, j, :], mid[2 * SP:R, j, :],
                                          ALU.subtract).then_inc(lo_ready, 1)
                    for h in range(2):
                        dve.wait_ge(soft_steps, 6 * b + 3 * h + 3)
                        dve.scalar_tensor_tensor(out=at(delta, (b * 2 + h) * L, L), in0=z[:, h, :], scalar=0.0,
                                                 in1=za[:, h, :], op0=ALU.max, op1=ALU.add).then_inc(delta_ready, 1)


def mamba_scan(nc, io, xs, gate, delta, parts_b, parts_c, ident):
    R = NPART * SP
    with stage(nc, "ms") as (sb, ps, sem):
        sel = sb("sel", [R, NS, P], BF16)
        a_log = sb("a_log", [P, 2, NS])
        a_exp = sb("a_exp", [P, 2, NS])
        a_neg = sb("a_neg", [P, 2, NS])
        w_d = sb("w_d", [P, 2])
        a_cur = sb("a_cur", [P, NS])
        d_cur = sb("d_cur", [P, 1])
        u = sb("u", [P, L])
        decay = sb("decay", [P, 2, L])
        c_sb = sb("c_sb", [P, 2, L])
        drive = sb("drive", [P, 2, L])
        hs = sb("hs", [P, 2, L])
        hc = sb("hc", [P, 2, L])
        y1 = sb("y1", [P, L])
        p_b = ps("p_b", [P, 2, L])
        p_c = ps("p_c", [P, L])
        p_y = ps("p_y", [P, L])
        loaded = sem("loaded")
        a_ready = sem("a_ready")
        cur_ready = sem("cur_ready")
        b_mm, c_mm, y_mm = sem("b_mm"), sem("c_mm"), sem("y_mm")
        decay_ready, c_ready = sem("decay_ready"), sem("c_ready")
        drive_ready, h_ready, hc_ready = sem("drive_ready"), sem("h_ready"), sem("hc_ready")
        y1_ready, y_done = sem("y1_ready"), sem("y_done")
        with nc.Block() as block:
            @block.sync
            def _(sp):
                load(sp, loaded, [(sel[:, :, :], io["m_sel"]), (a_log[:, :, :], io["m_alog"]), (w_d[:, :], io["m_wd"])])
                sp.wait_ge(loaded, 48)

            @block.tensor
            def _(pe):
                pe.wait_ge(loaded, 48)
                with pe.Fori(0, B) as b, pe.Fori(0, 2) as h:
                    it = b * 2 + h

                    def spread(n):
                        if n >= 2:
                            pe.wait_ge(drive_ready, it * NS + n - 1)
                        else:
                            pe.wait_ge(drive_ready, it * NS)
                        for c in range(2):
                            mm = pe.matmul(p_b[:, n % 2, c * CH:(c + 1) * CH], sel[:, n, :],
                                           parts_b[:, bass.ds(b * L + c * CH, CH)], start=True, stop=True)
                        mm.then_inc(b_mm, 1)
                        pe.wait_ge(c_ready, it * NS + n)
                        for c in range(2):
                            mm = pe.matmul(p_c[:, c * CH:(c + 1) * CH], sel[:, n, :],
                                           parts_c[:, bass.ds(b * L + c * CH, CH)], start=True, stop=True)
                        mm.then_inc(c_mm, 1)

                    def add(n):
                        if n == 0:
                            pe.wait_ge(y1_ready, it)
                        pe.wait_ge(hc_ready, it * NS + n + 1)
                        for c in range(2):
                            mm = pe.matmul(p_y[:, c * CH:(c + 1) * CH], ident[:, :], hc[:, n % 2, c * CH:(c + 1) * CH],
                                           start=(n == 0), stop=(n == NS - 1))
                        mm.then_inc(y_mm, 1)

                    spread(0)
                    for n in range(NS):
                        if n + 1 < NS:
                            spread(n + 1)
                        if n >= 1:
                            add(n - 1)
                    add(NS - 1)

            @block.scalar
            def _(act):
                act.wait_ge(loaded, 48)
                act.activation(a_exp[:, :, :], a_log[:, :, :], ACT.Exp).then_inc(a_ready, 1)
                with act.Fori(0, B) as b, act.Fori(0, 2) as h:
                    it = b * 2 + h
                    act.wait_ge(cur_ready, it + 1)
                    for n in range(NS):
                        if n >= 2:
                            wait_apart(act, h_ready, it * NS + n - 1)
                        act.activation(decay[:, n % 2, :], at(delta, it * L, L), ACT.Exp,
                                       scale=a_cur[:, n:n + 1]).then_inc(decay_ready, 1)
                        act.wait_ge(c_mm, it * NS + n + 1)
                        if n >= 2:
                            act.wait_ge(hc_ready, it * NS + n - 1)
                        else:
                            act.wait_ge(hc_ready, it * NS)
                        act.activation(c_sb[:, n % 2, :], p_c[:, :], ACT.Copy).then_inc(c_ready, 1)

            @block.gpsimd
            def _(pool):
                with pool.Fori(0, B * 2) as it:
                    for n in range(NS):
                        pool.wait_ge(h_ready, it * NS + n + 1)
                        pool.wait_ge(c_ready, it * NS + n + 1)
                        if n >= 2:
                            pool.wait_ge(y_mm, it * NS + n - 1)
                        else:
                            pool.wait_ge(y_mm, it * NS)
                        pool.tensor_tensor(hc[:, n % 2, :], hs[:, n % 2, :], c_sb[:, n % 2, :],
                                           ALU.mult).then_inc(hc_ready, 1)

            @block.vector
            def _(dve):
                dve.wait_ge(a_ready, 1)
                dve.tensor_scalar(a_neg[:, :, :], a_exp[:, :, :], -1.0, None, ALU.mult).then_inc(a_ready, 1)
                dve.wait_ge(a_ready, 2)
                with dve.Fori(0, B) as b, dve.Fori(0, 2) as h:
                    it = b * 2 + h
                    dve.wait_ge(decay_ready, it * NS)
                    dve.wait_ge(y_done, it)
                    dve.tensor_copy(a_cur[:, :], a_neg[:, bass.ds(h, 1), :].rearrange("p a n -> p (a n)"))
                    dve.tensor_copy(d_cur[:, :], w_d[:, bass.ds(h, 1)])
                    dve.tensor_tensor(u[:, :], at(delta, it * L, L), at(xs, it * L, L),
                                      ALU.mult).then_inc(cur_ready, 1)
                    dve.wait_ge(cur_ready, it + 1)
                    for n in range(NS):
                        dve.wait_ge(b_mm, it * NS + n + 1)
                        if n >= 2:
                            dve.wait_ge(h_ready, it * NS + n - 1)
                        dve.tensor_tensor(drive[:, n % 2, :], p_b[:, n % 2, :], u[:, :],
                                          ALU.mult).then_inc(drive_ready, 1)
                        dve.wait_ge(drive_ready, it * NS + n + 1)
                        dve.wait_ge(decay_ready, it * NS + n + 1)
                        if n >= 2:
                            dve.wait_ge(hc_ready, it * NS + n - 1)
                        else:
                            dve.wait_ge(hc_ready, it * NS)
                        dve.tensor_tensor_scan(hs[:, n % 2, :], decay[:, n % 2, :], drive[:, n % 2, :], 0.0,
                                               ALU.mult, ALU.add).then_inc(h_ready, 1)
                    dve.wait_ge(y_mm, it * NS + NS)
                    dve.scalar_tensor_tensor(out=y1[:, :], in0=at(xs, it * L, L), scalar=d_cur[:, 0:1], in1=p_y[:, :],
                                             op0=ALU.mult, op1=ALU.add).then_inc(y1_ready, 1)
                    dve.wait_ge(y1_ready, it + 1)
                    dve.tensor_tensor(at(xs, it * L, L), y1[:, :], at(gate, it * L, L),
                                      ALU.mult).then_inc(y_done, 1)


def mamba_out(nc, io, y, xn, s):
    with stage(nc, "mo") as (sb, ps, sem):
        w = sb("w", [P, 2, P])
        p = ps("p", [P, 2, L])
        loaded = sem("loaded")
        mm_ready = [sem(f"mm_ready{u}") for u in range(2)]
        s_ready = [sem(f"s_ready{u}") for u in range(2)]
        with nc.Block() as block:
            @block.sync
            def _(sp):
                load(sp, loaded, [(w[:, :, :], io["m_wo"])])
                sp.wait_ge(loaded, 16)

            @block.tensor
            def _(pe):
                pe.wait_ge(loaded, 16)
                with pe.Fori(0, B // 2) as i:
                    for u in range(2):
                        b = i * 2 + u
                        pe.wait_ge(s_ready[u], i)
                        for c in range(2):
                            for h in range(2):
                                mm = pe.matmul(p[:, u, c * CH:(c + 1) * CH], w[:, h, :],
                                               at(y, (b * 2 + h) * L + c * CH, CH), start=(h == 0), stop=(h == 1))
                        mm.then_inc(mm_ready[u], 1)

            @block.vector
            def _(dve):
                with dve.Fori(0, B // 2) as i:
                    for u in range(2):
                        dve.wait_ge(mm_ready[u], i + 1)
                        dve.tensor_tensor(at(s, (i * 2 + u) * L, L), at(xn, (i * 2 + u) * L, L), p[:, u, :],
                                          ALU.add).then_inc(s_ready[u], 1)


def route(nc, io, tag, xn, comb, experts, per_group, top, kind):
    E, EG = experts, per_group
    NG = E // EG
    R = NPART * EG + 1
    TT = CH // P
    grouped = kind.startswith("grouped")
    PAD = 256 if E > P else P
    with stage(nc, "r" + tag) as (sb, ps, sem):
        w = sb("w", [P, E])
        bias = sb("bias", [P, E])
        tri = sb("tri", [P, 4, 4])
        xst = sb("xst", [P, 2, CH])
        lin = sb("lin", [P, 2, TT, E])
        sc = sb("sc", [P, 2, TT, E])
        biased = sb("biased", [P, TT, E])
        pair = sb("pair", [P, TT * 4, 6])
        gsum = sb("gsum", [P, TT * 4])
        beats = sb("beats", [P, TT, 4, 4])
        ties = sb("ties", [P, TT, 4, 4])
        rank = sb("rank", [P, TT * 4])
        gmask = sb("gmask", [P, TT * 4])
        glow = sb("glow", [P, TT * 4])
        cand = sb("cand", [P, TT, E])
        top8 = sb("top8", [P, TT, 8])
        above = sb("above", [P, TT, E])
        equal = sb("equal", [P, TT, E])
        order = sb("order", [P, TT, E])
        ones = sb("ones", [P, E])
        count = sb("count", [P, TT])
        need = sb("need", [P, TT])
        low = sb("low", [P, TT, E])
        weight = sb("weight", [P, TT, E])
        total = sb("total", [P, TT])
        recip = sb("recip", [P, TT])
        rest = sb("rest", [P, TT, E])
        parts = sb("parts", [P, 2, TT, NG, R], BF16)
        plog = ps("plog", [P, 2, TT, PAD])
        pt = ps("pt", [P, NG, 2 * CH], BF16)
        loaded, set_up = sem("loaded"), sem("set_up")
        staged = [sem(f"staged{u}") for u in range(2)]
        logit_mm = [sem(f"logit_mm{u}") for u in range(2)]
        lin_ready = [sem(f"lin_ready{u}") for u in range(2)]
        sc_ready = [sem(f"sc_ready{u}") for u in range(2)]
        steps = sem("steps")
        parts_ready = [sem(f"parts_ready{u}") for u in range(2)]
        turned = sem("turned")
        comb_ready = sem("comb_ready")
        identb = io["sb_identb"]
        loads = [(w[:, :], io[f"r{tag}_w"]), (tri[:, :, :], io["tri"])]
        has_bias = kind != "softmax"
        if has_bias:
            loads.append((bias[:, :], io[f"r{tag}_b"]))
        NL = 16 * len(loads)
        prob_steps = 3 if kind == "softmax" else 0
        period = {"softmax": 0, "sigmoid": 0, "grouped": 12, "grouped_low": 14}[kind] + prob_steps
        period += 2 * TT + 8 + (0 if kind == "softmax" else 4 if kind != "sigmoid" else 5) + 3

        def wide(t, n):
            return t[:, :].unsqueeze(2).to_broadcast([P, TT, n])

        with nc.Block() as block:
            @block.sync
            def _(sp):
                load(sp, loaded, loads)
                sp.wait_ge(loaded, NL)

            @block.gpsimd
            def _(pool):
                with pool.Fori(0, NC // 2) as i:
                    for u in range(2):
                        pool.wait_ge(logit_mm[u], i)
                        pool.tensor_copy(xst[:, u, :], at(xn, i * 2 * CH + u * CH, CH)).then_inc(staged[u], 1)

            @block.tensor
            def _(pe):
                pe.wait_ge(loaded, NL)
                with pe.Fori(0, NC // 2) as i:
                    for u in range(2):
                        pe.wait_ge(staged[u], i + 1)
                        pe.wait_ge(sc_ready[u], i)
                        for t in range(TT):
                            mm = pe.matmul(plog[:, u, t, 0:E], xst[:, u, t * P:(t + 1) * P], w[:, :],
                                           start=True, stop=True)
                        mm.then_inc(logit_mm[u], 1)
                    for u in range(2):
                        pe.wait_ge(parts_ready[u], i + 1)
                        for g in range(NG):
                            wait_apart(pe, comb_ready, (2 * i + u) * NG)
                            for t in range(TT):
                                mm = pe.transpose(pt[0:R, g, t * P:(t + 1) * P], parts[:, u, t, g, :], identb[:, :])
                            mm.then_inc(turned, 1)

            @block.scalar
            def _(act):
                with act.Fori(0, NC // 2) as i:
                    for u in range(2):
                        act.wait_ge(parts_ready[u], i)
                        if kind == "softmax":
                            act.wait_ge(lin_ready[u], i + 1)
                            act.activation(sc[:, u], lin[:, u], ACT.Exp).then_inc(sc_ready[u], 1)
                        elif kind == "sigmoid":
                            act.wait_ge(lin_ready[u], i + 1)
                            act.activation(sc[:, u], lin[:, u], ACT.Sigmoid).then_inc(sc_ready[u], 1)
                        else:
                            act.wait_ge(logit_mm[u], i + 1)
                            act.activation(sc[:, u], plog[:, u, :, 0:E], ACT.Sigmoid).then_inc(sc_ready[u], 1)
                    for u in range(2):
                        for g in range(NG):
                            act.wait_ge(turned, (2 * i + u) * NG + g + 1)
                            act.activation(comb[0:R, g, bass.ds(i * 2 * CH + u * CH, CH)], pt[0:R, g, 0:CH],
                                           ACT.Copy).then_inc(comb_ready, 1)

            @block.vector
            def _(dve):
                dve.memset(parts[:, :, :, :, R - 1:R], 1.0).then_inc(set_up, 1)
                dve.memset(ones[:, :], 1.0).then_inc(set_up, 1)
                dve.wait_ge(set_up, 2)
                dve.wait_ge(loaded, NL)
                with dve.Fori(0, NC // 2) as i:
                    if kind in ("softmax", "sigmoid"):
                        for u in range(2):
                            dve.wait_ge(logit_mm[u], i + 1)
                            dve.wait_ge(sc_ready[u], i)
                            if kind == "softmax":
                                step = Steps(dve, steps, (2 * i + u) * 1 + 2 * i * period + 0)
                                ins = dve.tensor_reduce(total[:, :], plog[:, u, :, 0:E], AX.X, ALU.max)
                                step(ins)
                                dve.tensor_tensor(lin[:, u], plog[:, u, :, 0:E], wide(total, E),
                                                  ALU.subtract).then_inc(lin_ready[u], 1)
                                dve.wait_ge(lin_ready[u], i + 1)
                            else:
                                dve.tensor_tensor(lin[:, u], plog[:, u, :, 0:E],
                                                  bias[:, :].unsqueeze(1).to_broadcast([P, TT, E]),
                                                  ALU.add).then_inc(lin_ready[u], 1)
                    extra = 2 if kind == "softmax" else 0
                    for u in range(2):
                        dve.wait_ge(sc_ready[u], i + 1)
                        wait_apart(dve, turned, (2 * i + u) * NG)
                        step = Steps(dve, steps, (2 * i + u) * period + (2 * i + 2 if extra else 0))
                        score = sc[:, u]
                        if kind == "softmax":
                            step(dve.tensor_reduce(total[:, :], score, AX.X, ALU.add))
                            step(dve.reciprocal(recip[:, :], total[:, :]))
                            step(dve.tensor_tensor(cand[:, :, :], score, wide(recip, E), ALU.mult), apart=True)
                            score = cand[:, :, :]
                        elif kind == "sigmoid":
                            pass
                        else:
                            step(dve.tensor_tensor(biased[:, :, :], score,
                                                   bias[:, :].unsqueeze(1).to_broadcast([P, TT, E]), ALU.add))
                            four = biased[:, :, :].rearrange("p t (g e) -> p (t g) e", e=4)
                            for o, n, d in ((0, 3, 1), (3, 2, 2), (5, 1, 3)):
                                step(dve.tensor_tensor(pair[:, :, o:o + n], four[:, :, 0:n], four[:, :, d:d + n], ALU.add))
                            step(dve.tensor_reduce(gsum[:, :], pair[:, :, :], AX.X, ALU.max))
                            mine = gsum[:, :].rearrange("p (t g) -> p t g", g=4).unsqueeze(3).to_broadcast([P, TT, 4, 4])
                            other = gsum[:, :].rearrange("p (t g) -> p t g", g=4).unsqueeze(2).to_broadcast([P, TT, 4, 4])
                            step(dve.tensor_tensor(beats[:, :, :, :], other, mine, ALU.is_gt))
                            step(dve.tensor_tensor(ties[:, :, :, :], other, mine, ALU.is_equal))
                            step(dve.tensor_tensor(ties[:, :, :, :], ties[:, :, :, :],
                                                   tri[:, :, :].unsqueeze(1).to_broadcast([P, TT, 4, 4]), ALU.mult))
                            step(dve.tensor_tensor(beats[:, :, :, :], beats[:, :, :, :], ties[:, :, :, :], ALU.add))
                            step(dve.tensor_reduce(rank[:, :], beats[:, :, :, :], AX.X, ALU.add))
                            step(dve.tensor_scalar(gmask[:, :], rank[:, :], 2.0, None, ALU.is_lt))
                            cand4 = cand[:, :, :].rearrange("p t (g e) -> p (t g) e", e=4)
                            step(dve.tensor_tensor(cand4, four, gmask[:, :].unsqueeze(2).to_broadcast([P, TT * 4, 4]),
                                                   ALU.mult), apart=True)
                            if kind == "grouped_low":
                                step(dve.tensor_scalar(glow[:, :], gmask[:, :], BIG, -BIG, ALU.mult, ALU.add))
                                step(dve.tensor_tensor(cand4, cand4, glow[:, :].unsqueeze(2).to_broadcast([P, TT * 4, 4]),
                                                       ALU.add), apart=True)
                        src = sc[:, u] if kind == "sigmoid" else cand[:, :, :]
                        for t in range(TT):
                            step(dve.max(top8[:, t, :], src[:, t, :]), apart=True)
                        least = top8[:, :, top - 1:top].to_broadcast([P, TT, E])
                        step(dve.tensor_tensor(above[:, :, :], src, least, ALU.is_gt))
                        step(dve.tensor_tensor(equal[:, :, :], src, least, ALU.is_equal))
                        step(dve.tensor_reduce(count[:, :], above[:, :, :], AX.X, ALU.add))
                        step(dve.tensor_scalar(need[:, :], count[:, :], -1.0, float(top), ALU.mult, ALU.add))
                        for t in range(TT):
                            step(dve.tensor_tensor_scan(order[:, t, :], ones[:, :], equal[:, t, :], 0.0,
                                                        ALU.mult, ALU.add))
                        step(dve.tensor_tensor(low[:, :, :], order[:, :, :], wide(need, E), ALU.is_le))
                        step(dve.tensor_tensor(equal[:, :, :], equal[:, :, :], low[:, :, :], ALU.mult))
                        step(dve.tensor_tensor(above[:, :, :], above[:, :, :], equal[:, :, :], ALU.add))
                        step(dve.tensor_tensor(weight[:, :, :], score, above[:, :, :], ALU.mult))
                        if kind != "softmax":
                            step(dve.tensor_reduce(total[:, :], weight[:, :, :], AX.X, ALU.add))
                            step(dve.tensor_scalar(total[:, :], total[:, :], 1e-9 if kind == "sigmoid" else 1e-20, None,
                                                   ALU.add))
                            step(dve.reciprocal(recip[:, :], total[:, :]))
                            if kind == "sigmoid":
                                step(dve.tensor_scalar(recip[:, :], recip[:, :], 2.5, None, ALU.mult))
                            step(dve.tensor_tensor(weight[:, :, :], weight[:, :, :], wide(recip, E), ALU.mult))
                        wv = weight[:, :, :].rearrange("p t (g e) -> p t g e", e=EG)
                        rv = rest[:, :, :].rearrange("p t (g e) -> p t g e", e=EG)
                        part = [parts[:, u, :, :, a * EG:(a + 1) * EG] for a in range(NPART)]
                        step(dve.tensor_copy(part[0], wv))
                        step(dve.tensor_tensor(rv, wv, part[0], ALU.subtract))
                        step(dve.tensor_copy(part[1], rv))
                        dve.tensor_tensor(part[2], rv, part[1], ALU.subtract).then_inc(parts_ready[u], 1)
                        dve.wait_ge(parts_ready[u], i + 1)
                        assert step.n == period, (kind, step.n, period)


def experts_sum(nc, io, tag, xn, s, x, comb, R, groups, per_group, resident, up, first_load=(), out=None):
    W = 3 if up else 2
    NQ = groups * per_group
    NR = resident
    NB = NQ * 4 + NR
    NSEL = per_group * 4 + NR
    with stage(nc, "e" + tag) as (sb, ps, sem):
        ring = sb("ring", [P, 4, W, P])
        keep = sb("keep", [P, NR, W, P])
        sel = sb("sel", [R, NSEL, P], BF16)
        sg = sb("sg", [P, 2, CH])
        prod = sb("prod", [P, 2, CH])
        hid = sb("hid", [P, 2, CH])
        fs = sb("fs", [P, CH])
        sfs = sb("sfs", [P, CH])
        pg = ps("pg", [P, 2, CH])
        pu = ps("pu", [P, 2, CH])
        pw = ps("pw", [P, 2, CH])
        acc = ps("acc", [P, CH])
        loaded = sem("loaded")
        ring_loaded = [sem(f"ring_loaded{u}") for u in range(4)]
        gate_mm, block_mm = sem("gate_mm"), sem("block_mm")
        sg_ready, prod_ready, hid_ready = sem("sg_ready"), sem("prod_ready"), sem("hid_ready")
        ring_done = [sem(f"ring_done{u}") for u in range(4)]
        keep_done = sem("keep_done")
        fs_ready, x_steps, written = sem("fs_ready"), sem("x_steps"), sem("written")
        loads = [(keep[:, :, :, :], io[f"e{tag}_w"][:, NQ * 4:, :, :]), (sel[:, :, :], io[f"e{tag}_sel"])] + list(first_load)
        NL = 16 * len(loads)
        wd = io[f"e{tag}_w"]

        def blocks(c, eng, visit):
            if NQ:
                for u in range(4):
                    visit(u, u, 0, True)
                if NQ > 1:
                    with eng.Fori(1, NQ) as q:
                        for u in range(4):
                            visit(q * 4 + u, u, q, True)
            for r in range(NR):
                visit(NQ * 4 + r, r, None, False)

        with nc.Block() as block:
            @block.sync
            def _(sp):
                load(sp, loaded, loads)
                if NQ:
                    with sp.Fori(0, NC) as c, sp.Fori(0, NQ) as q:
                        for u in range(4):
                            sp.wait_ge(ring_done[u], c * NQ + q)
                            sp.dma_start(ring[:, u, :, :],
                                         wd[:, bass.ds(q * 4 + u, 1), :, :].rearrange("p a w m -> p (a w) m")
                                         ).then_inc(ring_loaded[u], 16)
                sp.wait_ge(loaded, NL)

            @block.tensor
            def _(pe):
                pe.wait_ge(loaded, NL)
                with pe.Fori(0, NC) as c:
                    base = c * NB
                    prev = []

                    def down(k, u, in_ring, first, last):
                        pe.wait_ge(hid_ready, base + k + 1)
                        if first:
                            pe.wait_ge(fs_ready, c)
                        w = ring if in_ring else keep
                        mm = pe.matmul(acc[:, :], w[:, u, W - 1, :], hid[:, u % 2, :], start=first, stop=last)
                        mm.then_inc(ring_done[u] if in_ring else keep_done, 1)

                    def visit(k, u, q, in_ring):
                        w = ring if in_ring else keep
                        if in_ring:
                            pe.wait_ge(ring_loaded[u], 16 * (c * NQ + q + 1))
                        if isinstance(k, int) and k < 2:
                            pe.wait_ge(hid_ready, base)
                        else:
                            pe.wait_ge(hid_ready, base + k - 1)
                        xc = at(xn, c * CH, CH)
                        pe.matmul(pg[:, u % 2, :], w[:, u, 0, :], xc, start=True, stop=True).then_inc(gate_mm, 1)
                        if up:
                            pe.matmul(pu[:, u % 2, :], w[:, u, 1, :], xc, start=True, stop=True)
                        if in_ring:
                            si = (q % per_group) * 4 + u if groups > 1 else q * 4 + u
                            lhs = sel[:, bass.ds(si, 1), :].rearrange("r a m -> r (a m)")
                            gi = q // per_group if groups > 1 else 0
                        else:
                            lhs, gi = sel[:, per_group * 4 + u, :], 0
                        rhs = comb[0:R, bass.ds(gi, 1), bass.ds(c * CH, CH)].rearrange("r a t -> r (a t)")
                        pe.matmul(pw[:, u % 2, :], lhs, rhs, start=True, stop=True).then_inc(block_mm, 1)
                        if in_ring:
                            if u > 0:
                                down(k - 1, u - 1, True, isinstance(k, int) and k == 1, False)
                            elif not isinstance(k, int):
                                down(k - 1, 3, True, False, False)
                        elif u > 0:
                            down(k - 1, u - 1, False, k == 1, False)
                        elif NQ:
                            down(k - 1, 3, True, False, False)

                    blocks(c, pe, visit)
                    down(NB - 1, NR - 1, False, NB == 1, True)

            @block.scalar
            def _(act):
                with act.Fori(0, NC) as c:
                    base = c * NB

                    def visit(k, u, q, in_ring):
                        act.wait_ge(gate_mm, base + k + 1)
                        if isinstance(k, int) and k < 2:
                            act.wait_ge(hid_ready, base)
                        else:
                            act.wait_ge(hid_ready, base + k - 1)
                        act.activation(sg[:, u % 2, :], pg[:, u % 2, :], ACT.Silu).then_inc(sg_ready, 1)

                    blocks(c, act, visit)
                    act.wait_ge(keep_done, (c + 1) * NR)
                    act.wait_ge(x_steps, 2 * c)
                    act.activation(fs[:, :], acc[:, :], ACT.Silu).then_inc(fs_ready, 1)

            @block.vector
            def _(dve):
                with dve.Fori(0, NC) as c:
                    base = c * NB

                    def visit(k, u, q, in_ring):
                        dve.wait_ge(sg_ready, base + k + 1)
                        dve.wait_ge(block_mm, base + k + 1)
                        if in_ring:
                            if u >= 2:
                                dve.wait_ge(ring_done[u - 2], c * NQ + q + 1)
                            else:
                                dve.wait_ge(ring_done[u + 2], c * NQ + q)
                                dve.wait_ge(keep_done, c * NR)
                        elif u >= 2:
                            dve.wait_ge(keep_done, c * NR + u - 1)
                        elif NQ:
                            dve.wait_ge(ring_done[u + 2], (c + 1) * NQ)
                        else:
                            dve.wait_ge(keep_done, c * NR)
                        gate = sg[:, u % 2, :]
                        if isinstance(k, int) and k < 2:
                            dve.wait_ge(hid_ready, base)
                        else:
                            dve.wait_ge(hid_ready, base + k - 1)
                        if up:
                            dve.tensor_tensor(prod[:, u % 2, :], pu[:, u % 2, :], gate, ALU.mult).then_inc(prod_ready, 1)
                            dve.wait_ge(prod_ready, base + k + 1)
                            gate = prod[:, u % 2, :]
                        dve.tensor_tensor(hid[:, u % 2, :], pw[:, u % 2, :], gate, ALU.mult).then_inc(hid_ready, 1)

                    blocks(c, dve, visit)

            @block.gpsimd
            def _(pool):
                pool.wait_ge(loaded, NL)
                with pool.Fori(0, NC) as c:
                    pool.wait_ge(fs_ready, c + 1)
                    pool.tensor_tensor(sfs[:, :], at(s, c * CH, CH), fs[:, :], ALU.mult).then_inc(x_steps, 1)
                    pool.wait_ge(x_steps, 2 * c + 1)
                    pool.tensor_tensor(at(x, c * CH, CH), at(x, c * CH, CH), sfs[:, :], ALU.add).then_inc(x_steps, 1)
                    wait_apart(pool, x_steps, 2 * c + 2)
                    if out is not None:
                        pool.dma_start(out[:, bass.ds(c * CH, CH)], at(x, c * CH, CH)).then_inc(written, 16)
                if out is not None:
                    pool.wait_ge(written, 16 * NC)


def angles(nc, io, trig):
    two_pi = 2 * np.pi
    c1 = 6.28125
    c2 = float(np.float32(np.round((two_pi - c1) * 2**21) / 2**21))
    c3 = float(np.float32(two_pi - c1 - c2))
    magic = 1.5 * 2**23
    with stage(nc, "an") as (sb, ps, sem):
        pos = sb("pos", [P, L])
        theta = sb("theta", [P, 2])
        pick = sb("pick", [P, 3])
        ang = sb("ang", [P, 2, L])
        turns = sb("turns", [P, 2, L])
        loaded, steps, mag_ready, table = sem("loaded"), sem("steps"), sem("mag_ready"), sem("table")
        with nc.Block() as block:
            @block.sync
            def _(sp):
                load(sp, loaded, [(pos[:, :], io["pos"]), (theta[:, :], io["a1_theta"]), (pick[:, :], io["a1_pick"])])
                sp.wait_ge(loaded, 48)

            @block.vector
            def _(dve):
                dve.wait_ge(loaded, 48)
                step = Steps(dve, steps)
                for g in range(2):
                    step(dve.tensor_scalar(ang[:, g, :], pos[:, :], theta[:, g:g + 1], None, ALU.mult))
                step(dve.tensor_scalar(turns[:, :, :], ang[:, :, :], 1 / two_pi, magic, ALU.mult, ALU.add))
                step(dve.tensor_scalar(turns[:, :, :], turns[:, :, :], -magic, None, ALU.add))
                for c in (c1, c2, c3):
                    step(dve.scalar_tensor_tensor(out=ang[:, :, :], in0=turns[:, :, :], scalar=-c, in1=ang[:, :, :],
                                                  op0=ALU.mult, op1=ALU.add))
                step(dve.tensor_scalar(ang[:, :, :], ang[:, :, :], 3.1415925, -3.1415925, ALU.min, ALU.max))
                dve.wait_ge(mag_ready, 1)
                step(dve.tensor_scalar(turns[:, :, :], turns[:, :, :], pick[:, 0:1], None, ALU.mult))
                step(dve.scalar_tensor_tensor(out=turns[:, :, :], in0=ang[:, :, :], scalar=pick[:, 1:2],
                                              in1=turns[:, :, :], op0=ALU.mult, op1=ALU.add))

            @block.scalar
            def _(act):
                act.wait_ge(steps, 8)
                act.activation(turns[:, :, :], ang[:, :, :], ACT.Abs).then_inc(mag_ready, 1)
                act.wait_ge(steps, 10)
                act.activation(trig[:, :, :], turns[:, :, :], ACT.Sin, bias=pick[:, 2:3]).then_inc(table, 1)


def linear_attention(nc, io, xn, s, trig):
    G = 2
    with stage(nc, "l1") as (sb, ps, sem):
        w = sb("w", [P, 2, G, P])
        wv = sb("wv", [P, P])
        pick = sb("pick", [P, NH // G])
        keep = sb("keep", [P, P])
        own = sb("own", [P, G, P])
        xst = sb("xst", [P, L])
        raw = sb("raw", [P, 2, G, L])
        q = sb("q", [P, G, L])
        k = sb("k", [P, G, L])
        q_one = sb("q_one", [P, G, NH // G, L])
        v = sb("v", [P, KT, P])
        v_pad = sb("v_pad", [P, KT, NH, 32])
        kt_sb = sb("kt_sb", [P, G, P])
        pm = sb("pm", [P, 2, 4, 4, P])
        state = sb("state", [P, 2, G, P])
        prod = ps("prod", [P, 4, 4, P])
        acc = ps("acc", [P, 2, CH])
        p_state = ps("p_state", [P, G, P])
        p_turn = ps("p_turn", [P, CH])
        loaded, v_zero, staged = sem("loaded"), sem("v_zero"), sem("staged")
        raw_mm = [sem("raw_mm_q"), sem("raw_mm_k")]
        raw_ready = [sem("raw_ready_q"), sem("raw_ready_k")]
        q_ready, k_ready, one_ready = sem("q_ready"), sem("k_ready"), [sem(f"one_ready{c}") for c in range(2)]
        v_mm, v_ready, pad_ready = sem("v_mm"), sem("v_ready"), sem("pad_ready")
        prod_mm, masked = sem("prod_mm"), sem("masked")
        turn_mm, turned = sem("turn_mm"), sem("turned")
        state_mm, state_ready = sem("state_mm"), sem("state_ready")
        sum_mm, sum_read = sem("sum_mm"), sem("sum_read")
        ident = io["sb_ident"]
        NST = KT - 1
        loads = [(w[:, :, :, :], io["a1_wqk"]), (wv[:, :], io["a1_wv"]), (pick[:, :], io["a1_heads"]),
                 (keep[:, :], io["keep"]), (own[:, :, :], io["a1_own"])]
        NL = 16 * len(loads)
        with nc.Block() as block:
            @block.sync
            def _(sp):
                load(sp, loaded, loads)
                sp.wait_ge(loaded, NL)

            @block.gpsimd
            def _(pool):
                pool.memset(v_pad[:, :, :, :], 0.0).then_inc(v_zero, 1)
                pool.wait_ge(v_zero, 1)
                pool.wait_ge(loaded, NL)
                with pool.Fori(0, B) as b:
                    pool.wait_ge(v_mm, b)
                    pool.tensor_copy(xst[:, :], at(xn, b * L, L)).then_inc(staged, 1)
                    pool.wait_ge(v_ready, b + 1)
                    wait_apart(pool, sum_mm, b * KT)
                    for i in range(4):
                        dst = v_pad[:, :, :, 8 * i:8 * i + 8].rearrange("p t (c i) e -> p t c i e", i=4)[:, :, :, i, :]
                        src = v[:, :, :].rearrange("p t (c i e) -> p t c i e", i=4, e=HD)[:, :, :, i, :]
                        pool.tensor_copy(dst, src).then_inc(pad_ready, 1)
                    wait_apart(pool, q_ready, G * (b + 1))
                    wait_apart(pool, prod_mm, b * 2 * KT)
                    for g in range(G):
                        for h in range(NH // G):
                            pool.tensor_scalar(q_one[:, g, h, CH:L], q[:, g, CH:L], pick[:, h:h + 1], 1.0,
                                               ALU.mult, ALU.mult).then_inc(one_ready[1], 1)

            @block.tensor
            def _(pe):
                pe.wait_ge(loaded, NL)
                with pe.Fori(0, B) as b:
                    for j in range(2):
                        if j == 0:
                            pe.wait_ge(masked, b * 2 * KT)
                        else:
                            pe.wait_ge(raw_ready[0], G * (b + 1))
                        for g in range(G):
                            for c in range(2):
                                bank = prod[:, 2 * g + c, :, :].rearrange("p a t -> p (a t)")
                                mm = pe.matmul(bank, w[:, j, g, :], at(xn, b * L + c * CH, CH), start=True, stop=True)
                            mm.then_inc(raw_mm[j], 1)
                    pe.wait_ge(staged, b + 1)
                    pe.wait_ge(sum_read, 2 * b)
                    for t in range(KT):
                        mm = pe.matmul(acc[:, t // 4, (t % 4) * P:(t % 4 + 1) * P], xst[:, t * P:(t + 1) * P], wv[:, :],
                                       start=True, stop=True)
                    mm.then_inc(v_mm, 1)

                    def add_up(t):
                        out = acc[:, t // 4, (t % 4) * P:(t % 4 + 1) * P]
                        if t > 0:
                            pe.wait_ge(state_ready, b * NST + t)
                            if t == 1:
                                pe.wait_ge(q_ready, G * (b + 1))
                            for g in range(G):
                                pe.matmul(out, state[:, t % 2, g, :], q[:, g, t * P:(t + 1) * P],
                                          start=(g == 0), stop=True, skip_group_check=True)
                        else:
                            pe.wait_ge(pad_ready, 4 * (b + 1))
                            pe.wait_ge(v_ready, b + 1)
                        pe.wait_ge(masked, (b * KT + t + 1) * 2)
                        for i in range(4):
                            for c in range(4):
                                h = 4 * c + i
                                mm = pe.matmul(acc[32 * c:32 * c + 32, t // 4, (t % 4) * P:(t % 4 + 1) * P],
                                               v_pad[:, t, h, :], pm[:, t % 2, c, i, :],
                                               start=(t == 0 and i == 0), stop=True, skip_group_check=True)
                        mm.then_inc(sum_mm, 1)

                    for t in range(KT):
                        for g in range(G):
                            if t == 0:
                                pe.wait_ge(raw_ready[1], G * (b + 1))
                                pe.wait_ge(k_ready, G * (b + 1))
                            else:
                                pe.wait_ge(masked, (b * KT + t - 1) * 2 + g + 1)
                            if t % 4 == 0:
                                pe.wait_ge(one_ready[t // 4], NH * b + NH // G * (g + 1))
                            for m in range(2):
                                mm = pe.matmul(prod[:, 2 * g + m, :, :], k[:, g, t * P:(t + 1) * P],
                                               q_one[:, g, 4 * m:4 * m + 4, t * P:(t + 1) * P], start=True, stop=True)
                            mm.then_inc(prod_mm, 1)
                        if t < NST:
                            pe.wait_ge(turned, b * NST + t)
                            for g in range(G):
                                mm = pe.matmul(p_turn[:, g * P:(g + 1) * P], k[:, g, t * P:(t + 1) * P], ident[:, :],
                                               start=True, stop=True)
                            mm.then_inc(turn_mm, 1)
                        if t > 0:
                            add_up(t - 1)
                        if t < NST:
                            pe.wait_ge(turned, b * NST + t + 1)
                            pe.wait_ge(state_ready, b * NST + t)
                            if t == 0:
                                pe.wait_ge(v_ready, b + 1)
                            for g in range(G):
                                mm = pe.matmul(p_state[:, g, :], kt_sb[:, g, :], v[:, t, :],
                                               start=(t == 0 and g == 0), stop=True, skip_group_check=True)
                            mm.then_inc(state_mm, 1)
                    add_up(KT - 1)

            @block.scalar
            def _(act):
                act.wait_ge(loaded, NL)
                with act.Fori(0, B) as b:
                    for j in range(2):
                        for g in range(G):
                            act.wait_ge(raw_mm[j], b * G + g + 1)
                            act.wait_ge((q_ready, k_ready)[j], b * G)
                            act.activation(raw[:, j, g, :], prod[:, 2 * g:2 * g + 2, :, :].rearrange("p c a t -> p (c a t)"),
                                           ACT.Silu).then_inc(raw_ready[j], 1)
                    for g in range(G):
                        act.wait_ge(q_ready, b * G + g + 1)
                        act.wait_ge(prod_mm, b * 2 * KT)
                        for h in range(NH // G):
                            act.activation(q_one[:, g, h, 0:CH], q[:, g, 0:CH], ACT.Copy, scale=pick[:, h:h + 1]
                                           ).then_inc(one_ready[0], 1)
                    act.wait_ge(v_mm, b + 1)
                    act.wait_ge(state_mm, b * NST)
                    act.wait_ge(pad_ready, 4 * b)
                    act.activation(v[:, :, :].rearrange("p t e -> p (t e)"), acc[:, :, :].rearrange("p c t -> p (c t)"),
                                   ACT.Copy).then_inc(v_ready, 1)
                    def read_sums(half):
                        act.wait_ge(sum_mm, b * KT + 4 * (half + 1))
                        act.activation(at(s, b * L + half * CH, CH), acc[:, half, :], ACT.Copy).then_inc(sum_read, 1)

                    for t in range(NST):
                        act.wait_ge(turn_mm, b * NST + t + 1)
                        act.wait_ge(state_mm, b * NST + t)
                        act.activation(kt_sb[:, :, :].rearrange("p g t -> p (g t)"), p_turn[:, 0:G * P],
                                       ACT.Copy).then_inc(turned, 1)
                        if t == 5:
                            read_sums(0)
                    read_sums(1)

            @block.vector
            def _(dve):
                dve.wait_ge(loaded, NL)
                with dve.Fori(0, B) as b:
                    for j, (dst, ready) in enumerate(((q, q_ready), (k, k_ready))):
                        for g in range(G):
                            dve.wait_ge(raw_ready[j], b * G + g + 1)
                            dve.wait_ge(sum_mm, b * KT)
                            dve.tensor_tensor(dst[:, g, :], raw[:, j, g, :], trig[:, g, :], ALU.mult).then_inc(ready, 1)
                    for t in range(KT):
                        for half in range(2):
                            dve.wait_ge(prod_mm, (b * KT + t) * 2 + half + 1)
                            if t > 1:
                                dve.wait_ge(sum_mm, b * KT + t - 1)
                            banks = slice(2 * half, 2 * half + 2)
                            dve.tensor_tensor(pm[:, t % 2, banks, :, :].rearrange("p r a t -> p (r a) t"),
                                              prod[:, banks, :, :].rearrange("p r a t -> p (r a) t"),
                                              keep[:, :].unsqueeze(1).to_broadcast([P, 8, P]), ALU.mult).then_inc(masked, 1)
                        if t < NST:
                            dve.wait_ge(state_mm, b * NST + t + 1)
                            dve.tensor_tensor(state[:, (t + 1) % 2, :, :], p_state[:, :, :], own[:, :, :],
                                              ALU.mult).then_inc(state_ready, 1)


def project_plain(nc, io, xn, feat, v):
    with stage(nc, "p2") as (sb, ps, sem):
        w = sb("w", [P, 4, P])
        xd = sb("xd", [P, L])
        pd = ps("pd", [P, L])
        pq = ps("pq", [P, 2, L])
        pv = ps("pv", [P, L])
        loaded, d_mm, qk_mm, v_mm = sem("loaded"), sem("d_mm"), sem("qk_mm"), sem("v_mm")
        d_ready, qk_ready, v_ready = sem("d_ready"), sem("qk_ready"), sem("v_ready")
        with nc.Block() as block:
            @block.sync
            def _(sp):
                load(sp, loaded, [(w[:, :, :], io["a2_w"])])
                sp.wait_ge(loaded, 16)

            @block.tensor
            def _(pe):
                pe.wait_ge(loaded, 16)
                with pe.Fori(0, B) as b:
                    for c in range(2):
                        mm = pe.matmul(pd[:, c * CH:(c + 1) * CH], w[:, 0, :], at(xn, b * L + c * CH, CH),
                                       start=True, stop=True)
                    mm.then_inc(d_mm, 1)
                    pe.wait_ge(d_ready, b + 1)
                    for j in range(2):
                        pe.wait_ge(qk_ready, 2 * b)
                        for c in range(2):
                            mm = pe.matmul(pq[:, j, c * CH:(c + 1) * CH], w[:, 1 + j, :], xd[:, c * CH:(c + 1) * CH],
                                           start=True, stop=True)
                        mm.then_inc(qk_mm, 1)
                    pe.wait_ge(v_ready, b)
                    for t in range(KT):
                        mm = pe.matmul(pv[:, t * P:(t + 1) * P], xd[:, t * P:(t + 1) * P], w[:, 3, :],
                                       start=True, stop=True)
                    mm.then_inc(v_mm, 1)

            @block.scalar
            def _(act):
                with act.Fori(0, B) as b:
                    act.wait_ge(d_mm, b + 1)
                    act.wait_ge(v_mm, b)
                    act.activation(xd[:, :], pd[:, :], ACT.Copy).then_inc(d_ready, 1)
                    for j in range(2):
                        act.wait_ge(qk_mm, 2 * b + j + 1)
                        act.activation(at(feat, (j * B + b) * L, L), pq[:, j, :], ACT.Copy,
                                       scale=float(HD) ** -0.25).then_inc(qk_ready, 1)

            @block.vector
            def _(dve):
                with dve.Fori(0, B) as b:
                    dve.wait_ge(v_mm, b + 1)
                    dve.tensor_copy(at(v, b * L, L), pv[:, :]).then_inc(v_ready, 1)


def project_rotary(nc, io, xn, feat, v):
    DC = 32
    with stage(nc, "p3") as (sb, ps, sem):
        w = sb("w", [P, 4, P])
        bias = sb("bias", [P, 4])
        wkv = sb("wkv", [P, DC])
        bkv = sb("bkv", [DC, 1])
        wv = sb("wv", [DC + 1, P])
        trig = sb("trig", [P, 2, L])
        ckv = sb("ckv", [DC + 1, L])
        rot = sb("rot", [P, 4, L])
        pre = sb("pre", [P, 2, L])
        pw = ps("pw", [P, 4, L])
        loaded, one_set, w_mm, c_mm, v_mm = sem("loaded"), sem("one_set"), sem("w_mm"), sem("c_mm"), sem("v_mm")
        rot_ready, pre_ready, feat_ready = sem("rot_ready"), sem("pre_ready"), sem("feat_ready")
        ckv_ready, v_ready = sem("ckv_ready"), sem("v_ready")
        with nc.Block() as block:
            @block.sync
            def _(sp):
                load(sp, loaded, [(w[:, :, :], io["a3_w"]), (bias[:, :], io["a3_b"]), (wkv[:, :], io["a3_wkv"]),
                                  (bkv[:, :], io["a3_bkv"]), (wv[:, :], io["a3_wv"]), (trig[:, :, :], io["trig"])])
                sp.wait_ge(loaded, 96)

            @block.tensor
            def _(pe):
                pe.wait_ge(loaded, 96)
                with pe.Fori(0, B) as b:
                    for j in range(4):
                        pe.wait_ge(rot_ready, 4 * b)
                        if j == 0:
                            pe.wait_ge(ckv_ready, b)
                        if j == 1:
                            pe.wait_ge(v_ready, b)
                        for c in range(2):
                            mm = pe.matmul(pw[:, j, c * CH:(c + 1) * CH], w[:, j, :], at(xn, b * L + c * CH, CH),
                                           start=True, stop=True)
                        mm.then_inc(w_mm, 1)
                    wait_apart(pe, rot_ready, 4 * b + 1)
                    for c in range(2):
                        mm = pe.matmul(pw[0:DC, 0, c * CH:(c + 1) * CH], wkv[:, :], at(xn, b * L + c * CH, CH),
                                       start=True, stop=True)
                    mm.then_inc(c_mm, 1)
                    pe.wait_ge(ckv_ready, b + 1)
                    pe.wait_ge(rot_ready, 4 * b + 2)
                    pe.wait_ge(one_set, 1)
                    for t in range(KT):
                        mm = pe.matmul(pw[:, 1, t * P:(t + 1) * P], ckv[:, t * P:(t + 1) * P], wv[:, :],
                                       start=True, stop=True)
                    mm.then_inc(v_mm, 1)

            @block.scalar
            def _(act):
                act.wait_ge(loaded, 96)
                with act.Fori(0, B) as b:
                    act.wait_ge(c_mm, b + 1)
                    act.wait_ge(v_mm, b)
                    act.activation(ckv[0:DC, :], pw[0:DC, 0, :], ACT.Gelu, bias=bkv[:, 0:1]).then_inc(ckv_ready, 1)
                    for j in range(2):
                        act.wait_ge(pre_ready, 2 * b + j + 1)
                        act.activation(at(feat, (j * B + b) * L, L), pre[:, j, :], ACT.Gelu).then_inc(feat_ready, 1)

            @block.vector
            def _(dve):
                dve.memset(ckv[DC:DC + 1, :], 1.0).then_inc(one_set, 1)
                dve.wait_ge(loaded, 96)
                with dve.Fori(0, B) as b:
                    for j in range(4):
                        dve.wait_ge(w_mm, 4 * b + j + 1)
                        dve.wait_ge(pre_ready, 2 * b)
                        dve.scalar_tensor_tensor(out=rot[:, j, :], in0=pw[:, j, :], scalar=bias[:, j:j + 1],
                                                 in1=trig[:, j % 2, :], op0=ALU.add, op1=ALU.mult).then_inc(rot_ready, 1)
                    dve.wait_ge(v_mm, b + 1)
                    dve.tensor_copy(at(v, b * L, L), pw[:, 1, :]).then_inc(v_ready, 1)

            @block.gpsimd
            def _(pool):
                with pool.Fori(0, B) as b:
                    for j in range(2):
                        pool.wait_ge(rot_ready, 4 * b + 2 * j + 2)
                        pool.wait_ge(feat_ready, 2 * b)
                        pool.tensor_tensor(pre[:, j, :], rot[:, 2 * j, :], rot[:, 2 * j + 1, :],
                                           ALU.add).then_inc(pre_ready, 1)


def split_store(nc, tag, feat, items, scratch):
    with stage(nc, "s" + tag) as (sb, ps, sem):
        parts = sb("parts", [P, 2, NPART, L], BF16)
        rest = sb("rest", [P, 2, L])
        hi = [sem(f"hi{u}") for u in range(2)]
        rest_ready = [sem(f"rest_ready{u}") for u in range(2)]
        mid = [sem(f"mid{u}") for u in range(2)]
        lo = [sem(f"lo{u}") for u in range(2)]
        stored = [sem(f"stored{u}") for u in range(2)]
        n = items // 2
        with nc.Block() as block:
            @block.sync
            def _(sp):
                with sp.Fori(0, n) as i:
                    for u in range(2):
                        sp.wait_ge(lo[u], i + 1)
                        for a in range(NPART):
                            dst = bass.AP(scratch.tensor, ((i * 2 + u) * NH * NPART + a) * HD * L,
                                          [[NPART * HD * L, NH], [L, HD], [1, L]])
                            sp.dma_start(dst, parts[:, u, a, :]).then_inc(stored[u], 16)
                for u in range(2):
                    sp.wait_ge(stored[u], 16 * NPART * n)

            @block.scalar
            def _(act):
                with act.Fori(0, n) as i:
                    for u in range(2):
                        act.wait_ge(stored[u], 16 * NPART * i)
                        act.activation(parts[:, u, 0, :], at(feat, (i * 2 + u) * L, L), ACT.Copy).then_inc(hi[u], 1)
                    for u in range(2):
                        act.wait_ge(rest_ready[u], i + 1)
                        act.activation(parts[:, u, 1, :], rest[:, u, :], ACT.Copy).then_inc(mid[u], 1)

            @block.vector
            def _(dve):
                with dve.Fori(0, n) as i:
                    for u in range(2):
                        dve.wait_ge(hi[u], i + 1)
                        dve.wait_ge(lo[u], i)
                        dve.tensor_tensor(rest[:, u, :], at(feat, (i * 2 + u) * L, L), parts[:, u, 0, :],
                                          ALU.subtract).then_inc(rest_ready[u], 1)
                    for u in range(2):
                        dve.wait_ge(mid[u], i + 1)
                        dve.wait_ge(rest_ready[u], i + 1)
                        dve.tensor_tensor(parts[:, u, 2, :], rest[:, u, :], parts[:, u, 1, :],
                                          ALU.subtract).then_inc(lo[u], 1)


def pass_plan(groups, width, uses, use_cost):
    NU = len(uses)
    total_use, total = sum(use_cost), sum(width) * GH
    plan, done, m, cost = [], 0, 0, 0
    for g in range(len(groups)):
        for hh in range(GH):
            plan.append(("score", g, hh))
            done += width[g]
            if hh == 1:
                plan.append(("sum", g - 1, 0))
            while m < NU and (cost + use_cost[m] / 2) * total <= done * total_use:
                plan.append(("use", m, 0))
                cost += use_cost[m]
                m += 1
    return plan + [("use", k, 0) for k in range(m, NU)]


def attend(nc, io, tag, v, scratch, result, causal, scale=1.0):
    MR = NPART
    NG = NH // GH
    NPASS = B * NG
    LOADS = (1 + NPART) * GH * 16
    tiles = []
    for qt in range(KT):
        for half in range(2):
            end = min((half + 1) * CH, (qt + 1) * P if causal else L)
            if end > half * CH:
                tiles.append((qt, half, half * CH, end))
    LEAD = len(tiles)
    uses = []
    for hh in (1, 2, 3, 0):
        for n, tile in enumerate(tiles):
            if n == 4:
                uses.append(("turn", (hh - 1) % GH, None))
            uses.append(("tile", hh, tile))
    NU = len(uses)
    NSE, NSC = 4, 2
    assert NU % NSE == 0 and LEAD % NSE == 0
    use_cost = [60 + (t[3] - t[2] if what == "tile" else P) for what, _, t in uses]
    last_tile = {hh: max(m for m, x in enumerate(uses) if x[0] == "tile" and x[1] == hh) for hh in range(GH)}
    turn_at = {x[1]: m for m, x in enumerate(uses) if x[0] == "turn"}
    groups = []
    for kt in range(KT):
        for c in range(2):
            lo = max(kt * P if causal else 0, c * CH)
            if lo < (c + 1) * CH:
                groups.append((kt, c, lo, (c + 1) * CH))
    NGR = len(groups)
    NS1 = NGR * GH
    assert NS1 % NSC == 0
    before = [max(n for n in range(g + NGR) if groups[n % NGR][0] % 2 == kt % 2 and groups[n % NGR][1] == c)
              for g, (kt, c, _, _) in enumerate(groups)]
    final = {c: max(g for g in range(NGR) if groups[g][1] == c) for c in range(2)}
    plan = pass_plan(groups, [hi - lo + 100 for _, _, lo, hi in groups], uses, use_cost)

    def searched(grp, m):
        return LEAD + grp * NU + m

    with stage(nc, "a" + tag) as (sb, ps, sem):
        kst = sb("kst", [ROWS + MR, 2, GH, L], BF16)
        qst = sb("qst", [ROWS + MR, 2, GH, L], BF16)
        ksr = sb("ksr", [ROWS, GH, L], BF16)
        qsr = sb("qsr", [ROWS, GH, L], BF16)
        mx = sb("mx", [P, GH, KT, 2])
        mxf = sb("mxf", [P, GH, KT])
        neg = sb("neg", [P, GH, KT])
        nrest = sb("nrest", [P, GH, KT])
        mparts = sb("mparts", [P, GH, NPART, KT], BF16)
        mrow = sb("mrow", [NPART * KT, GH, P], BF16)
        vst = sb("vst", [P, KT, GH, 32])
        prob = sb("prob", [P, 2, GH, L])
        accs = sb("accs", [P, L])
        search = ps("search", [P, NSE, CH])
        score = ps("score", [P, NSC, CH])
        acc = ps("acc", [P, L])
        set_up, mx_set, loaded = sem("set_up"), sem("mx_set"), sem("loaded")
        stacks, ones_in = sem("stacks"), sem("ones_in")
        search_in = [sem(f"search_in{h}") for h in range(GH)]
        search_mm, search_used = sem("search_mm"), sem("search_used")
        max_ready, pool_steps, mparts_ready = sem("max_ready"), sem("pool_steps"), sem("mparts_ready")
        mrow_in = [sem(f"mrow_in{h}") for h in range(GH)]
        v_staged, score_mm, prob_ready = sem("v_staged"), sem("score_mm"), sem("prob_ready")
        av_mm, acc_read, acc_out = sem("av_mm"), sem("acc_read"), sem("acc_out")
        identb = io["sb_identb"]
        consts = []
        if causal:
            mask = sb("mask", [P, 2, P], BF16)
            consts = [(mask[:, :, :], io["mask"])]
        NCST = 16 * len(consts)

        def stack(eng, q_dst, k_dst, it, hh, signal):
            q_at = (it * GH + hh) * (NPART * HD * L)
            k_at = B * NH * NPART * HD * L + q_at
            eng.dma_start(q_dst(0, ROWS), bass.AP(scratch.tensor, q_at, [[0, NPART], [L, NPART * HD], [1, L]])
                          ).then_inc(signal, 16)
            for t in range(NPART):
                eng.dma_start(k_dst(t * NPART * HD, (t + 1) * NPART * HD),
                              bass.AP(scratch.tensor, k_at + t * HD * L, [[0, NPART], [L, HD], [1, L]])
                              ).then_inc(signal, 16)

        with nc.Block() as block:
            @block.sync
            def _(sp):
                def load_stacks(it, par):
                    for hh in range(GH):
                        def into(t):
                            return lambda r0, r1: t[r0:r1, bass.ds(par, 1), hh, :].rearrange("r o t -> r (o t)")

                        stack(sp, into(qst), into(kst), it, hh, stacks)

                def load_search(grp, hh):
                    stack(sp, lambda r0, r1: qsr[r0:r1, hh, :], lambda r0, r1: ksr[r0:r1, hh, :], grp, hh,
                          search_in[hh])

                def store(it):
                    sp.wait_ge(acc_read, it + 1)
                    for hh in range(GH):
                        for nd in range(2):
                            dst = bass.AP(result.tensor, ((nd * P + ((it % NG) * GH + hh) * HD) * B + it // NG) * L,
                                          [[B * L, HD], [1, L]])
                            sp.dma_start(dst, accs[32 * hh + HD * nd:32 * hh + HD * nd + HD, :]).then_inc(acc_out, 16)

                for hh in range(GH):
                    load_search(0, hh)
                load(sp, loaded, consts)
                for par in range(2):
                    sp.dma_start(kst[ROWS:ROWS + MR, par, :, :], io["ones_rows"]).then_inc(ones_in, 16)
                load_stacks(0, 0)
                sp.wait_ge(search_mm, LEAD)
                load_search(1, 0)

                def next_search(it, hh):
                    sp.wait_ge(search_mm, searched(it, last_tile[hh] + 1))
                    load_search(it + (2 if hh == 0 else 1), hh)

                for hh in range(1, GH):
                    next_search(0, hh)

                def body(it, search=True):
                    if search:
                        next_search(it, 0)
                    if not isinstance(it, int) or it > 0:
                        wait_apart(sp, score_mm, it * NS1)
                    sp.wait_ge(stacks, LOADS * (it + 1))
                    load_stacks(it + 1, (it + 1) % 2)
                    if not isinstance(it, int) or it > 0:
                        store(it - 1)
                    for hh in range(1, GH if search else 1):
                        next_search(it + 1, hh)

                body(0)
                with sp.Fori(1, NPASS - 2) as it:
                    body(it)
                body(NPASS - 2, search=False)
                store(NPASS - 2)
                store(NPASS - 1)
                sp.wait_ge(acc_out, NPASS * GH * 2 * 16)
                if NCST:
                    sp.wait_ge(loaded, NCST)

            @block.gpsimd
            def _(pool):
                pool.memset(vst[:, :, :, HD:32], 0.0).then_inc(set_up, 1)
                pool.wait_ge(set_up, 1)
                pool.memset(vst[:, :, :, HD:2 * HD], 1.0).then_inc(set_up, 1)
                pool.wait_ge(set_up, 2)

                def stage_values(it):
                    if not isinstance(it, int) or it > 0:
                        pool.wait_ge(av_mm, it * NGR)
                    src = v[:, bass.ds((it // NG) * L, L)].rearrange("p (k f) -> p k f", f=P)
                    src = src[:, :, bass.ds((it % NG) * GH * HD, GH * HD)].rearrange("p k (h e) -> p k h e", e=HD)
                    pool.tensor_copy(vst[:, :, :, 0:HD], src).then_inc(v_staged, 1)

                def split_maxima(grp, hh):
                    step = Steps(pool, pool_steps, (grp * GH + hh) * 4)
                    wait_apart(pool, max_ready, grp * GH + hh + 1)
                    step(pool.tensor_scalar(neg[:, hh, :], mxf[:, hh, :], -1.0, None, ALU.mult), apart=True)
                    step(pool.tensor_copy(mparts[:, hh, 0, :], neg[:, hh, :]))
                    step(pool.tensor_tensor(nrest[:, hh, :], neg[:, hh, :], mparts[:, hh, 0, :], ALU.subtract),
                         apart=True)
                    step(pool.tensor_copy(mparts[:, hh, 1, :], nrest[:, hh, :]))
                    pool.tensor_tensor(mparts[:, hh, 2, :], nrest[:, hh, :], mparts[:, hh, 1, :],
                                       ALU.subtract).then_inc(mparts_ready, 1)

                def move_maxima(grp, hh):
                    pool.wait_ge(search_used, searched(grp, turn_at[hh] + 1))
                    if hh == 0 and (not isinstance(grp, int) or grp > 1):
                        pool.wait_ge(score_mm, (grp - 1) * NS1)
                    rows = qst[ROWS:ROWS + MR, bass.ds(grp % 2, 1), hh, :].rearrange("r o (k q) -> r (o k) q", q=P)
                    pool.dma_start(rows, mrow[:, hh, :]).then_inc(mrow_in[hh], 16)

                def maxima(grp, heads):
                    for hh in heads:
                        split_maxima(grp, hh)
                        move_maxima(grp, hh)

                maxima(0, range(GH))
                stage_values(0)
                maxima(1, range(GH))
                with pool.Fori(1, NPASS - 1) as it:
                    split_maxima(it + 1, 0)
                    stage_values(it)
                    move_maxima(it + 1, 0)
                    maxima(it + 1, range(1, GH))
                stage_values(NPASS - 1)

            @block.tensor
            def _(pe):
                def use(grp, m):
                    first_head = isinstance(grp, int) and grp < 0
                    what, hh, tile = ("tile", 0, tiles[m]) if first_head else uses[m]
                    n = m if first_head else searched(grp, m)
                    if not isinstance(n, int) or n >= NSE:
                        pe.wait_ge(search_used, n - NSE + 1)
                    slot = search[:, m % NSE, :]
                    if what == "turn":
                        pe.wait_ge(mparts_ready, grp * GH + hh + 1)
                        out = slot.bitcast(BF16)[0:NPART * KT, 0:P]
                        pe.transpose(out, mparts[:, hh, :, :].rearrange("p a k -> p (a k)"), identb[:, :]
                                     ).then_inc(search_mm, 1)
                        return
                    qt, half, k0, k1 = tile
                    loads = grp + (2 if hh == 0 else 1)
                    pe.wait_ge(search_in[hh], (1 + NPART) * 16 * (min(loads, NPASS) if isinstance(loads, int) else loads))
                    diag = causal and k0 <= qt * P < k1
                    mm = pe.matmul(slot[:, 0:k1 - k0], qsr[:, hh, qt * P:(qt + 1) * P], ksr[:, hh, k0:k1],
                                   start=True, stop=True)
                    if diag:
                        mm = pe.matmul(slot[:, qt * P - k0:qt * P - k0 + P], identb[:, :], mask[:, 0, :],
                                       start=False, stop=True, skip_group_check=True)
                    mm.then_inc(search_mm, 1)

                def add_up(it, g):
                    kt, c, lo, hi = groups[g]
                    pe.wait_ge(prob_ready, it * NS1 + (g + 1) * GH)
                    if g == 0:
                        pe.wait_ge(v_staged, it + 1)
                        if not isinstance(it, int) or it > 0:
                            pe.wait_ge(acc_read, it)
                    for hh in range(GH):
                        mm = pe.matmul(acc[32 * hh:32 * hh + 32, lo:hi], vst[:, kt, hh, :], prob[:, kt % 2, hh, lo:hi],
                                       start=(kt == 0), stop=(g == final[c]), skip_group_check=True)
                    mm.then_inc(av_mm, 1)

                def scores(it, par, g, hh):
                    kt, c, lo, hi = groups[g]
                    n = g * GH + hh
                    if n == 0:
                        pe.wait_ge(stacks, LOADS * (it + 1))
                    if g == 0:
                        pe.wait_ge(mrow_in[hh], 16 * (it + 1))
                    if not isinstance(it, int) or it * NS1 + n >= NSC:
                        pe.wait_ge(prob_ready, it * NS1 + n - NSC + 1)
                    slot = score[:, n % NSC, :]
                    mm = pe.matmul(slot[:, 0:hi - lo],
                                   kst[:, bass.ds(par, 1), hh, kt * P:(kt + 1) * P].rearrange("r o t -> r (o t)"),
                                   qst[:, bass.ds(par, 1), hh, lo:hi].rearrange("r o t -> r (o t)"),
                                   start=True, stop=True)
                    if causal and lo == kt * P:
                        mm = pe.matmul(slot[:, 0:P], identb[:, :], mask[:, 1, :],
                                       start=False, stop=True, skip_group_check=True)
                    mm.then_inc(score_mm, 1)

                def one_pass(it, par, carry=True, searches=NU):
                    for what, a, hh in plan:
                        if what == "score":
                            scores(it, par, a, hh)
                        elif what == "use":
                            if a < searches:
                                use(it + 1, a)
                        elif a >= 0:
                            add_up(it, a)
                        elif carry:
                            add_up(it - 1, NGR - 1)

                if NCST:
                    pe.wait_ge(loaded, NCST)
                for m in range(LEAD):
                    use(-1, m)
                for m in range(NU):
                    use(0, m)
                pe.wait_ge(ones_in, 32)
                one_pass(0, 0, carry=False)
                with pe.Fori(1, NPASS - 2) as it:
                    one_pass(it, it % 2)
                one_pass(NPASS - 2, 0, searches=turn_at[3] + 1)
                one_pass(NPASS - 1, 1, searches=0)
                add_up(NPASS - 1, NGR - 1)

            @block.scalar
            def _(act):
                def read_sums(it):
                    act.wait_ge(av_mm, (it + 1) * NGR)
                    if not isinstance(it, int) or it > 0:
                        act.wait_ge(acc_out, it * GH * 2 * 16)
                    act.activation(accs[:, :], acc[:, :], ACT.Copy).then_inc(acc_read, 1)

                def exponentials(it, g):
                    kt, c, lo, hi = groups[g]
                    if not isinstance(it, int) or (it - 1) * NGR + before[g] >= 0:
                        act.wait_ge(av_mm, (it - 1) * NGR + before[g] + 1)
                    for hh in range(GH):
                        n = g * GH + hh
                        act.wait_ge(score_mm, it * NS1 + n + 1)
                        act.activation(prob[:, kt % 2, hh, lo:hi], score[:, n % NSC, 0:hi - lo], ACT.Exp,
                                       scale=scale).then_inc(prob_ready, 1)

                for g in range(NGR):
                    exponentials(0, g)
                with act.Fori(1, NPASS) as it:
                    exponentials(it, 0)
                    read_sums(it - 1)
                    for g in range(1, NGR):
                        exponentials(it, g)
                read_sums(NPASS - 1)

            @block.vector
            def _(dve):
                dve.memset(mx[:, :, :, :], -3e38).then_inc(mx_set, 1)
                dve.wait_ge(mx_set, 1)

                def consume(grp, m):
                    first_head = isinstance(grp, int) and grp < 0
                    what, hh, tile = ("tile", 0, tiles[m]) if first_head else uses[m]
                    group = grp + 1 if hh == 0 and what == "tile" else grp
                    done = m + 1 if first_head else searched(grp, m + 1)
                    dve.wait_ge(search_mm, done)
                    slot = search[:, m % NSE, :]
                    if what == "turn":
                        if not isinstance(grp, int) or grp > 0:
                            dve.wait_ge(mrow_in[hh], 16 * grp)
                        dve.tensor_copy(mrow[:, hh, :], slot.bitcast(BF16)[0:NPART * KT, 0:P]
                                        ).then_inc(search_used, 1)
                        return
                    qt, half, k0, k1 = tile
                    if (qt, half) == (0, 0) and (not isinstance(group, int) or group > 0):
                        dve.wait_ge(max_ready, (group - 1) * GH + hh + 1)
                    dve.tensor_reduce(mx[:, hh, qt, half:half + 1], slot[:, 0:k1 - k0], AX.X,
                                      ALU.max).then_inc(search_used, 1)
                    if tile == tiles[-1]:
                        dve.wait_ge(search_used, done)
                        if not isinstance(group, int) or group > 0:
                            dve.wait_ge(mparts_ready, (group - 1) * GH + hh + 1)
                        dve.tensor_reduce(mxf[:, hh, :], mx[:, hh, :, :], AX.X, ALU.max).then_inc(max_ready, 1)

                for m in range(LEAD):
                    consume(-1, m)
                for m in range(NU):
                    consume(0, m)
                with dve.Fori(1, NPASS - 1) as grp:
                    for m in range(NU):
                        consume(grp, m)
                for m in range(turn_at[3] + 1):
                    consume(NPASS - 1, m)


def attention_out(nc, io, tag, result, s, softmax, xn=None):
    with stage(nc, "o" + tag) as (sb, ps, sem):
        w = sb("w", [P, P])
        bias = sb("bias", [P, 1])
        g1 = sb("g1", [P, HD])
        g2 = sb("g2", [HD, P])
        num = sb("num", [P, 2, L])
        den = sb("den", [P, 2, L])
        rec = sb("rec", [P, 2, L])
        ratio = sb("ratio", [P, 2, L])
        lowr = sb("lowr", [HD, L])
        gate = sb("gate", [P, L])
        po = ps("po", [P, 2, L])
        pl = ps("pl", [P, L])
        pgt = ps("pgt", [P, L])
        loaded = sem("loaded")
        fetched = [sem(f"fetched{u}") for u in range(2)]
        rec_ready = [sem(f"rec_ready{u}") for u in range(2)]
        ratio_ready = [sem(f"ratio_ready{u}") for u in range(2)]
        out_mm = [sem(f"out_mm{u}") for u in range(2)]
        s_ready = [sem(f"s_ready{u}") for u in range(2)]
        low_mm, low_ready, gate_mm, gate_ready = sem("low_mm"), sem("low_ready"), sem("gate_mm"), sem("gate_ready")
        loads = [(w[:, :], io[f"o{tag}_w"])]
        loads += [(bias[:, :], io[f"o{tag}_b"])] if softmax else [(g1[:, :], io["a1_g1"]), (g2[:, :], io["a1_g2"])]
        NL = 16 * len(loads)
        with nc.Block() as block:
            @block.sync
            def _(sp):
                load(sp, loaded, loads)
                if softmax:
                    with sp.Fori(0, B // 2) as i:
                        for u in range(2):
                            sp.wait_ge(out_mm[u], i)
                            for nd, t in ((0, num), (1, den)):
                                sp.dma_start(t[:, u, :], result[nd, :, bass.ds(i * 2 + u, 1), :].rearrange("f o t -> f (o t)")
                                             ).then_inc(fetched[u], 16)
                sp.wait_ge(loaded, NL)

            @block.tensor
            def _(pe):
                pe.wait_ge(loaded, NL)
                with pe.Fori(0, B // 2) as i:
                    for u in range(2):
                        b = i * 2 + u
                        if softmax:
                            pe.wait_ge(ratio_ready[u], i + 1)
                        pe.wait_ge(s_ready[u], i)
                        for c in range(2):
                            rhs = ratio[:, u, c * CH:(c + 1) * CH] if softmax else at(s, b * L + c * CH, CH)
                            mm = pe.matmul(po[:, u, c * CH:(c + 1) * CH], w[:, :], rhs, start=True, stop=True)
                        mm.then_inc(out_mm[u], 1)
                        if not softmax:
                            pe.wait_ge(low_ready, b)
                            for c in range(2):
                                mm = pe.matmul(pl[0:HD, c * CH:(c + 1) * CH], g1[:, :], at(xn, b * L + c * CH, CH),
                                               start=True, stop=True)
                            mm.then_inc(low_mm, 1)
                            pe.wait_ge(low_ready, b + 1)
                            pe.wait_ge(gate_ready, b)
                            for c in range(2):
                                mm = pe.matmul(pgt[:, c * CH:(c + 1) * CH], g2[:, :], lowr[:, c * CH:(c + 1) * CH],
                                               start=True, stop=True)
                            mm.then_inc(gate_mm, 1)

            @block.scalar
            def _(act):
                act.wait_ge(loaded, NL)
                with act.Fori(0, B // 2) as i:
                    for u in range(2):
                        b = i * 2 + u
                        if softmax:
                            act.wait_ge(out_mm[u], i + 1)
                            act.activation(at(s, b * L, L), po[:, u, :], ACT.Identity,
                                           bias=bias[:, 0:1]).then_inc(s_ready[u], 1)
                        else:
                            act.wait_ge(low_mm, b + 1)
                            act.wait_ge(gate_mm, b)
                            act.activation(lowr[:, :], pl[0:HD, :], ACT.Copy).then_inc(low_ready, 1)
                            act.wait_ge(gate_mm, b + 1)
                            act.wait_ge(s_ready[1 - u], i + u)
                            act.activation(gate[:, :], pgt[:, :], ACT.Sigmoid).then_inc(gate_ready, 1)

            @block.vector
            def _(dve):
                with dve.Fori(0, B // 2) as i:
                    for u in range(2):
                        b = i * 2 + u
                        if softmax:
                            dve.wait_ge(fetched[u], 32 * (i + 1))
                            dve.wait_ge(ratio_ready[u], i)
                            dve.reciprocal(rec[:, u, :], den[:, u, :]).then_inc(rec_ready[u], 1)
                            dve.wait_ge(rec_ready[u], i + 1)
                            dve.wait_ge(out_mm[u], i)
                            dve.tensor_tensor(ratio[:, u, :], num[:, u, :], rec[:, u, :], ALU.mult).then_inc(ratio_ready[u], 1)
                        else:
                            dve.wait_ge(out_mm[u], i + 1)
                            dve.wait_ge(gate_ready, b + 1)
                            dve.tensor_tensor(at(s, b * L, L), po[:, u, :], gate[:, :], ALU.mult).then_inc(s_ready[u], 1)


def program(nc, io):
    with ExitStack() as ctx:
        def sb(n, shape, dt=F32):
            return ctx.enter_context(nc.sbuf_tensor(n, shape, dt))

        xn = sb("xn", [P, T])
        s = sb("s", [P, T])
        average = sb("average", [P, P])
        ident = sb("ident", [P, P])
        identb = sb("identb", [P, P], BF16)
        consts = [(average[:, :], io["average"]), (ident[:, :], io["ident"]), (identb[:, :], io["identb"])]
        io["sb_ident"], io["sb_identb"] = ident, identb
        with ExitStack() as early:
            x0 = early.enter_context(nc.sbuf_tensor("x0", [P, T], F32))
            normalise(nc, "n0", x0, xn, average, True, first_load=consts + [
                (x0[:, b * L:(b + 1) * L], io["x"][:, b * L:(b + 1) * L]) for b in range(B)])
        with ExitStack() as mamba:
            def msb(n, shape, dt=F32):
                return mamba.enter_context(nc.sbuf_tensor(n, shape, dt))

            norm_w = msb("norm_w", [P, 1])
            gate = msb("gate", [P, 2 * T])
            xs = msb("xs", [P, 2 * T])
            normalise(nc, "n0r", xn, s, average, False, weight=norm_w, first_load=[(norm_w[:, :], io["m_nw"])])
            mamba_inputs(nc, io, s, gate, xs, None)
            delta = msb("delta", [P, 2 * T])
            parts_b = msb("parts_b", [NPART * SP, T], BF16)
            parts_c = msb("parts_c", [NPART * SP, T], BF16)
            mamba_steps(nc, io, xs, delta, parts_b, parts_c)
            mamba_scan(nc, io, xs, gate, delta, parts_b, parts_c, ident)
            mamba_out(nc, io, xs, xn, s)
        x = sb("x", [P, T])
        with ExitStack() as ffn:
            comb = ffn.enter_context(nc.sbuf_tensor("comb0", [49, 1, T], BF16))
            route(nc, io, "0", xn, comb, 16, 16, 4, "grouped_low")
            experts_sum(nc, io, "0", xn, s, x, comb, 49, 0, 0, 6, True, first_load=[(x[:, :], io["x"])])

        normalise(nc, "n1", x, xn, average, True)
        with ExitStack() as mix:
            with ExitStack() as project:
                trig = project.enter_context(nc.sbuf_tensor("trig1", [P, 2, L], F32))
                angles(nc, io, trig)
                linear_attention(nc, io, xn, s, trig)
            attention_out(nc, io, "1", None, s, False, xn=xn)
            gamma = mix.enter_context(nc.sbuf_tensor("gamma", [P, 1], F32))
            beta = mix.enter_context(nc.sbuf_tensor("beta", [P, 1], F32))
            normalise(nc, "n1s", s, s, average, True, weight=gamma, shift=beta,
                      first_load=[(gamma[:, :], io["a1_gamma"]), (beta[:, :], io["a1_beta"])])
        with ExitStack() as ffn:
            comb = ffn.enter_context(nc.sbuf_tensor("comb1", [121, 4, T], BF16))
            route(nc, io, "1", xn, comb, 160, 40, 8, "sigmoid")
            experts_sum(nc, io, "1", xn, s, x, comb, 121, 4, 5, 1, False)

        normalise(nc, "n2", x, xn, average, True)
        scratch2 = nc.dram_tensor("scratch2", [2 * B, NH, NPART, HD, L], BF16).ap()
        result2 = nc.dram_tensor("result2", [2, P, B, L], F32).ap()
        with ExitStack() as mix:
            v = mix.enter_context(nc.sbuf_tensor("v2", [P, T], F32))
            with ExitStack() as project:
                feat = project.enter_context(nc.sbuf_tensor("feat2", [P, 2 * T], F32))
                project_plain(nc, io, xn, feat, v)
                split_store(nc, "2", feat, 2 * B, scratch2)
            attend(nc, io, "2", v, scratch2, result2, False)
        attention_out(nc, io, "2", result2, s, True)
        with ExitStack() as ffn:
            comb = ffn.enter_context(nc.sbuf_tensor("comb2", [49, 1, T], BF16))
            route(nc, io, "2", xn, comb, 16, 16, 4, "grouped")
            experts_sum(nc, io, "2", xn, s, x, comb, 49, 0, 0, 8, True)

        normalise(nc, "n3", x, xn, average, True)
        with ExitStack() as mix:
            v = mix.enter_context(nc.sbuf_tensor("v3", [P, T], F32))
            with ExitStack() as project:
                feat = project.enter_context(nc.sbuf_tensor("feat3", [P, 2 * T], F32))
                project_rotary(nc, io, xn, feat, v)
                split_store(nc, "3", feat, 2 * B, scratch2)
            attend(nc, io, "3", v, scratch2, result2, True, scale=float(HD) ** -0.5)
        attention_out(nc, io, "3", result2, s, True)
        with ExitStack() as ffn:
            comb = ffn.enter_context(nc.sbuf_tensor("comb3", [25, 1, T], BF16))
            route(nc, io, "3", xn, comb, 8, 8, 2, "softmax")
            experts_sum(nc, io, "3", xn, s, x, comb, 25, 1, 8, 2, True, out=io["out"])


def layouts(i):
    f = {k: np.asarray(v) for k, v in i.items()}
    bf = mybir.dt.np(BF16)
    o = {}
    c = np.ascontiguousarray
    o["x"] = c(f["L0_attn_resid"].transpose(2, 0, 1).reshape(P, T))
    o["average"] = np.full((P, P), 1.0 / P, np.float32)
    o["ident"] = np.eye(P, dtype=np.float32)
    o["identb"] = np.eye(P).astype(bf)

    def col(v):
        return c(v.reshape(-1, P).T)

    o["m_nw"] = col(f["L0_attn_norm_w"])
    o["m_w"] = c(np.stack([f["L0_attn_skip_w"].T.reshape(P, 2, P), f["L0_attn_in_w"].T.reshape(P, 2, P)], axis=1))
    o["m_cw"] = c(f["L0_attn_conv_w"].reshape(2, P, NT).transpose(1, 0, 2))
    o["m_cb"] = col(f["L0_attn_conv_b"])
    o["m_w1"] = c(f["L0_attn_Wd1"].T.reshape(2, P, DD).transpose(1, 0, 2))
    wbc = np.zeros((P, 2, 2, NPART, SP), np.float32)
    for j, n in enumerate(("WB", "WC")):
        wbc[:, :, j, :, :NS] = f["L0_attn_" + n].T.reshape(2, P, NS).transpose(1, 0, 2)[:, :, None, :]
    o["m_wbc"] = wbc.reshape(P, 2, 2, NPART * SP)
    o["m_w2"] = c(f["L0_attn_Wd2_w"].T.reshape(DD, 2, P))
    o["m_b2"] = col(f["L0_attn_Wd2_b"])
    o["m_alog"] = c(f["L0_attn_A_log"].reshape(2, P, NS).transpose(1, 0, 2))
    o["m_wd"] = col(f["L0_attn_W_D"])
    o["m_wo"] = c(f["L0_attn_out_w"].T.reshape(2, P, P).transpose(1, 0, 2))
    sel = np.zeros((NPART, SP, NS, P), np.float32)
    for n in range(NS):
        sel[:, n, n, :] = 1.0
    o["m_sel"] = sel.reshape(NPART * SP, NS, P).astype(bf)
    o["pos"] = np.broadcast_to(np.arange(L, dtype=np.float32), (P, L)).copy()
    def rows1(t):
        t = t.reshape(t.shape[:-1] + (2, NH // 2, 1, HD))
        return np.broadcast_to(t, t.shape[:-2] + (2, HD)).reshape(t.shape[:-4] + (2, P))

    row = np.arange(P)
    sine = row // HD % 2
    o["a1_theta"] = c(rows1(f["L1_attn_theta"].reshape(P)).T)
    o["a1_pick"] = np.stack([sine - 1, sine, (1 - sine) * (np.pi / 2)], axis=1).astype(np.float32)
    o["a1_heads"] = (row[:, None] // 16 == np.arange(NH // 2)[None, :]).astype(np.float32)
    o["a1_wqk"] = c(np.stack([rows1(f["L1_attn_Wq"]), rows1(f["L1_attn_Wk"])], axis=1))
    o["a1_wv"] = f["L1_attn_Wv"]
    o["a1_own"] = np.stack([row[:, None] // 16 + g * (NH // 2) == row[None, :] // HD for g in range(2)],
                           axis=1).astype(np.float32)
    o["a1_g1"], o["a1_g2"] = f["L1_attn_G1"], f["L1_attn_G2"]
    o["a1_gamma"], o["a1_beta"] = col(f["L1_attn_gamma"]), col(f["L1_attn_beta"])
    o["o1_w"] = f["L1_attn_Wo"]
    below = np.triu(np.ones((P, P), np.float32))
    o["keep"] = below
    o["mask"] = np.stack([np.where(below.T > 0, 0, -BIG), np.where(below > 0, 0, -BIG)], axis=1).astype(bf)
    o["ones_rows"] = np.ones((NPART, GH, L), bf)

    def diagonal(w):
        out = np.zeros((NH, HD, NH, HD), np.float32)
        for h in range(NH):
            out[h, :, h, :] = w[h].T
        return out.reshape(P, P)

    o["a2_w"] = c(np.stack([f["L2_attn_W_down"], diagonal(f["L2_attn_toqueries"]), diagonal(f["L2_attn_tokeys"]),
                            diagonal(f["L2_attn_tovalues"])], axis=1))
    o["o2_w"], o["o2_b"] = f["L2_attn_W_unify"], col(f["L2_attn_b_unify"])

    def swapped(v):
        return np.concatenate([v[..., P // 2:], v[..., :P // 2]], axis=-1)

    wq, wk, bq, bk = (f["L3_attn_" + n] for n in ("wqr", "wkr", "bqr", "bkr"))
    o["a3_w"] = c(np.stack([wq, swapped(wq), wk, swapped(wk)], axis=1))
    o["a3_b"] = c(np.stack([bq, swapped(bq), bk, swapped(bk)], axis=1))
    o["a3_wkv"], o["a3_bkv"] = f["L3_attn_wkv"], f["L3_attn_bkv"].reshape(-1, 1)
    o["a3_wv"] = np.concatenate([f["L3_attn_wv"], f["L3_attn_bv"][None, :]], axis=0)
    inv = (np.float32(1.0) / np.float32(10000.0) ** (np.arange(0, P, 2, dtype=np.float32) / np.float32(P))).astype(np.float32)
    ang = np.arange(L, dtype=np.float32)[None, :] * inv[:, None]
    sine = np.sin(ang)
    o["trig"] = c(np.stack([np.concatenate([np.cos(ang)] * 2), np.concatenate([-sine, sine])], axis=1).astype(np.float32))
    o["o3_w"], o["o3_b"] = f["L3_attn_wo"], col(f["L3_attn_bo"])
    o["tri"] = np.broadcast_to(np.tril(np.ones((4, 4), np.float32), -1), (P, 4, 4)).copy()

    def router(tag, w, b):
        o[f"r{tag}_w"] = c(f[w].T)
        if b is not None:
            o[f"r{tag}_b"] = np.broadcast_to(f[b], (P, f[b].shape[0])).copy()

    router("0", "L0_ffn_router_w", "L0_ffn_correction_bias")
    router("1", "L1_ffn_router_w", "L1_ffn_expert_bias")
    router("2", "L2_ffn_gate_weight", "L2_ffn_e_bias")
    router("3", "L3_ffn_gate_w", None)

    def pack(*blocks):
        return c(np.stack(blocks, axis=2).transpose(1, 0, 2, 3))

    def select(per_block, per_group, n_loop, n_res_shared, repeat=1):
        out = np.zeros((NPART * per_group + 1, n_loop + n_res_shared, P), np.float32)
        for blk in range(n_loop):
            for m in range(P):
                e = (blk // repeat) * per_block + m // (P // per_block)
                out[np.arange(NPART) * per_group + e, blk, m] = 1.0
        out[-1, n_loop:, :] = 1.0
        return out.astype(bf)

    def cat(a, b):
        return np.concatenate([a, b], axis=0)

    def gate0(w):
        return w.reshape(4, 4, P, 32).transpose(0, 2, 1, 3).reshape(4, P, P)

    o["e0_w"] = pack(cat(gate0(f["L0_ffn_gate_w"]), f["L0_ffn_shared_gate_w"].reshape(2, P, P).transpose(0, 2, 1)),
                     cat(gate0(f["L0_ffn_up_w"]), f["L0_ffn_shared_up_w"].reshape(2, P, P).transpose(0, 2, 1)),
                     cat(f["L0_ffn_down_w"].reshape(4, P, P), f["L0_ffn_shared_down_w"].T.reshape(2, P, P)))
    o["e0_sel"] = select(4, 16, 4, 2)
    sg = np.zeros((1, P, P), np.float32)
    sg[0, :, :64] = f["L1_ffn_w_gate_shared"].T
    sd = np.zeros((1, P, P), np.float32)
    sd[0, :64, :] = f["L1_ffn_w_down_shared"].T
    o["e1_w"] = pack(cat(f["L1_ffn_w_gate"].reshape(80, P, P).transpose(0, 2, 1), sg),
                     cat(f["L1_ffn_w_down"].reshape(80, 2, P, 64).transpose(0, 1, 3, 2).reshape(80, P, P), sd))
    o["e1_sel"] = select(2, 40, 20, 1)
    o["e2_w"] = pack(f["L2_ffn_gate_proj"].reshape(8, P, P).transpose(0, 2, 1),
                     f["L2_ffn_up_proj"].reshape(8, P, P).transpose(0, 2, 1),
                     f["L2_ffn_down_proj"].reshape(8, 2, P, 64).transpose(0, 1, 3, 2).reshape(8, P, P))
    o["e2_sel"] = select(2, 16, 8, 0)

    def gate3(w):
        return w.reshape(8, P, 4, P).transpose(0, 2, 1, 3).reshape(32, P, P)

    def shared3(w):
        return w.reshape(P, 2, P).transpose(1, 0, 2)

    o["e3_w"] = pack(cat(gate3(f["L3_ffn_gate_k"]), shared3(f["L3_ffn_sh_gate"])),
                     cat(gate3(f["L3_ffn_up_k"]), shared3(f["L3_ffn_sh_up"])),
                     cat(f["L3_ffn_down_k"].reshape(32, P, P), f["L3_ffn_sh_down"].reshape(2, P, P)))
    o["e3_sel"] = select(1, 8, 32, 2, repeat=4)
    return o


def kernel(**inputs):
    import concourse.bacc as bacc
    from concourse.bass_utils import run_bass_kernel_spmd

    nc = bacc.Bacc("TRN2", target_bir_lowering=False, num_devices=1)
    arrays, io = {}, {}
    for name, a in layouts(inputs).items():
        a = np.ascontiguousarray(a)
        arrays[f"in_{name}"] = a
        io[name] = nc.dram_tensor(f"in_{name}", a.shape, mybir.dt.from_np(a.dtype), kind="ExternalInput").ap()
    io["out"] = nc.dram_tensor("out_x", (P, T), F32, kind="ExternalOutput").ap()
    program(nc, io)
    r = run_bass_kernel_spmd(nc, [arrays], core_ids=[0])
    return np.ascontiguousarray(r.results[0]["out_x"].reshape(P, B, L).transpose(1, 2, 0))
```
